# Optimizing a Trainium2 kernel written in Bass

```python
import numpy as np
import jax
import jax.numpy as jnp

def _softmax(x, axis=-1):
    return jax.nn.softmax(x, axis=axis)

def _gelu(x):
    return jax.nn.gelu(x, approximate=True)

def _silu(x):
    return jax.nn.silu(x)

def _sigmoid(x):
    return jax.nn.sigmoid(x)

def _layernorm(x, axis=-1, eps=1e-05):
    m = jnp.mean(x, axis=axis, keepdims=True)
    v = jnp.var(x, axis=axis, keepdims=True)
    return (x - m) / jnp.sqrt(v + eps)

def _scatter_add(tgt, idx, src, axis=0):
    return tgt.at[idx].add(src)

def _segment_sum(src, seg, n):
    return jax.ops.segment_sum(src, seg, n)
kernel_name = 'mk_decoder_postln_d1_seqx_r4_bd3b26'

def setup_inputs(seed: int=0):
    np.random.seed(seed)
    _w = jnp.asarray

    def _rec_inputs():
        import jax
        import jax.numpy as jnp
        _rk = jax.random.key(seed)
        x = -0.0002928 + 1 * jax.random.normal(jax.random.fold_in(_rk, 1), (16, 128, 256), jnp.float32)
        _lenS = 128 - jax.random.randint(jax.random.fold_in(_rk, 7), (16,), 0, max(1, 128 // 4) + 1, jnp.int32)
        _lenS2 = 128 - jax.random.randint(jax.random.fold_in(_rk, 8), (16,), 0, max(1, 128 // 4) + 1, jnp.int32)
        _ctx_1024P = jax.random.normal(jax.random.fold_in(_rk, 11), (16, 16, 256), jnp.float32)
        _ctx_1024c = jax.random.dirichlet(jax.random.fold_in(_rk, 511), 0.3 * jnp.ones((16,), jnp.float32), (16, 128))
        _ctx_1024t = jnp.einsum('bsk,bkd->bsd', _ctx_1024c, _ctx_1024P)
        _ctx_1024t = _ctx_1024t * jax.lax.rsqrt(jnp.mean(jnp.square(_ctx_1024t)) + 1e-12) * 0.953939
        ctx_1024 = -1.39393e-06 + 0.999914 * (_ctx_1024t + 0.3 * jax.random.normal(jax.random.fold_in(_rk, 611), (16, 128, 256), jnp.float32))
        _validS = jnp.arange(128)[None, :] < _lenS[:, None]
        _validS2 = jnp.arange(128)[None, :] < _lenS2[:, None]
        _causal = jnp.tril(jnp.ones((128, 128), dtype=bool))
        mask_BxS2_bf1 = jnp.ones((16, 128), dtype=bool)
        return (x, ctx_1024, mask_BxS2_bf1)
    x, ctx_1024, mask_BxS2_bf1 = _rec_inputs()

    def _L0_attn_setup():
        import jax, jax.numpy as jnp
        import numpy as np
        from jax import lax
        D_STATE = 16
        D_CONV = 4
        EPS = 1e-06

        def _rmsnorm(x, w):
            var = jnp.mean(x * x, axis=-1, keepdims=True)
            return x * lax.rsqrt(var + EPS) * w

        def _silu(x):
            return x * jax.nn.sigmoid(x)

        def _mamba_forward(x, norm_w, w_in, conv_w, conv_b, w_xproj, A_log, D_param, w_out):
            B, L, H = x.shape
            d_inner = w_in.shape[1] // 2
            residual = x
            h = _rmsnorm(x, norm_w)
            xz = h @ w_in
            x_ssm, z = jnp.split(xz, 2, axis=-1)
            xc = jnp.swapaxes(x_ssm, 1, 2)
            xc = jnp.pad(xc, ((0, 0), (0, 0), (D_CONV - 1, 0)))
            xc = lax.conv_general_dilated(xc, conv_w, (1,), 'VALID', feature_group_count=d_inner)
            xc = xc + conv_b[None, :, None]
            x_ssm = _silu(jnp.swapaxes(xc, 1, 2))
            proj = x_ssm @ w_xproj
            B_in = proj[..., :D_STATE]
            C_in = proj[..., D_STATE:2 * D_STATE]
            delta = jax.nn.softplus(proj[..., 2 * D_STATE:])
            A = -jnp.exp(A_log)

            def step(hst, inp):
                xs, dt, Bt, Ct = inp
                dA = jnp.exp(dt[..., None] * A)
                hst = dA * hst + (dt * xs)[..., None] * Bt[:, None, :]
                y = jnp.einsum('bdn,bn->bd', hst, Ct)
                return (hst, y)
            h0 = jnp.zeros((B, d_inner, D_STATE), x_ssm.dtype)
            xs_t = jnp.swapaxes(x_ssm, 0, 1)
            dt_t = jnp.swapaxes(delta, 0, 1)
            Bt_t = jnp.swapaxes(B_in, 0, 1)
            Ct_t = jnp.swapaxes(C_in, 0, 1)
            _, ys = lax.scan(step, h0, (xs_t, dt_t, Bt_t, Ct_t))
            y = jnp.swapaxes(ys, 0, 1)
            y = (y + D_param * x_ssm) * _silu(z)
            return residual + y @ w_out
        key = jax.random.key(seed)
        ks = jax.random.split(key, 8)
        B, L, H = (2, 512, 256)
        d_inner = 2 * H
        s = lambda n: 1.0 / np.sqrt(n)
        x = jax.random.normal(ks[0], (B, L, H), jnp.float32)
        norm_w = jnp.ones((H,), jnp.float32)
        w_in = jax.random.normal(ks[1], (H, 2 * d_inner), jnp.float32) * s(H)
        conv_w = jax.random.normal(ks[2], (d_inner, 1, D_CONV), jnp.float32) * s(D_CONV)
        conv_b = jnp.zeros((d_inner,), jnp.float32)
        w_xproj = jax.random.normal(ks[3], (d_inner, 2 * D_STATE + d_inner), jnp.float32) * s(d_inner)
        A_log = jnp.broadcast_to(jnp.log(jnp.arange(1, D_STATE + 1, dtype=jnp.float32)), (d_inner, D_STATE))
        D_param = jnp.ones((d_inner,), jnp.float32)
        w_out = jax.random.normal(ks[4], (d_inner, H), jnp.float32) * s(d_inner)
        return {'x': x, 'norm_w': norm_w, 'w_in': w_in, 'conv_w': conv_w, 'conv_b': conv_b, 'w_xproj': w_xproj, 'A_log': A_log, 'D_param': D_param, 'w_out': w_out}
    _L0_attn_all = _L0_attn_setup()
    _L0_attn_in = {k: v for k, v in _L0_attn_all.items() if k in ('norm_w', 'w_in', 'conv_w', 'conv_b', 'w_xproj', 'A_log', 'D_param', 'w_out')}
    del _L0_attn_all

    def _L0_xattn_setup():
        import jax, jax.numpy as jnp
        import numpy as np
        HEADS = 16
        CAUSAL = True
        NEG_BIAS = 999999.0
        key = jax.random.key(seed)
        k1, k2, k3 = jax.random.split(key, 3)
        B, Sq, Sk, C = (2, 512, 512, 256)
        return {'queries': jax.random.normal(k1, (B, Sq, C), dtype=jnp.float32), 'keys': jax.random.normal(k2, (B, Sk, C), dtype=jnp.float32), 'values': jax.random.normal(k3, (B, Sk, C), dtype=jnp.float32), 'queries_mask': jnp.ones((B, Sq), dtype=bool), 'values_mask': jnp.ones((B, Sk), dtype=bool)}
    _L0_xattn_all = _L0_xattn_setup()
    _L0_xattn_in = {k: v for k, v in _L0_xattn_all.items() if k in ()}
    del _L0_xattn_all

    def _L0_ffn_setup():
        import jax, jax.numpy as jnp
        import numpy as np
        B, T, D, E, H, K = (2, 512, 256, 8, 1024, 2)
        key = jax.random.key(seed)
        ks = jax.random.split(key, 8)
        s = 0.02
        return {'x': jax.random.normal(ks[0], (B, T, D), jnp.float32), 'rw1': jax.random.normal(ks[1], (D, D), jnp.float32) * s, 'rb1': jnp.zeros((D,), jnp.float32), 'rw2': jax.random.normal(ks[2], (D, E), jnp.float32) * s, 'rb2': jnp.zeros((E,), jnp.float32), 'we1': jax.random.normal(ks[3], (E, D, H), jnp.float32) * s, 'be1': jnp.zeros((E, H), jnp.float32), 'we2': jax.random.normal(ks[4], (E, H, D), jnp.float32) * s, 'be2': jnp.zeros((E, D), jnp.float32)}
    _L0_ffn_all = _L0_ffn_setup()
    _L0_ffn_in = {k: v for k, v in _L0_ffn_all.items() if k in ('rw1', 'rb1', 'rw2', 'rb2', 'we1', 'be1', 'we2', 'be2')}
    del _L0_ffn_all
    return {'x': x, 'ctx_1024': ctx_1024, 'mask_BxS2_bf1': mask_BxS2_bf1, 'L0_attn_norm_w': _L0_attn_in['norm_w'], 'L0_attn_w_in': _L0_attn_in['w_in'], 'L0_attn_conv_w': _L0_attn_in['conv_w'], 'L0_attn_conv_b': _L0_attn_in['conv_b'], 'L0_attn_w_xproj': _L0_attn_in['w_xproj'], 'L0_attn_A_log': _L0_attn_in['A_log'], 'L0_attn_D_param': _L0_attn_in['D_param'], 'L0_attn_w_out': _L0_attn_in['w_out'], 'L0_ffn_rw1': _L0_ffn_in['rw1'], 'L0_ffn_rb1': _L0_ffn_in['rb1'], 'L0_ffn_rw2': _L0_ffn_in['rw2'], 'L0_ffn_rb2': _L0_ffn_in['rb2'], 'L0_ffn_we1': _L0_ffn_in['we1'], 'L0_ffn_be1': _L0_ffn_in['be1'], 'L0_ffn_we2': _L0_ffn_in['we2'], 'L0_ffn_be2': _L0_ffn_in['be2']}

def reference(x, ctx_1024, mask_BxS2_bf1, L0_attn_norm_w, L0_attn_w_in, L0_attn_conv_w, L0_attn_conv_b, L0_attn_w_xproj, L0_attn_A_log, L0_attn_D_param, L0_attn_w_out, L0_ffn_rw1, L0_ffn_rb1, L0_ffn_rw2, L0_ffn_rb2, L0_ffn_we1, L0_ffn_be1, L0_ffn_we2, L0_ffn_be2):
    import jax
    import jax.numpy as jnp

    def _L0_attn_ref(x, norm_w, w_in, conv_w, conv_b, w_xproj, A_log, D_param, w_out):
        import jax, jax.numpy as jnp
        import numpy as np
        from jax import lax
        D_STATE = 16
        D_CONV = 4
        EPS = 1e-06

        def _rmsnorm(x, w):
            var = jnp.mean(x * x, axis=-1, keepdims=True)
            return x * lax.rsqrt(var + EPS) * w

        def _silu(x):
            return x * jax.nn.sigmoid(x)

        def _mamba_forward(x, norm_w, w_in, conv_w, conv_b, w_xproj, A_log, D_param, w_out):
            B, L, H = x.shape
            d_inner = w_in.shape[1] // 2
            residual = x
            h = _rmsnorm(x, norm_w)
            xz = h @ w_in
            x_ssm, z = jnp.split(xz, 2, axis=-1)
            xc = jnp.swapaxes(x_ssm, 1, 2)
            xc = jnp.pad(xc, ((0, 0), (0, 0), (D_CONV - 1, 0)))
            xc = lax.conv_general_dilated(xc, conv_w, (1,), 'VALID', feature_group_count=d_inner)
            xc = xc + conv_b[None, :, None]
            x_ssm = _silu(jnp.swapaxes(xc, 1, 2))
            proj = x_ssm @ w_xproj
            B_in = proj[..., :D_STATE]
            C_in = proj[..., D_STATE:2 * D_STATE]
            delta = jax.nn.softplus(proj[..., 2 * D_STATE:])
            A = -jnp.exp(A_log)

            def step(hst, inp):
                xs, dt, Bt, Ct = inp
                dA = jnp.exp(dt[..., None] * A)
                hst = dA * hst + (dt * xs)[..., None] * Bt[:, None, :]
                y = jnp.einsum('bdn,bn->bd', hst, Ct)
                return (hst, y)
            h0 = jnp.zeros((B, d_inner, D_STATE), x_ssm.dtype)
            xs_t = jnp.swapaxes(x_ssm, 0, 1)
            dt_t = jnp.swapaxes(delta, 0, 1)
            Bt_t = jnp.swapaxes(B_in, 0, 1)
            Ct_t = jnp.swapaxes(C_in, 0, 1)
            _, ys = lax.scan(step, h0, (xs_t, dt_t, Bt_t, Ct_t))
            y = jnp.swapaxes(ys, 0, 1)
            y = (y + D_param * x_ssm) * _silu(z)
            return residual + y @ w_out
        return _mamba_forward(x, norm_w, w_in, conv_w, conv_b, w_xproj, A_log, D_param, w_out)

    def _L0_xattn_ref(queries, keys, values, queries_mask, values_mask):
        import jax, jax.numpy as jnp
        import numpy as np
        HEADS = 16
        CAUSAL = True
        NEG_BIAS = 999999.0
        B, Sq, C = queries.shape
        Sk = keys.shape[1]
        H = HEADS
        d = C // H
        q = queries.reshape(B, Sq, H, d).transpose(2, 0, 1, 3)
        k = keys.reshape(B, Sk, H, d).transpose(2, 0, 1, 3)
        v = values.reshape(B, Sk, H, d).transpose(2, 0, 1, 3)
        scale = jnp.sqrt(jnp.float32(d))
        scores = jnp.einsum('hbqd,hbkd->hbqk', q, k) / scale
        mask = values_mask[None, :, None, :]
        if CAUSAL:
            causal = jnp.arange(Sq)[:, None] >= jnp.arange(Sk)[None, :]
            mask = jnp.logical_and(mask, causal[None, None])
        weights = jax.nn.softmax(scores - NEG_BIAS * mask.astype(jnp.float32), axis=-1)
        out = jnp.einsum('hbqk,hbkd->hbqd', weights, v)
        out = out.transpose(1, 2, 0, 3).reshape(B, Sq, C)
        return jnp.where(queries_mask[:, :, None], out, jnp.zeros_like(out))

    def _L0_ffn_ref(x, rw1, rb1, rw2, rb2, we1, be1, we2, be2):
        import jax, jax.numpy as jnp
        import numpy as np
        B, T, D, E, H, K = (2, 512, 256, 8, 1024, 2)
        b, t, d = x.shape
        xt = x.reshape(b * t, d)
        n = xt.shape[0]
        logits = jax.nn.silu(xt @ rw1 + rb1) @ rw2 + rb2
        _, idx = jax.lax.top_k(logits, K)
        mask = jnp.zeros((n, E), bool).at[jnp.arange(n)[:, None], idx].set(True)
        w = jax.nn.softmax(jnp.where(mask, logits, -jnp.inf), axis=1)
        h = jax.nn.silu(jnp.einsum('nd,edh->enh', xt, we1) + be1[:, None, :])
        eo = jnp.einsum('enh,ehd->end', h, we2) + be2[:, None, :]
        y = xt + jnp.einsum('ne,end->nd', w, eo)
        return y.reshape(b, t, d)
    x = _layernorm(x + _L0_attn_ref(x, L0_attn_norm_w, L0_attn_w_in, L0_attn_conv_w, L0_attn_conv_b, L0_attn_w_xproj, L0_attn_A_log, L0_attn_D_param, L0_attn_w_out), axis=-1)
    x = _layernorm(x + _L0_xattn_ref(x, ctx_1024, ctx_1024, mask_BxS2_bf1, mask_BxS2_bf1), axis=-1)
    x = _layernorm(x + _L0_ffn_ref(x, L0_ffn_rw1, L0_ffn_rb1, L0_ffn_rw2, L0_ffn_rb2, L0_ffn_we1, L0_ffn_be1, L0_ffn_we2, L0_ffn_be2), axis=-1)
    return x

_drawn_inputs = setup_inputs


def setup_inputs(seed=0):
    import zlib

    import numpy as np

    out = dict(_drawn_inputs(seed))
    spreads = {'L0_attn_norm_w': (1.0, 0.2),
     'L0_attn_conv_b': (0.0, 0.1),
     'L0_attn_D_param': (1.0, 0.2),
     'L0_ffn_rb1': (0.0, 0.361),
     'L0_ffn_rb2': (0.0, 0.1),
     'L0_ffn_be1': (0.0, 0.693),
     'L0_ffn_be2': (0.0, 0.1)}
    factors = {}
    for name, (base, spread) in spreads.items():
        noise = np.random.default_rng([zlib.crc32(name.encode()), seed]).standard_normal(out[name].shape)
        drawn = base * np.exp(spread * noise) if base else spread * noise
        out[name] = jnp.asarray(drawn.astype(out[name].dtype))
    for name, factor in factors.items():
        out[name] = (out[name] * factor).astype(out[name].dtype)
    return out
```

```python
from contextlib import ExitStack

import concourse.bass as bass
import numpy as np
from concourse import mybir

F32 = mybir.dt.float32
U8 = mybir.dt.uint8
I32 = mybir.dt.int32
U32 = mybir.dt.uint32
ALU = mybir.AluOpType
ACT = mybir.ActivationFunctionType
X = mybir.AxisListType.X

P = 128
BATCH, SEQ, DM = 16, 128, 256
DI = 512
NS = 16
TAPS = 4
HEADS, HD = 16, 16
NE, FH, TOPK = 8, 1024, 2
GB = 2
NG = BATCH // GB
GT = GB * SEQ
KC = DM // P
JC = DI // P
HC = FH // P
HPC = P // HD
VW = HD + 1
NEG = 999999.0
RMS_EPS, LN_EPS = 1e-6, 1e-5
TOKENS = BATCH * SEQ
TILES = (TOKENS * TOPK + NE * (P - 1)) // P
FJ = 10
BJ = 25
LAG = 2


def decoder_layer(nc, x, ctxk, ctxt, mask, maskt, norm_w, w_in, conv_w, conv_b, w_xproj, a_log, d_par,
                  w_out, rw1, rb1, rw2, rb2, we1, be1, we2, be2, out):
    xs_dram = nc.dram_tensor("expert_rows_in", [TILES * P, DM], F32, kind="Internal").ap()
    ys_dram = nc.dram_tensor("expert_rows_out", [TILES * P, DM], F32, kind="Internal").ap()

    top = ExitStack()
    with top:
        def sem(name):
            return top.enter_context(nc.semaphore(name))

        def keep(name, shape, dt=F32):
            return top.enter_context(nc.sbuf_tensor(name, shape, dt))

        ident = keep("ident", [P, P])
        x2_all = keep("x2_all", [P, BATCH, DM])
        logits = keep("logits", [P, BATCH, NE])
        eps_pow = keep("eps_pow", [P, BATCH])
        rms_eps = keep("rms_eps", [P, GB])
        ones_col = keep("ones_col", [P, 1])
        qmask = keep("qmask", [P, BATCH])
        slots_i = keep("slots_i", [P, TOPK, BATCH], U32)
        gate = keep("gate", [P, TOPK, BATCH])
        tile_expert = keep("tile_expert", [P, TILES], I32)

        grp = ExitStack()

        def sb(name, shape, dt=F32):
            return grp.enter_context(nc.sbuf_tensor(name, shape, dt))

        w_in_s = sb("w_in_s", [P, KC, 2 * DI])
        norm_s = sb("norm_s", [P, KC])
        convw_s = sb("convw_s", [P, JC, TAPS])
        convb_s = sb("convb_s", [P, JC])
        wx_s = sb("wx_s", [P, JC, 2 * NS + DI])
        a_s = sb("a_s", [P, JC, NS])
        dpar_s = sb("dpar_s", [P, JC])
        wo_s = sb("wo_s", [P, JC, DM])
        rw1_s = sb("rw1_s", [P, KC, DM])
        rb1_s = sb("rb1_s", [P, KC])
        rw2_s = sb("rw2_s", [P, KC, NE])
        rb2_s = sb("rb2_s", [P, NE])
        mask_s = sb("mask_s", [P, BATCH, SEQ], U8)
        maskt_s = sb("maskt_s", [P, BATCH], U8)
        causal = sb("causal", [P, SEQ])
        neg_bias = sb("neg_bias", [P, BATCH, SEQ])
        zrow = sb("zrow", [P, DM])

        xf = sb("xf", [P, GB, DM])
        sq_junk = sb("sq_junk", [P, DM])
        ssq = sb("ssq", [P, GB])
        msq = sb("msq", [P, GB])
        rrms = sb("rrms", [P, GB])
        xn = sb("xn", [P, GB, DM])
        xnT = sb("xnT", [P, KC, GB, SEQ])
        xpad = sb("xpad", [P, JC, GB, TAPS - 1 + SEQ])
        xc = sb("xc", [P, JC, GB, SEQ])
        xs = [sb(f"xs{i}", [P, JC, GB, SEQ]) for i in range(2)]
        sz = [sb(f"sz{i}", [P, JC, GB, SEQ]) for i in range(2)]
        bc = [sb(f"bc{i}", [P, GB, 2 * NS]) for i in range(2)]
        dabs = sb("dabs", [P, JC, GB, SEQ])
        dpos = sb("dpos", [P, JC, GB, SEQ])
        dt = [sb(f"dt{i}", [P, JC, GB, SEQ]) for i in range(2)]
        dtx = sb("dtx", [P, JC, GB, SEQ])
        dtxT = [sb(f"dtxT{i}", [P, GB, DI]) for i in range(2)]

        u = [sb(f"u{i}", [P, GB, DI]) for i in range(LAG)]
        da = [sb(f"da{i}", [P, JC, GB, SEQ]) for i in range(LAG)]
        h = [sb(f"h{i}", [P, JC, GB, SEQ]) for i in range(LAG)]
        acc = [sb(f"acc{i}", [P, GB, DI]) for i in range(2)]

        xb = sb("xb", [P, GB, DM])
        y = sb("y", [P, JC, GB, SEQ])
        v = sb("v", [P, GB, DM])
        stats = sb("stats", [P, GB, 6])
        mv = sb("mv", [P, GB, 2])
        var = sb("var", [P, GB])
        rstd = sb("rstd", [P, GB])
        counts = sb("counts", [P, GB])
        x1 = sb("x1", [P, GB, DM])
        x1T = sb("x1T", [P, KC, GB, SEQ])
        ctx_s = sb("ctx_s", [P, GB, DM])
        vaug = sb("vaug", [P, GB, HEADS, VW])
        kbd = sb("kbd", [P, GB, KC, HPC, SEQ])
        s_s = sb("s_s", [P, HEADS, SEQ])
        smax = sb("smax", [P, HEADS])
        pT = sb("pT", [P, HEADS, SEQ])
        rsum = sb("rsum", [P, HEADS])
        v2 = sb("v2", [P, GB, DM])
        stats2 = sb("stats2", [P, GB, 6])
        mv2 = sb("mv2", [P, GB, 2])
        var2 = sb("var2", [P, GB])
        rstd2 = sb("rstd2", [P, GB])
        x2 = sb("x2", [P, GB, DM])
        x2T = sb("x2T", [P, KC, GB, SEQ])
        rh = sb("rh", [P, KC, GB, SEQ])
        grp.close()

        rt = ExitStack()

        def rb(name, shape, dt=F32):
            return rt.enter_context(nc.sbuf_tensor(name, shape, dt))

        m8 = rb("m8", [P, BATCH, 8])
        mi = rb("mi", [P, BATCH, 8], U32)
        mif = rb("mif", [P, BATCH, TOPK])
        iota_e = rb("iota_e", [P, NE])
        iota_i = rb("iota_i", [P, TILES])
        lower = rb("lower", [P, P])
        ones_sq = rb("ones_sq", [P, P])
        pick = [rb(f"pick{k}", [P, BATCH, NE]) for k in range(TOPK)]
        picks = rb("picks", [P, BATCH, NE])
        tot = rb("tot", [P, NE, BATCH])
        keep_on = rb("keep_on", [P, NE, BATCH])
        incl = rb("incl", [P, NE, BATCH])
        cnt_f = rb("cnt_f", [P, NE])
        cnt_i = rb("cnt_i", [P, NE], I32)
        nt_i = rb("nt_i", [P, NE], I32)
        nt_f = rb("nt_f", [P, NE])
        cum = rb("cum", [P, NE])
        base = rb("base", [P, NE])
        row = rb("row", [P, BATCH, NE])
        rowk = [rb(f"rowk{k}", [P, BATCH, NE]) for k in range(TOPK)]
        rowf = rb("rowf", [P, TOPK, BATCH])
        dlt = rb("dlt", [P, BATCH])
        e2 = rb("e2", [P, BATCH])
        e2p = rb("e2p", [P, BATCH])
        ge = rb("ge", [P, TILES, NE - 1])
        te_f = rb("te_f", [P, TILES])
        rt.close()

        ex = ExitStack()

        def eb(name, shape, dt=F32):
            return ex.enter_context(nc.sbuf_tensor(name, shape, dt))

        w1_s = eb("w1_s", [P, NE * KC * FH])
        w2_s = eb("w2_s", [P, NE * HC * DM])
        xt = [eb(f"xt{i}", [P, DM]) for i in range(2)]
        xtT = [eb(f"xtT{i}", [P, KC, P]) for i in range(2)]
        b1_s = [eb(f"b1_s{i}", [P, FH]) for i in range(2)]
        b2_s = [eb(f"b2_s{i}", [P, DM]) for i in range(2)]
        hs = [eb(f"hs{i}", [P, FH]) for i in range(2)]
        hT = eb("hT", [P, HC, P])
        yo = [eb(f"yo{i}", [P, DM]) for i in range(2)]
        ex.close()

        fin = ExitStack()

        def fb(name, shape, dt=F32):
            return fin.enter_context(nc.sbuf_tensor(name, shape, dt))

        yg = [fb(f"yg{k}", [P, BATCH, DM]) for k in range(TOPK)]
        v3 = fb("v3", [P, BATCH, DM])
        stats3 = fb("stats3", [P, BATCH, 6])
        mv3 = fb("mv3", [P, BATCH, 2])
        var3 = fb("var3", [P, BATCH])
        rstd3 = fb("rstd3", [P, BATCH])
        res = fb("res", [P, BATCH, DM])
        fin.close()

        pg = ExitStack()

        def pb(name, shape):
            return pg.enter_context(nc.psum_tensor(name, shape, F32))

        p_bx = [pb(f"p_bx{i}", [P, JC, GB, SEQ]) for i in range(2)]
        p_y = [pb(f"p_y{b}", [P, DI]) for b in range(GB)]
        p_f = pb("p_f", [P, 512])
        p_b = pb("p_b", [P, 512])
        pg.close()
        px = ExitStack()

        def qb(name, shape):
            return px.enter_context(nc.psum_tensor(name, shape, F32))

        p_h = [qb(f"p_h{i}", [P, 512]) for i in range(2)]
        p_hT = [qb(f"p_hT{i}", [P, 512]) for i in range(2)]
        p_o = [qb(f"p_o{i}", [P, 512]) for i in range(2)]
        p_x = [qb(f"p_x{i}", [P, 512]) for i in range(2)]
        px.close()

        w_loaded = sem("w_loaded")
        zero_rows = sem("zero_rows")
        consts = sem("consts")
        prepared = sem("prepared")
        a_ready = sem("a_ready")
        xf_ready = sem("xf_ready")
        ssq_done = sem("ssq_done")
        rms_step = sem("rms_step")
        xn_done = sem("xn_done")
        fj_done = sem("fj_done")
        fe_done = sem("fe_done")
        conv_step = sem("conv_step")
        silu_done = sem("silu_done")
        sp_step = sem("sp_step")
        dt_done = sem("dt_done")
        dtx_done = sem("dtx_done")
        u_done = sem("u_done")
        da_done = sem("da_done")
        bx_done = sem("bx_done")
        scan_done = sem("scan_done")
        yt_done = sem("yt_done")
        acc_done = sem("acc_done")
        xb_ready = sem("xb_ready")
        ctx_ready = sem("ctx_ready")
        kbd_ready = sem("kbd_ready")
        bj_done = sem("bj_done")
        be_done = sem("be_done")
        yg_done = sem("yg_done")
        vaug_done = sem("vaug_done")
        ln_step = sem("ln_step")
        var_done = sem("var_done")
        rstd_done = sem("rstd_done")
        x1_done = sem("x1_done")
        smax_done = sem("smax_done")
        ssub_done = sem("ssub_done")
        exp_done = sem("exp_done")
        att_step = sem("att_step")
        x2_done = sem("x2_done")
        x2_kept = sem("x2_kept")
        route = sem("route")
        gate_exp = sem("gate_exp")
        route_c = sem("route_c")
        ranks = sem("ranks")
        scattered = sem("scattered")
        w1_ready = [sem(f"w1_ready{e}") for e in range(NE)]
        w2_ready = [sem(f"w2_ready{e}") for e in range(NE)]
        xt_ready = [sem(f"xt_ready{k}") for k in range(2)]
        b1_ready = [sem(f"b1_ready{k}") for k in range(2)]
        b2_ready = [sem(f"b2_ready{k}") for k in range(2)]
        xt_turned = sem("xt_turned")
        xtT_done = sem("xtT_done")
        up_done = sem("up_done")
        upb_done = sem("upb_done")
        hs_done = sem("hs_done")
        ht_turned = sem("ht_turned")
        hT_done = sem("hT_done")
        down_done = sem("down_done")
        yo_done = sem("yo_done")
        ys_stored = [sem(f"ys_stored{k}") for k in range(2)]
        gathered = [sem(f"gathered{b}") for b in range(BATCH)]
        mix_step = sem("mix_step")
        fin_rstd = sem("fin_rstd")
        fin_done = sem("fin_done")
        stored = sem("stored")

        def need(eng, s, value):
            if isinstance(value, int) and value <= 0:
                return
            eng.wait_ge(s, value)


        block = top.enter_context(nc.Block())

        def all_groups(eng, front, middle, back):
            front(0, 0)
            middle(0, 0)
            front(1, 1)
            with eng.Fori(0, (NG - 2) // 2) as i:
                for k in (1, 2):
                    g, p = i * 2 + k, k % 2
                    middle(g, p)
                    back(g - 1, 1 - p)
                    front(g + 1, 1 - p)
            middle(NG - 1, 1)
            back(NG - 2, 0)
            back(NG - 1, 1)

        @block.sync
        def _(sp):
            loads = [
                (w_in_s[:], w_in.rearrange("(c p) n -> p c n", p=P)),
                (norm_s[:], norm_w.rearrange("(c p) -> p c", p=P)),
                (convw_s[:], conv_w.rearrange("(c p) o k -> p c (o k)", p=P)),
                (convb_s[:], conv_b.rearrange("(c p) -> p c", p=P)),
                (wx_s[:], w_xproj.rearrange("(c p) n -> p c n", p=P)),
                (a_s[:], a_log.rearrange("(c p) n -> p c n", p=P)),
                (dpar_s[:], d_par.rearrange("(c p) -> p c", p=P)),
                (wo_s[:], w_out.rearrange("(c p) n -> p c n", p=P)),
                (rw1_s[:], rw1.rearrange("(c p) n -> p c n", p=P)),
                (rb1_s[:], rb1.rearrange("(c p) -> p c", p=P)),
                (rw2_s[:], rw2.rearrange("(c p) n -> p c n", p=P)),
                (rb2_s[:], rb2.rearrange("(o n) -> o n", o=1).broadcast_to([P, NE])),
                (mask_s[:], mask.rearrange("(o b) s -> o b s", o=1).broadcast_to([P, BATCH, SEQ])),
                (maskt_s[:], maskt),
            ]

            def load_front(f):
                need(sp, xn_done, f)
                sp.dma_start(xf[:], x_rows(x, f)).then_inc(xf_ready, 16)

            def keep_x2(q):
                sp.wait_ge(x2_done, q + 1)
                sp.dma_start(x2_all[:, bass.ds(q * GB, GB), :], x2[:]).then_inc(x2_kept, 16)

            def load_back(q):
                need(sp, be_done, BJ * q)
                need(sp, vaug_done, q)
                sp.dma_start(xb[:], x_rows(x, q)).then_inc(xb_ready, 16)
                sp.dma_start(ctx_s[:], x_rows(ctxk, q)).then_inc(ctx_ready, 16)
                for hh in range(HPC):
                    r = slice(HD * hh, HD * hh + HD)
                    for b in range(GB):
                        sp.dma_start(kbd[r, b, :, hh, :], ctxt[q * GB + b, r]).then_inc(kbd_ready, 16)

            load_front(0)
            with nc.allow_non_contiguous_dma(reason="small vectors, once"):
                for to, of in loads:
                    sp.dma_start(to, of).then_inc(w_loaded, 16)
            load_front(1)
            sp.wait_ge(consts, 1)
            load_back(0)
            rows = xs_dram.rearrange("(n p) d -> p n d", p=P)
            sp.dma_start(rows, zrow[:, :].unsqueeze(1).broadcast_to([P, TILES, DM])).then_inc(zero_rows, 16)
            with sp.Fori(1, NG - 1) as g:
                load_front(g + 1)
                keep_x2(g - 1)
                load_back(g)
            keep_x2(NG - 2)
            load_back(NG - 1)
            keep_x2(NG - 1)

            sp.wait_ge(be_done, BJ * NG)
            sp.wait_ge(x2_kept, 16 * NG)
            sp.wait_ge(route, N_ROUTE)
            sp.wait_ge(gate_exp, 1)
            for e in range(NE):
                sp.dma_start(w1_s[:, e * KC * FH:(e + 1) * KC * FH].rearrange("p (c n) -> p c n", c=KC),
                             we1[e].rearrange("(c p) n -> p c n", p=P)).then_inc(w1_ready[e], 16)
                sp.dma_start(w2_s[:, e * HC * DM:(e + 1) * HC * DM].rearrange("p (c n) -> p c n", c=HC),
                             we2[e].rearrange("(c p) n -> p c n", p=P)).then_inc(w2_ready[e], 16)

            def load_rows(m, k):
                i = m * 2 + k
                e = sp.value_load(tile_expert[0:1, bass.ds(i, 1)], min_val=0, max_val=NE - 1)
                need(sp, xt_turned, i - 1)
                sp.dma_start(xt[k][:], xs_dram[bass.ds(i * P, P), :]).then_inc(xt_ready[k], 16)
                need(sp, upb_done, (i - 1) * 2)
                sp.dma_start(b1_s[k][:], be1[bass.ds(e, 1), :].broadcast_to([P, FH])).then_inc(b1_ready[k], 16)
                return e

            def load_b2(m, k, e):
                i = m * 2 + k
                need(sp, yo_done, i - 1)
                sp.dma_start(b2_s[k][:], be2[bass.ds(e, 1), :].broadcast_to([P, DM])).then_inc(b2_ready[k], 16)

            def store(m, k):
                i = m * 2 + k
                sp.wait_ge(yo_done, i + 1)
                sp.dma_start(ys_dram[bass.ds(i * P, P), :], yo[k][:]).then_inc(ys_stored[k], 16)

            sp.wait_ge(scattered, 16 * TOPK * BATCH)
            for k in range(2):
                load_b2(0, k, load_rows(0, k))
            with sp.Fori(0, TILES // 2 - 1) as m:
                for k in range(2):
                    e = load_rows(m + 1, k)
                    store(m, k)
                    load_b2(m + 1, k, e)
            e = load_rows(TILES // 2, 0)
            store(TILES // 2 - 1, 0)
            load_b2(TILES // 2, 0, e)
            store(TILES // 2 - 1, 1)
            store(TILES // 2, 0)
            for b in range(BATCH):
                sp.wait_ge(fin_done, b + 1)
                sp.dma_start(out[b], res[:, b, :]).then_inc(stored, 16)
            sp.wait_ge(stored, 16 * BATCH)

        @block.tensor
        def _(pe):
            def front(f, p):
                def job(k):
                    need(pe, fe_done, f * FJ + k)

                job(0)
                pe.wait_ge(xn_done, f + 1)
                for c in range(KC):
                    for b in range(GB):
                        t = pe.transpose(p_f[:, (c * GB + b) * P:(c * GB + b + 1) * P],
                                         xn[:, b, c * P:(c + 1) * P], ident[:])
                t.then_inc(fj_done, 1)
                for k in range(4):
                    job(1 + k)
                    for jj in range(2):
                        col = (2 * k + jj) * P
                        for c in range(KC):
                            m = pe.matmul(p_f[:, jj * GT:(jj + 1) * GT], w_in_s[:, c, col:col + P],
                                          xnT[:, c, :, :].rearrange("p b s -> p (b s)"),
                                          start=c == 0, stop=c == KC - 1)
                    m.then_inc(fj_done, 1)
                job(5)
                pe.wait_ge(silu_done, f + 1)
                for b in range(GB):
                    for c in range(JC):
                        m = pe.matmul(p_f[:, b * 2 * NS:(b + 1) * 2 * NS], xs[p][:, c, b, :],
                                      wx_s[:, c, 0:2 * NS], start=c == 0, stop=c == JC - 1)
                m.then_inc(fj_done, 1)
                for k in range(2):
                    job(6 + k)
                    for jj in range(2):
                        col = 2 * NS + (2 * k + jj) * P
                        for c in range(JC):
                            m = pe.matmul(p_f[:, jj * GT:(jj + 1) * GT], wx_s[:, c, col:col + P],
                                          xs[p][:, c, :, :].rearrange("p b s -> p (b s)"),
                                          start=c == 0, stop=c == JC - 1)
                    m.then_inc(fj_done, 1)
                for b in range(GB):
                    job(8 + b)
                    pe.wait_ge(dtx_done, f + 1)
                    for j in range(JC):
                        t = pe.transpose(p_f[:, j * P:(j + 1) * P], dtx[:, j, b, :], ident[:])
                    t.then_inc(fj_done, 1)

            def turn_u(g, n):
                k = g * NS + n
                pe.wait_ge(u_done, k + 1)
                need(pe, scan_done, k - 1)
                for j in range(JC):
                    for b in range(GB):
                        t = pe.transpose(p_bx[n % 2][:, j, b, :], u[n % LAG][:, b, j * P:(j + 1) * P], ident[:])
                t.then_inc(bx_done, 1)

            def turn_h(g, n):
                k = g * NS + n
                pe.wait_ge(scan_done, k + 1)
                for b in range(GB):
                    need(pe, acc_done, (k - 1) * GB + b + 1)
                    for j in range(JC):
                        t = pe.transpose(p_y[b][:, j * P:(j + 1) * P], h[n % LAG][:, j, b, :], ident[:])
                    t.then_inc(yt_done, 1)

            def middle(g, p):
                turn_u(g, 0)
                for n in range(NS):
                    if n + 1 < NS:
                        turn_u(g, n + 1)
                    turn_h(g, n)

            def back(q, p):
                def job(k):
                    need(pe, be_done, q * BJ + k)

                for k in range(2):
                    job(k)
                    pe.wait_ge(acc_done, (q + 1) * NS * GB)
                    for jj in range(2):
                        j = 2 * k + jj
                        for b in range(GB):
                            t = pe.transpose(p_b[:, (jj * GB + b) * P:(jj * GB + b + 1) * P],
                                             acc[p][:, b, j * P:(j + 1) * P], ident[:])
                    t.then_inc(bj_done, 1)
                job(2)
                pe.wait_ge(yg_done, q + 1)
                for b in range(GB):
                    for j in range(JC):
                        m = pe.matmul(p_b[:, b * DM:(b + 1) * DM], y[:, j, b, :], wo_s[:, j, :],
                                      start=j == 0, stop=j == JC - 1)
                m.then_inc(bj_done, 1)
                job(3)
                pe.wait_ge(x1_done, q + 1)
                turn_rows(x1)
                pe.wait_ge(kbd_ready, (q + 1) * 16 * HPC * GB)
                pe.wait_ge(vaug_done, q + 1)
                for b in range(GB):
                    at = 4 + 9 * b
                    for k in range(4):
                        job(at + k)
                        c, half = k // 2, k % 2
                        pe.matmul(p_b[:], x1T[:, c, b, :],
                                  kbd[:, b, c, 4 * half:4 * half + 4, :].rearrange("p h s -> p (h s)"),
                                  start=True, stop=True).then_inc(bj_done, 1)
                    for k in range(4):
                        job(at + 4 + k)
                        pe.wait_ge(exp_done, GB * q + b + 1)
                        for hh in range(4):
                            t = pe.transpose(p_b[:, hh * P:(hh + 1) * P], s_s[:, 4 * k + hh, :], ident[:])
                        t.then_inc(bj_done, 1)
                    job(at + 8)
                    for hh in range(HEADS):
                        m = pe.matmul(p_b[:, hh * VW:(hh + 1) * VW], pT[:, hh, :], vaug[:, b, hh, :],
                                      start=True, stop=True)
                    m.then_inc(bj_done, 1)
                job(22)
                pe.wait_ge(x2_done, q + 1)
                turn_rows(x2)
                job(23)
                for m_ in range(KC):
                    for c in range(KC):
                        m = pe.matmul(p_b[:, m_ * GT:(m_ + 1) * GT], rw1_s[:, c, m_ * P:(m_ + 1) * P],
                                      x2T[:, c, :, :].rearrange("p b s -> p (b s)"),
                                      start=c == 0, stop=c == KC - 1)
                m.then_inc(bj_done, 1)
                job(24)
                for b in range(GB):
                    for c in range(KC):
                        m = pe.matmul(p_b[:, b * NE:(b + 1) * NE], rh[:, c, b, :], rw2_s[:, c, :],
                                      start=c == 0, stop=c == KC - 1)
                m.then_inc(bj_done, 1)

            def turn_rows(rows):
                for c in range(KC):
                    for b in range(GB):
                        t = pe.transpose(p_b[:, (c * GB + b) * P:(c * GB + b + 1) * P],
                                         rows[:, b, c * P:(c + 1) * P], ident[:])
                t.then_inc(bj_done, 1)

            pe.wait_ge(prepared, 1)
            all_groups(pe, front, middle, back)

            pe.wait_ge(route_c, 4)
            pe.wait_ge(route, R_PICKS)
            flat = picks[:].rearrange("p b e -> p (b e)")
            pe.matmul(p_h[0][:, 0:BATCH * NE], lower[:], flat, start=True, stop=True)
            pe.matmul(p_h[1][:, 0:BATCH * NE], ones_sq[:], flat, start=True, stop=True).then_inc(ranks, 1)

            def turn_x(m, k):
                i = m * 2 + k
                pe.wait_ge(xt_ready[k], (m + 1) * 16)
                need(pe, xtT_done, i - 1)
                for c in range(KC):
                    t = pe.transpose(p_x[k][:, c * P:(c + 1) * P], xt[k][:, c * P:(c + 1) * P], ident[:])
                t.then_inc(xt_turned, 1)

            def up(i, k, e):
                pe.wait_ge(xtT_done, i + 1)
                for half in range(2):
                    need(pe, upb_done, (i - 1) * 2 + half + 1)
                    for c in range(KC):
                        m = pe.matmul(p_h[half][:], xtT[k][:, c, :],
                                      w1_s[:, bass.ds(e * (KC * FH) + (c * FH + half * 512), 512)],
                                      start=c == 0, stop=c == KC - 1)
                    m.then_inc(up_done, 1)

            def turn_hs(i, k):
                pe.wait_ge(hs_done, i + 1)
                for half in range(2):
                    need(pe, hT_done, (i - 1) * 2 + half + 1)
                    for c in range(4):
                        col = (half * 4 + c) * P
                        t = pe.transpose(p_hT[half][:, c * P:(c + 1) * P], hs[k][:, col:col + P], ident[:])
                    t.then_inc(ht_turned, 1)

            def down(i, k, e):
                need(pe, yo_done, i - 1)
                for half in range(2):
                    pe.wait_ge(hT_done, i * 2 + (half + 1))
                    for c in range(half * 4, half * 4 + 4):
                        m = pe.matmul(p_o[k][:, 0:DM], hT[:, c, :],
                                      w2_s[:, bass.ds(e * (HC * DM) + c * DM, DM)],
                                      start=c == 0, stop=c == HC - 1)
                m.then_inc(down_done, 1)

            def expert_of(i):
                return pe.value_load(tile_expert[0:1, bass.ds(i, 1)], min_val=0, max_val=NE - 1)

            def tile(m, k, first=False, last=False):
                i = m * 2 + k
                if not last:
                    turn_x(m + k, 1 - k)
                if not first:
                    turn_hs(i - 1, 1 - k)
                e = expert_of(i)
                up(i, k, e)
                if not first:
                    down(i - 1, 1 - k, expert_of(i - 1))

            for e in range(NE):
                pe.wait_ge(w1_ready[e], 16)
                pe.wait_ge(w2_ready[e], 16)
            turn_x(0, 0)
            tile(0, 0, first=True)
            tile(0, 1)
            with pe.Fori(1, TILES // 2) as m:
                tile(m, 0)
                tile(m, 1)
            tile(TILES // 2, 0, last=True)
            turn_hs(TILES - 1, 0)
            down(TILES - 1, 0, expert_of(TILES - 1))

        @block.scalar
        def _(act):
            def front(f, p):
                fj = f * FJ

                def read_out(k, to, of, func=ACT.Copy):
                    act.wait_ge(fj_done, fj + (k + 1))
                    act.activation(to, of, func).then_inc(fe_done, 1)

                act.wait_ge(xf_ready, (f + 1) * 16)
                need(act, rms_step, 3 * f)
                for b in range(GB):
                    s = act.activation(sq_junk[:], xf[:, b, :], ACT.Square, scale=DM ** -0.5,
                                       accum_out=ssq[:, b:b + 1])
                    s.then_inc(ssq_done, 1)
                    act.wait_ge(ssq_done, GB * f + b + 1)
                read_out(0, xnT[:].rearrange("p c b s -> p (c b s)"), p_f[:])
                for k in range(2):
                    read_out(1 + k, xpad[:, 2 * k:2 * k + 2, :, TAPS - 1:].rearrange("p j b s -> p (j b) s"),
                             p_f[:].rearrange("p (a s) -> p a s", s=SEQ))
                for k in range(2):
                    read_out(3 + k, sz[p][:, 2 * k:2 * k + 2].rearrange("p j b s -> p (j b s)"), p_f[:])
                act.wait_ge(conv_step, (f + 1) * TAPS)
                act.wait_ge(fe_done, fj + 5)
                act.activation(xs[p][:], xc[:], ACT.Silu)
                act.activation(sz[p][:], sz[p][:], ACT.Silu).then_inc(silu_done, 1)
                for k in range(2):
                    act.wait_ge(fj_done, fj + (7 + k))
                    to = slice(2 * k, 2 * k + 2)
                    act.activation(dabs[:, to].rearrange("p j b s -> p (j b s)"), p_f[:], ACT.Abs).then_inc(sp_step, 1)
                    act.activation(dpos[:, to].rearrange("p j b s -> p (j b s)"), p_f[:], ACT.Relu).then_inc(fe_done, 1)
                act.wait_ge(sp_step, f * 4 + 2)
                act.activation(dabs[:], dabs[:], ACT.Exp, scale=-1.0).then_inc(sp_step, 1)
                act.wait_ge(sp_step, f * 4 + 3)
                act.activation(dabs[:], dabs[:], ACT.Ln, bias=ones_col[:]).then_inc(sp_step, 1)
                for b in range(GB):
                    read_out(8 + b, dtxT[p][:, b, :], p_f[:])

            def middle(g, p):
                act.wait_ge(dt_done, g + 1)
                for n in range(NS):
                    k = g * NS + n
                    need(act, scan_done, k - 1)
                    for j in range(JC):
                        a = act.activation(da[n % LAG][:, j, :, 1:], dt[p][:, j, :, 1:], ACT.Exp,
                                           scale=a_s[:, j, n:n + 1])
                    a.then_inc(da_done, 1)

            def back(q, p):
                bj = q * BJ

                def read_out(k, to, of):
                    act.wait_ge(bj_done, bj + (k + 1))
                    act.activation(to, of, ACT.Copy).then_inc(be_done, 1)

                read_out(3, x1T[:].rearrange("p c b s -> p (c b s)"), p_b[:])
                for b in range(GB):
                    act.wait_ge(ssub_done, GB * q + b + 1)
                    act.activation(s_s[:], s_s[:], ACT.Exp).then_inc(exp_done, 1)
                    for k in range(4):
                        read_out(4 + 9 * b + 4 + k, pT[:, 4 * k:4 * k + 4, :].rearrange("p h s -> p (h s)"), p_b[:])
                read_out(22, x2T[:].rearrange("p c b s -> p (c b s)"), p_b[:])
                act.wait_ge(bj_done, bj + 24)
                for m in range(KC):
                    a = act.activation(rh[:, m].rearrange("p b s -> p (b s)"), p_b[:, m * GT:(m + 1) * GT],
                                       ACT.Silu, bias=rb1_s[:, m:m + 1])
                a.then_inc(be_done, 1)

            act.wait_ge(w_loaded, 16 * 14)
            act.activation(a_s[:], a_s[:], ACT.Exp).then_inc(a_ready, 1)
            act.wait_ge(prepared, 1)
            all_groups(act, front, middle, back)

            act.wait_ge(route, R_DLT)
            act.activation(e2[:], dlt[:], ACT.Exp).then_inc(gate_exp, 1)

            def tile(i, k):
                act.wait_ge(xt_turned, i + 1)
                act.activation(xtT[k][:].rearrange("p c s -> p (c s)"), p_x[k][:, 0:KC * P],
                               ACT.Copy).then_inc(xtT_done, 1)

            def hidden(i, k):
                act.wait_ge(upb_done, i * 2 + 2)
                act.activation(hs[k][:], hs[k][:], ACT.Silu).then_inc(hs_done, 1)
                act.wait_ge(ht_turned, i * 2 + 1)
                need(act, down_done, i)
                act.activation(hT[:, 0:4, :].rearrange("p c s -> p (c s)"), p_hT[0][:], ACT.Copy).then_inc(hT_done, 1)
                act.wait_ge(ht_turned, i * 2 + 2)
                act.activation(hT[:, 4:8, :].rearrange("p c s -> p (c s)"), p_hT[1][:], ACT.Copy).then_inc(hT_done, 1)

            def pair(i):
                for k in range(2):
                    tile(i * 2 + (k + 1), 1 - k)
                    hidden(i * 2 + k, k)

            tile(0, 0)
            pair(0)
            with act.Fori(1, (TILES - 1) // 2) as i:
                pair(i)
            hidden(TILES - 1, 0)

        @block.gpsimd
        def _(pool):
            pool.memset(ident[:], 0.0).then_inc(route_c, 1)
            pool.wait_ge(route_c, 1)
            pool.affine_select(out=ident[:], in_=ident[:], compare_op=ALU.not_equal, fill=1.0, base=0,
                               pattern=[[-1, P]], channel_multiplier=1)
            pool.memset(eps_pow[:], -0.5)
            pool.memset(rms_eps[:], RMS_EPS)
            pool.memset(ones_col[:], 1.0)
            pool.memset(causal[:], NEG).then_inc(route_c, 1)
            pool.wait_ge(route_c, 2)
            pool.affine_select(out=causal[:], in_=causal[:], compare_op=ALU.is_ge, fill=0.0, base=0,
                               pattern=[[-1, SEQ]], channel_multiplier=1)
            pool.memset(zrow[:], 0.0)
            pool.memset(vaug[:], 1.0)
            pool.memset(xpad[:, :, :, 0:TAPS - 1], 0.0)
            for k in range(LAG):
                pool.memset(da[k][:, :, :, 0:1], 0.0)
            pool.memset(kbd[:], 0.0).then_inc(consts, 1)

            def front(f, p):
                pool.wait_ge(ssq_done, (f + 1) * GB)
                pool.tensor_tensor(msq[:], ssq[:], rms_eps[:], ALU.add).then_inc(rms_step, 1)
                pool.wait_ge(rms_step, f * 3 + 1)
                need(pool, xn_done, f)
                pool.tensor_tensor(rrms[:], msq[:], eps_pow[:, 0:GB], ALU.pow).then_inc(rms_step, 2)

            def middle(g, p):
                pool.wait_ge(fe_done, (g + 1) * FJ)
                for n in range(NS):
                    k = g * NS + n
                    need(pool, bx_done, k - 1)
                    pool.tensor_tensor(u[n % LAG][:], dtxT[p][:], bc[p][:, :, n:n + 1].broadcast_to([P, GB, DI]),
                                       ALU.mult).then_inc(u_done, 1)

            def back(q, p):
                pool.wait_ge(ctx_ready, (q + 1) * 16)
                pool.wait_ge(be_done, q * BJ + 2)
                pool.tensor_tensor(y[:], y[:], sz[p][:], ALU.mult).then_inc(yg_done, 1)
                pool.tensor_copy(vaug[:, :, :, 0:HD].rearrange("p b h d -> p (b h) d"),
                                 ctx_s[:].rearrange("p b (h d) -> p (b h) d", d=HD)).then_inc(vaug_done, 1)
                pool.wait_ge(var_done, q * 2 + 1)
                pool.tensor_tensor(rstd[:], var[:], eps_pow[:, 0:GB], ALU.pow).then_inc(rstd_done, 1)
                for b in range(GB):
                    pool.wait_ge(smax_done, GB * q + b + 1)
                    pool.tensor_tensor(s_s[:], s_s[:], smax[:].unsqueeze(2).broadcast_to([P, HEADS, SEQ]),
                                       ALU.subtract).then_inc(ssub_done, 1)
                pool.wait_ge(var_done, q * 2 + 2)
                pool.tensor_tensor(rstd2[:], var2[:], eps_pow[:, 0:GB], ALU.pow).then_inc(rstd_done, 1)

            pool.wait_ge(prepared, 1)
            all_groups(pool, front, middle, back)

            pool.wait_ge(be_done, BJ * NG)
            pool.iota(iota_e[:], pattern=[[1, NE]], base=0, channel_multiplier=0, allow_small_or_imprecise_dtypes=True)
            pool.iota(iota_i[:], pattern=[[1, TILES]], base=0, channel_multiplier=0,
                      allow_small_or_imprecise_dtypes=True)
            pool.memset(ones_sq[:], 1.0)
            pool.memset(keep_on[:], 1.0).then_inc(route_c, 1)
            pool.wait_ge(route_c, 3)
            pool.memset(keep_on[:, :, 0:1], 0.0)
            pool.affine_select(out=lower[:], in_=ones_sq[:], compare_op=ALU.is_ge, fill=0.0, base=-1,
                               pattern=[[1, P]], channel_multiplier=-1).then_inc(route_c, 1)

            pool.wait_ge(zero_rows, 16)
            pool.wait_ge(route, N_ROUTE)
            for b in range(BATCH):
                for k in range(TOPK):
                    pool.indirect_dma_start(
                        out=xs_dram[:, :], out_offset=bass.IndirectOffsetOnAxis(ap=slots_i[:, k, b:b + 1], axis=0),
                        in_=x2_all[:, b, :], in_offset=None).then_inc(scattered, 16)
            for k in range(2):
                pool.wait_ge(ys_stored[k], 16 * ((TILES + 1 - k) // 2))
            for b in range(BATCH):
                for k in range(TOPK):
                    pool.indirect_dma_start(
                        out=yg[k][:, b, :], out_offset=None, in_=ys_dram[:, :],
                        in_offset=bass.IndirectOffsetOnAxis(ap=slots_i[:, k, b:b + 1], axis=0)).then_inc(gathered[b], 16)
            pool.wait_ge(mix_step, 4 * BATCH + 1)
            pool.tensor_tensor(rstd3[:], var3[:], eps_pow[:], ALU.pow).then_inc(fin_rstd, 1)

        @block.vector
        def _(dve):
            def front(f, p):
                fj = f * FJ
                dve.wait_ge(rms_step, f * 3 + 3)
                for b in range(GB):
                    s = dve.tensor_scalar(xn[:, b, :], xf[:, b, :], rrms[:, b:b + 1], None, ALU.mult)
                s.then_inc(xn_done, 1)
                dve.wait_ge(fe_done, fj + 3)
                need(dve, silu_done, f)
                for k in range(TAPS):
                    if k:
                        dve.wait_ge(conv_step, f * TAPS + k)
                    for j in range(JC):
                        of, w = xpad[:, j, :, k:k + SEQ], convw_s[:, j, k:k + 1]
                        if k == 0:
                            s = dve.tensor_scalar(xc[:, j], of, w, convb_s[:, j:j + 1], ALU.mult, ALU.add)
                        else:
                            s = dve.scalar_tensor_tensor(out=xc[:, j], in0=of, scalar=w, in1=xc[:, j],
                                                         op0=ALU.mult, op1=ALU.add)
                    s.then_inc(conv_step, 1)
                dve.wait_ge(fj_done, fj + 6)
                dve.tensor_copy(bc[p][:].rearrange("p b n -> p (b n)"), p_f[:, 0:GB * 2 * NS]).then_inc(fe_done, 1)
                dve.wait_ge(sp_step, f * 4 + 4)
                dve.tensor_tensor(dt[p][:], dpos[:], dabs[:], ALU.add).then_inc(dt_done, 1)
                dve.wait_ge(dt_done, f + 1)
                dve.tensor_tensor(dtx[:], dt[p][:], xs[p][:], ALU.mult).then_inc(dtx_done, 1)

            def scan(g, n):
                k = g * NS + n
                dve.wait_ge(da_done, k + 1)
                dve.wait_ge(bx_done, k + 1)
                need(dve, yt_done, (k - 1) * GB)
                dve.tensor_tensor_scan(out=h[n % LAG][:].rearrange("p j b s -> p (j b s)"),
                                       data0=da[n % LAG][:].rearrange("p j b s -> p (j b s)"),
                                       data1=p_bx[n % 2][:].rearrange("p j b s -> p (j b s)"),
                                       initial=0.0, op0=ALU.mult, op1=ALU.add).then_inc(scan_done, 1)

            def sum_states(g, p, n):
                k = g * NS + n
                for b in range(GB):
                    dve.wait_ge(yt_done, k * GB + (b + 1))
                    c = bc[p][:, b, NS + n:NS + n + 1]
                    if n == 0:
                        dve.tensor_scalar(acc[p][:, b, :], p_y[b][:], c, None, ALU.mult).then_inc(acc_done, 1)
                    else:
                        dve.wait_ge(acc_done, (k - 1) * GB + (b + 1))
                        dve.scalar_tensor_tensor(out=acc[p][:, b, :], in0=p_y[b][:], scalar=c, in1=acc[p][:, b, :],
                                                 op0=ALU.mult, op1=ALU.add).then_inc(acc_done, 1)

            def middle(g, p):
                scan(g, 0)
                for n in range(NS):
                    if n + 1 < NS:
                        scan(g, n + 1)
                    sum_states(g, p, n)

            def norm_stats(src, st, m, vr, done):
                for b in range(GB):
                    s = dve.bn_stats(st[:, b, :], src[:, b, :])
                s.then_inc(ln_step, 1)
                dve.wait_ge(ln_step, done + 1)
                dve.tensor_copy(counts[:], st[:, :, 0:1].rearrange("p b o -> p (b o)"))
                for b in range(GB):
                    s = dve.bn_aggr(m[:, b, :], st[:, b, :])
                s.then_inc(ln_step, 1)
                dve.wait_ge(ln_step, done + 2)
                dve.tensor_scalar(vr[:], m[:, :, 1:2].rearrange("p b o -> p (b o)"), LN_EPS, None,
                                  ALU.add).then_inc(var_done, 1)

            def norm_apply(to, src, m, rs):
                for b in range(GB):
                    s = dve.tensor_scalar(to[:, b, :], src[:, b, :], m[:, b, 0:1], rs[:, b:b + 1],
                                          ALU.subtract, ALU.mult)
                return s

            def back(q, p):
                bj = q * BJ
                for k in range(2):
                    dve.wait_ge(bj_done, bj + (k + 1))
                    for jj in range(2):
                        j = 2 * k + jj
                        s = dve.scalar_tensor_tensor(out=y[:, j].rearrange("p b s -> p (b s)"),
                                                     in0=xs[p][:, j].rearrange("p b s -> p (b s)"),
                                                     scalar=dpar_s[:, j:j + 1], in1=p_b[:, jj * GT:(jj + 1) * GT],
                                                     op0=ALU.mult, op1=ALU.add)
                    s.then_inc(be_done, 1)
                dve.wait_ge(bj_done, bj + 3)
                dve.wait_ge(xb_ready, (q + 1) * 16)
                dve.scalar_tensor_tensor(out=v[:].rearrange("p b d -> p (b d)"), in0=xb[:].rearrange("p b d -> p (b d)"),
                                         scalar=2.0, in1=p_b[:], op0=ALU.mult, op1=ALU.add).then_inc(be_done, 1)
                dve.wait_ge(be_done, bj + 3)
                norm_stats(v, stats, mv, var, q * 4)
                dve.wait_ge(rstd_done, q * 2 + 1)
                norm_apply(x1, v, mv, rstd).then_inc(x1_done, 1)
                for b in range(GB):
                    at = bj + 4 + 9 * b
                    bias = neg_bias[:, bass.ds(q * GB + b, 1), :].broadcast_to([P, 4, SEQ])
                    for k in range(4):
                        dve.wait_ge(bj_done, at + (k + 1))
                        dve.scalar_tensor_tensor(out=s_s[:, 4 * k:4 * k + 4, :],
                                                 in0=p_b[:].rearrange("p (h s) -> p h s", s=SEQ),
                                                 scalar=1.0 / HD ** 0.5, in1=bias, op0=ALU.mult,
                                                 op1=ALU.subtract).then_inc(be_done, 1)
                    dve.wait_ge(be_done, at + 4)
                    dve.tensor_reduce(smax[:], s_s[:], X, ALU.max).then_inc(smax_done, 1)
                    dve.wait_ge(bj_done, at + 9)
                    heads = p_b[:, 0:HEADS * VW].rearrange("p (h w) -> p h w", w=VW)
                    a0 = (q * GB + b) * 3
                    dve.reciprocal(rsum[:], heads[:, :, HD:VW].rearrange("p h o -> p (h o)")).then_inc(att_step, 1)
                    dve.wait_ge(att_step, a0 + 1)
                    dve.tensor_scalar(rsum[:], rsum[:], qmask[:, bass.ds(q * GB + b, 1)], None,
                                      ALU.mult).then_inc(att_step, 1)
                    dve.wait_ge(att_step, a0 + 2)
                    dve.tensor_tensor(v2[:, b, :].rearrange("p (h d) -> p h d", d=HD), heads[:, :, 0:HD],
                                      rsum[:].unsqueeze(2).broadcast_to([P, HEADS, HD]), ALU.mult).then_inc(be_done, 1)
                    dve.wait_ge(be_done, at + 9)
                    dve.tensor_tensor(v2[:, b, :], v2[:, b, :], x1[:, b, :], ALU.add).then_inc(att_step, 1)
                dve.wait_ge(att_step, (q + 1) * 3 * GB)
                norm_stats(v2, stats2, mv2, var2, q * 4 + 2)
                dve.wait_ge(rstd_done, q * 2 + 2)
                need(dve, x2_kept, q * 16)
                norm_apply(x2, v2, mv2, rstd2).then_inc(x2_done, 1)
                dve.wait_ge(bj_done, bj + 25)
                dve.tensor_tensor(logits[:, bass.ds(q * GB, GB), :], p_b[:, 0:GB * NE].rearrange("p (b e) -> p b e", e=NE),
                                  rb2_s[:].unsqueeze(1).broadcast_to([P, GB, NE]), ALU.add).then_inc(be_done, 1)

            dve.wait_ge(w_loaded, 16 * 14)
            for c in range(KC):
                dve.tensor_scalar(w_in_s[:, c, :], w_in_s[:, c, :], norm_s[:, c:c + 1], None, ALU.mult)
            dve.wait_ge(a_ready, 1)
            dve.tensor_scalar(a_s[:], a_s[:], -1.0, None, ALU.mult)
            dve.tensor_copy(qmask[:], maskt_s[:])
            dve.wait_ge(consts, 1)
            dve.tensor_tensor(neg_bias[:], mask_s[:], causal[:].unsqueeze(1).broadcast_to([P, BATCH, SEQ]),
                              ALU.mult).then_inc(prepared, 1)
            all_groups(dve, front, middle, back)

            steps = [0]

            def step(ins):
                ins.then_inc(route, 1)
                steps[0] += 1
                dve.wait_ge(route, steps[0])

            dve.wait_ge(be_done, BJ * NG)
            dve.wait_ge(x2_kept, 16 * NG)
            for b in range(BATCH):
                s = dve.max(m8[:, b, :], logits[:, b, :])
            step(s)
            for b in range(BATCH):
                s = dve.max_index(mi[:, b, :], m8[:, b, :], logits[:, b, :])
            step(s)
            step(dve.tensor_tensor(dlt[:], m8[:, :, 1], m8[:, :, 0], ALU.subtract))
            assert steps[0] == R_DLT
            step(dve.tensor_copy(mif[:], mi[:, :, 0:TOPK]))
            dve.wait_ge(route_c, 4)
            for k in range(TOPK):
                s = dve.tensor_tensor(pick[k][:], mif[:, :, k:k + 1].broadcast_to([P, BATCH, NE]),
                                      iota_e[:].unsqueeze(1).broadcast_to([P, BATCH, NE]), ALU.is_equal)
            step(s)
            step(dve.tensor_tensor(picks[:], pick[0][:], pick[1][:], ALU.add))
            assert steps[0] == R_PICKS
            dve.wait_ge(ranks, 1)
            step(dve.tensor_copy(tot[:], p_h[1][:, 0:BATCH * NE].rearrange("p (b e) -> p e b", e=NE)))
            step(dve.tensor_tensor_scan(out=incl[:].rearrange("p e b -> p (e b)"),
                                        data0=keep_on[:].rearrange("p e b -> p (e b)"),
                                        data1=tot[:].rearrange("p e b -> p (e b)"), initial=0.0,
                                        op0=ALU.mult, op1=ALU.add))
            step(dve.tensor_scalar(cnt_f[:], incl[:, :, BATCH - 1], float(P - 1), None, ALU.add))
            step(dve.tensor_copy(cnt_i[:], cnt_f[:]))
            step(dve.tensor_single_scalar(nt_i[:], cnt_i[:], 7, ALU.arith_shift_right))
            step(dve.tensor_copy(nt_f[:], nt_i[:]))
            step(dve.tensor_tensor_scan(out=cum[:], data0=ones_sq[:, 0:NE], data1=nt_f[:], initial=0.0,
                                        op0=ALU.mult, op1=ALU.add))
            step(dve.tensor_tensor(base[:], cum[:], nt_f[:], ALU.subtract))
            step(dve.tensor_scalar(base[:], base[:], float(P), None, ALU.mult))
            step(dve.tensor_tensor(incl[:], incl[:], tot[:], ALU.subtract))
            step(dve.tensor_tensor(incl[:], incl[:], base[:].unsqueeze(2).broadcast_to([P, NE, BATCH]), ALU.add))
            step(dve.tensor_tensor(row[:], p_h[0][:, 0:BATCH * NE].rearrange("p (b e) -> p b e", e=NE),
                                   incl[:].rearrange("p e b -> p b e"), ALU.add))
            for k in range(TOPK):
                s = dve.tensor_tensor(rowk[k][:], row[:], pick[k][:], ALU.mult)
            step(s)
            for k in range(TOPK):
                s = dve.tensor_reduce(rowf[:, k, :], rowk[k][:], X, ALU.add)
            step(s)
            step(dve.tensor_copy(slots_i[:], rowf[:]))
            step(dve.tensor_tensor(ge[:], iota_i[:].unsqueeze(2).broadcast_to([P, TILES, NE - 1]),
                                   cum[:, 0:NE - 1].unsqueeze(1).broadcast_to([P, TILES, NE - 1]), ALU.is_ge))
            step(dve.tensor_reduce(te_f[:], ge[:], X, ALU.add))
            step(dve.tensor_copy(tile_expert[:], te_f[:]))
            dve.wait_ge(gate_exp, 1)
            step(dve.tensor_scalar(e2p[:], e2[:], 1.0, None, ALU.add))
            step(dve.reciprocal(gate[:, 0, :], e2p[:]))
            step(dve.tensor_tensor(gate[:, 1, :], gate[:, 0, :], e2[:], ALU.mult))
            assert steps[0] == N_ROUTE, steps[0]

            def add_b1(m, k):
                i = m * 2 + k
                dve.wait_ge(b1_ready[k], (m + 1) * 16)
                need(dve, ht_turned, (i - 1) * 2)
                for half in range(2):
                    dve.wait_ge(up_done, i * 2 + (half + 1))
                    dve.tensor_tensor(hs[k][:, half * 512:(half + 1) * 512], p_h[half][:],
                                      b1_s[k][:, half * 512:(half + 1) * 512], ALU.add).then_inc(upb_done, 1)

            def add_b2(m, k):
                i = m * 2 + k
                dve.wait_ge(down_done, i + 1)
                dve.wait_ge(b2_ready[k], (m + 1) * 16)
                need(dve, ys_stored[k], m * 16)
                dve.tensor_tensor(yo[k][:], p_o[k][:, 0:DM], b2_s[k][:], ALU.add).then_inc(yo_done, 1)

            def pair(m):
                for k in range(2):
                    add_b1(m + k, 1 - k)
                    add_b2(m, k)

            add_b1(0, 0)
            pair(0)
            with dve.Fori(1, (TILES - 1) // 2) as i:
                pair(i)
            add_b2(TILES // 2, 0)

            for b in range(BATCH):
                dve.wait_ge(gathered[b], 32)
                dve.tensor_scalar(v3[:, b, :], x2_all[:, b, :], 2.0, None, ALU.mult).then_inc(mix_step, 1)
                for k in range(TOPK):
                    dve.wait_ge(mix_step, 4 * b + 1 + k)
                    dve.scalar_tensor_tensor(out=v3[:, b, :], in0=yg[k][:, b, :], scalar=gate[:, k, b:b + 1],
                                             in1=v3[:, b, :], op0=ALU.mult, op1=ALU.add).then_inc(mix_step, 1)
                dve.wait_ge(mix_step, 4 * b + 3)
                dve.bn_stats(stats3[:, b, :], v3[:, b, :]).then_inc(mix_step, 1)
            dve.wait_ge(mix_step, 4 * BATCH)
            for b in range(BATCH):
                s = dve.bn_aggr(mv3[:, b, :], stats3[:, b, :])
            s.then_inc(route, 1)
            dve.wait_ge(route, N_ROUTE + 1)
            dve.tensor_scalar(var3[:], mv3[:, :, 1], LN_EPS, None, ALU.add).then_inc(mix_step, 1)
            dve.wait_ge(fin_rstd, 1)
            for b in range(BATCH):
                dve.tensor_scalar(res[:, b, :], v3[:, b, :], mv3[:, b, 0:1], rstd3[:, b:b + 1],
                                  ALU.subtract, ALU.mult).then_inc(fin_done, 1)


R_DLT, R_PICKS, N_ROUTE = 3, 6, 27


def x_rows(t, g):
    return t[bass.ds(g * GB, GB)].rearrange("b s d -> s b d")


def kernel(x, ctx_1024, mask_BxS2_bf1, L0_attn_norm_w, L0_attn_w_in, L0_attn_conv_w, L0_attn_conv_b,
           L0_attn_w_xproj, L0_attn_A_log, L0_attn_D_param, L0_attn_w_out, L0_ffn_rw1, L0_ffn_rb1, L0_ffn_rw2,
           L0_ffn_rb2, L0_ffn_we1, L0_ffn_be1, L0_ffn_we2, L0_ffn_be2):
    import concourse.bacc as bacc
    from concourse.bass_utils import run_bass_kernel_spmd

    ctx = np.asarray(ctx_1024)
    mask = np.asarray(mask_BxS2_bf1).view(np.uint8)
    arrays = {
        "x": x, "ctxk": ctx,
        "ctxt": ctx.transpose(0, 2, 1).reshape(BATCH, KC, P, SEQ).transpose(0, 2, 1, 3),
        "mask": mask, "maskt": mask.T,
        "norm_w": L0_attn_norm_w, "w_in": L0_attn_w_in, "conv_w": L0_attn_conv_w, "conv_b": L0_attn_conv_b,
        "w_xproj": L0_attn_w_xproj, "a_log": L0_attn_A_log, "d_par": L0_attn_D_param, "w_out": L0_attn_w_out,
        "rw1": L0_ffn_rw1, "rb1": L0_ffn_rb1, "rw2": L0_ffn_rw2, "rb2": L0_ffn_rb2,
        "we1": L0_ffn_we1, "be1": L0_ffn_be1, "we2": L0_ffn_we2, "be2": L0_ffn_be2,
    }
    arrays = {f"in_{n}": np.ascontiguousarray(a) for n, a in arrays.items()}
    nc = bacc.Bacc("TRN2", target_bir_lowering=False, num_devices=1)
    args = [nc.dram_tensor(n, a.shape, mybir.dt.from_np(a.dtype), kind="ExternalInput").ap()
            for n, a in arrays.items()]
    out = nc.dram_tensor("out", [BATCH, SEQ, DM], F32, kind="ExternalOutput").ap()
    decoder_layer(nc, *args, out)
    r = run_bass_kernel_spmd(nc, [arrays], core_ids=[0])
    return r.results[0]["out"]
```

```python
from contextlib import ExitStack

import concourse.bass as bass
import numpy as np
from concourse import mybir

F32 = mybir.dt.float32
U8 = mybir.dt.uint8
I32 = mybir.dt.int32
U32 = mybir.dt.uint32
ALU = mybir.AluOpType
ACT = mybir.ActivationFunctionType
X = mybir.AxisListType.X

P = 128
BATCH, SEQ, DM = 16, 128, 256
DI = 512
NS = 16
TAPS = 4
HEADS, HD = 16, 16
NE, FH, TOPK = 8, 1024, 2
GB = 2
NG = BATCH // GB
GT = GB * SEQ
KC = DM // P
JC = DI // P
HC = FH // P
HPC = P // HD
VW = HD + 1
NEG = 999999.0
RMS_EPS, LN_EPS = 1e-6, 1e-5
TOKENS = BATCH * SEQ
TILES = (TOKENS * TOPK + NE * (P - 1)) // P
FJ = 10
BJ = 25
J_SUM, J_OUT, J_X1T = 0, 2, 3
J_SCORE = [4 + 4 * b for b in range(2)]
J_TURN = [12 + 5 * b for b in range(2)]
J_ATT = [16 + 5 * b for b in range(2)]
J_X2T, J_RH, J_LOGIT = 22, 23, 24
LAG = 2


def decoder_layer(nc, x, ctxk, ctxt, mask, maskt, norm_w, w_in, conv_w, conv_b, w_xproj, a_log, d_par,
                  w_out, rw1, rb1, rw2, rb2, we1, be1, we2, be2, out):
    xs_dram = nc.dram_tensor("expert_rows_in", [TILES * P, DM], F32, kind="Internal").ap()
    ys_dram = nc.dram_tensor("expert_rows_out", [TILES * P, DM], F32, kind="Internal").ap()

    top = ExitStack()
    with top:
        def sem(name):
            return top.enter_context(nc.semaphore(name))

        def keep(name, shape, dt=F32):
            return top.enter_context(nc.sbuf_tensor(name, shape, dt))

        ident = keep("ident", [P, P])
        x2_all = keep("x2_all", [P, BATCH, DM])
        logits = keep("logits", [P, BATCH, NE])
        eps_pow = keep("eps_pow", [P, BATCH])
        rms_eps = keep("rms_eps", [P, GB])
        ones_col = keep("ones_col", [P, 1])
        qmask = keep("qmask", [P, BATCH])
        slots_i = keep("slots_i", [P, TOPK, BATCH], U32)
        gate = keep("gate", [P, TOPK, BATCH])
        tile_expert = keep("tile_expert", [P, TILES], I32)

        grp = ExitStack()

        def sb(name, shape, dt=F32):
            return grp.enter_context(nc.sbuf_tensor(name, shape, dt))

        w_in_s = sb("w_in_s", [P, KC, 2 * DI])
        norm_s = sb("norm_s", [P, KC])
        convw_s = sb("convw_s", [P, JC, TAPS])
        convb_s = sb("convb_s", [P, JC])
        wx_s = sb("wx_s", [P, JC, 2 * NS + DI])
        a_s = sb("a_s", [P, JC, NS])
        dpar_s = sb("dpar_s", [P, JC])
        wo_s = sb("wo_s", [P, JC, DM])
        rw1_s = sb("rw1_s", [P, KC, DM])
        rb1_s = sb("rb1_s", [P, KC])
        rw2_s = sb("rw2_s", [P, KC, NE])
        rb2_s = sb("rb2_s", [P, NE])
        mask_s = sb("mask_s", [P, BATCH, SEQ], U8)
        maskt_s = sb("maskt_s", [P, BATCH], U8)
        causal = sb("causal", [P, SEQ])
        neg_bias = sb("neg_bias", [P, BATCH, SEQ])
        zrow = sb("zrow", [P, DM])

        xf = sb("xf", [P, GB, DM])
        sq_junk = sb("sq_junk", [P, DM])
        ssq = sb("ssq", [P, GB])
        msq = sb("msq", [P, GB])
        rrms = sb("rrms", [P, GB])
        xn = sb("xn", [P, GB, DM])
        xnT = sb("xnT", [P, KC, GB, SEQ])
        xpad = sb("xpad", [P, JC, GB, TAPS - 1 + SEQ])
        xc = sb("xc", [P, JC, GB, SEQ])
        xs = [sb(f"xs{i}", [P, JC, GB, SEQ]) for i in range(2)]
        sz = [sb(f"sz{i}", [P, JC, GB, SEQ]) for i in range(2)]
        bc = [sb(f"bc{i}", [P, GB, 2 * NS]) for i in range(2)]
        dabs = sb("dabs", [P, JC, GB, SEQ])
        dpos = sb("dpos", [P, JC, GB, SEQ])
        dt = [sb(f"dt{i}", [P, JC, GB, SEQ]) for i in range(2)]
        dtx = sb("dtx", [P, JC, GB, SEQ])
        dtxT = [sb(f"dtxT{i}", [P, GB, DI]) for i in range(2)]

        u = [sb(f"u{i}", [P, GB, DI]) for i in range(LAG)]
        da = [sb(f"da{i}", [P, JC, GB, SEQ]) for i in range(LAG)]
        h = [sb(f"h{i}", [P, JC, GB, SEQ]) for i in range(LAG)]
        acc = [sb(f"acc{i}", [P, GB, DI]) for i in range(2)]

        xb = sb("xb", [P, GB, DM])
        y = sb("y", [P, JC, GB, SEQ])
        v = sb("v", [P, GB, DM])
        stats = sb("stats", [P, GB, 6])
        mv = sb("mv", [P, GB, 2])
        var = sb("var", [P, GB])
        rstd = sb("rstd", [P, GB])
        counts = sb("counts", [P, GB])
        x1 = sb("x1", [P, GB, DM])
        x1T = sb("x1T", [P, KC, GB, SEQ])
        ctx_s = sb("ctx_s", [P, GB, DM])
        vaug = sb("vaug", [P, GB, HEADS, VW])
        kbd = sb("kbd", [P, GB, KC, HPC, SEQ])
        s_s = [sb(f"s_s{b}", [P, HEADS, SEQ]) for b in range(GB)]
        smax = [sb(f"smax{b}", [P, HEADS]) for b in range(GB)]
        pT = sb("pT", [P, HEADS, SEQ])
        rsum = sb("rsum", [P, HEADS])
        v2 = sb("v2", [P, GB, DM])
        stats2 = sb("stats2", [P, GB, 6])
        mv2 = sb("mv2", [P, GB, 2])
        var2 = sb("var2", [P, GB])
        rstd2 = sb("rstd2", [P, GB])
        x2 = sb("x2", [P, GB, DM])
        x2T = sb("x2T", [P, KC, GB, SEQ])
        rh = x2T
        grp.close()

        rt = ExitStack()

        def rb(name, shape, dt=F32):
            return rt.enter_context(nc.sbuf_tensor(name, shape, dt))

        m8 = rb("m8", [P, BATCH, 8])
        mi = rb("mi", [P, BATCH, 8], U32)
        mif = rb("mif", [P, BATCH, TOPK])
        iota_e = rb("iota_e", [P, NE])
        iota_i = rb("iota_i", [P, TILES])
        lower = rb("lower", [P, P])
        ones_sq = rb("ones_sq", [P, P])
        pick = [rb(f"pick{k}", [P, BATCH, NE]) for k in range(TOPK)]
        picks = rb("picks", [P, BATCH, NE])
        tot = rb("tot", [P, NE, BATCH])
        keep_on = rb("keep_on", [P, NE, BATCH])
        incl = rb("incl", [P, NE, BATCH])
        cnt_f = rb("cnt_f", [P, NE])
        cnt_i = rb("cnt_i", [P, NE], I32)
        nt_i = rb("nt_i", [P, NE], I32)
        nt_f = rb("nt_f", [P, NE])
        cum = rb("cum", [P, NE])
        base = rb("base", [P, NE])
        row = rb("row", [P, BATCH, NE])
        rowk = [rb(f"rowk{k}", [P, BATCH, NE]) for k in range(TOPK)]
        rowf = rb("rowf", [P, TOPK, BATCH])
        dlt = rb("dlt", [P, BATCH])
        e2 = rb("e2", [P, BATCH])
        e2p = rb("e2p", [P, BATCH])
        ge = rb("ge", [P, TILES, NE - 1])
        te_f = rb("te_f", [P, TILES])
        rt.close()

        ex = ExitStack()

        def eb(name, shape, dt=F32):
            return ex.enter_context(nc.sbuf_tensor(name, shape, dt))

        w1_s = eb("w1_s", [P, NE * KC * FH])
        w2_s = eb("w2_s", [P, NE * HC * DM])
        xt = [eb(f"xt{i}", [P, DM]) for i in range(2)]
        xtT = [eb(f"xtT{i}", [P, KC, P]) for i in range(2)]
        b1_s = [eb(f"b1_s{i}", [P, FH]) for i in range(2)]
        b2_s = [eb(f"b2_s{i}", [P, DM]) for i in range(2)]
        hs = [eb(f"hs{i}", [P, FH]) for i in range(2)]
        hT = eb("hT", [P, HC, P])
        yo = [eb(f"yo{i}", [P, DM]) for i in range(2)]
        ex.close()

        fin = ExitStack()

        def fb(name, shape, dt=F32):
            return fin.enter_context(nc.sbuf_tensor(name, shape, dt))

        yg = [fb(f"yg{k}", [P, BATCH, DM]) for k in range(TOPK)]
        v3 = fb("v3", [P, BATCH, DM])
        stats3 = fb("stats3", [P, BATCH, 6])
        mv3 = fb("mv3", [P, BATCH, 2])
        var3 = fb("var3", [P, BATCH])
        rstd3 = fb("rstd3", [P, BATCH])
        res = fb("res", [P, BATCH, DM])
        fin.close()

        pg = ExitStack()

        def pb(name, shape):
            return pg.enter_context(nc.psum_tensor(name, shape, F32))

        p_bx = [pb(f"p_bx{i}", [P, JC, GB, SEQ]) for i in range(2)]
        p_y = [pb(f"p_y{b}", [P, DI]) for b in range(GB)]
        p_f = pb("p_f", [P, 512])
        p_b = pb("p_b", [P, 512])
        pg.close()
        px = ExitStack()

        def qb(name, shape):
            return px.enter_context(nc.psum_tensor(name, shape, F32))

        p_h = [qb(f"p_h{i}", [P, 512]) for i in range(2)]
        p_hT = [qb(f"p_hT{i}", [P, 512]) for i in range(2)]
        p_o = [qb(f"p_o{i}", [P, 512]) for i in range(2)]
        p_x = [qb(f"p_x{i}", [P, 512]) for i in range(2)]
        px.close()

        w_loaded = sem("w_loaded")
        zero_rows = sem("zero_rows")
        consts = sem("consts")
        prepared = sem("prepared")
        a_ready = sem("a_ready")
        xf_ready = sem("xf_ready")
        ssq_done = sem("ssq_done")
        rms_step = sem("rms_step")
        xn_done = sem("xn_done")
        fj_done = sem("fj_done")
        fe_done = sem("fe_done")
        conv_step = sem("conv_step")
        silu_done = sem("silu_done")
        sp_step = sem("sp_step")
        dt_done = sem("dt_done")
        dtx_done = sem("dtx_done")
        u_done = sem("u_done")
        da_done = sem("da_done")
        bx_done = sem("bx_done")
        scan_done = sem("scan_done")
        yt_done = sem("yt_done")
        acc_done = sem("acc_done")
        xb_ready = sem("xb_ready")
        ctx_ready = sem("ctx_ready")
        kbd_ready = sem("kbd_ready")
        bj_done = sem("bj_done")
        be_done = sem("be_done")
        yg_done = sem("yg_done")
        vaug_done = sem("vaug_done")
        ln_step = sem("ln_step")
        var_done = sem("var_done")
        rstd_done = sem("rstd_done")
        x1_done = sem("x1_done")
        smax_done = sem("smax_done")
        ssub_done = sem("ssub_done")
        exp_done = sem("exp_done")
        att_step = sem("att_step")
        x2_done = sem("x2_done")
        x2_kept = sem("x2_kept")
        route = sem("route")
        gate_exp = sem("gate_exp")
        route_c = sem("route_c")
        ranks = sem("ranks")
        scattered = sem("scattered")
        w1_ready = [sem(f"w1_ready{e}") for e in range(NE)]
        w2_ready = [sem(f"w2_ready{e}") for e in range(NE)]
        xt_ready = [sem(f"xt_ready{k}") for k in range(2)]
        b1_ready = [sem(f"b1_ready{k}") for k in range(2)]
        b2_ready = [sem(f"b2_ready{k}") for k in range(2)]
        xt_turned = sem("xt_turned")
        xtT_done = sem("xtT_done")
        up_done = sem("up_done")
        upb_done = sem("upb_done")
        hs_done = sem("hs_done")
        ht_turned = sem("ht_turned")
        hT_done = sem("hT_done")
        down_done = sem("down_done")
        yo_done = sem("yo_done")
        ys_stored = [sem(f"ys_stored{k}") for k in range(2)]
        gathered = [sem(f"gathered{b}") for b in range(BATCH)]
        mix_step = sem("mix_step")
        fin_rstd = sem("fin_rstd")
        fin_done = sem("fin_done")
        stored = sem("stored")

        def need(eng, s, value):
            if isinstance(value, int) and value <= 0:
                return
            eng.wait_ge(s, value)


        block = top.enter_context(nc.Block())

        def all_groups(eng, front, start, slot, back):
            for n in range(NS):
                front(0, 0, n)
            start()
            for n in range(NS):
                slot(0, 0, n, first=True)
            with eng.Fori(0, (NG - 2) // 2) as i:
                for k in (1, 2):
                    for n in range(NS):
                        slot(i * 2 + k, k % 2, n)
            for n in range(NS):
                slot(NG - 1, 1, n, last=True)
            for n in range(NS):
                back(NG - 1, 1, n)

        def ahead(g, p, n, by):
            return (g, p, n + by) if n + by < NS else (g + 1, 1 - p, n + by - NS)

        @block.sync
        def _(sp):
            loads = [
                (w_in_s[:], w_in.rearrange("(c p) n -> p c n", p=P)),
                (norm_s[:], norm_w.rearrange("(c p) -> p c", p=P)),
                (convw_s[:], conv_w.rearrange("(c p) o k -> p c (o k)", p=P)),
                (convb_s[:], conv_b.rearrange("(c p) -> p c", p=P)),
                (wx_s[:], w_xproj.rearrange("(c p) n -> p c n", p=P)),
                (a_s[:], a_log.rearrange("(c p) n -> p c n", p=P)),
                (dpar_s[:], d_par.rearrange("(c p) -> p c", p=P)),
                (wo_s[:], w_out.rearrange("(c p) n -> p c n", p=P)),
                (rw1_s[:], rw1.rearrange("(c p) n -> p c n", p=P)),
                (rb1_s[:], rb1.rearrange("(c p) -> p c", p=P)),
                (rw2_s[:], rw2.rearrange("(c p) n -> p c n", p=P)),
                (rb2_s[:], rb2.rearrange("(o n) -> o n", o=1).broadcast_to([P, NE])),
                (mask_s[:], mask.rearrange("(o b) s -> o b s", o=1).broadcast_to([P, BATCH, SEQ])),
                (maskt_s[:], maskt),
            ]

            def load_front(f):
                need(sp, xn_done, f)
                sp.dma_start(xf[:], x_rows(x, f)).then_inc(xf_ready, 16)

            def keep_x2(q):
                sp.wait_ge(x2_done, q + 1)
                sp.dma_start(x2_all[:, bass.ds(q * GB, GB), :], x2[:]).then_inc(x2_kept, 16)

            def load_back(q):
                need(sp, be_done, BJ * (q - 1) + J_OUT + 1)
                sp.dma_start(xb[:], x_rows(x, q)).then_inc(xb_ready, 16)
                need(sp, vaug_done, q)
                sp.dma_start(ctx_s[:], x_rows(ctxk, q)).then_inc(ctx_ready, 16)
                need(sp, be_done, BJ * (q - 1) + J_SCORE[1] + 4)
                for hh in range(HPC):
                    r = slice(HD * hh, HD * hh + HD)
                    for b in range(GB):
                        sp.dma_start(kbd[r, b, :, hh, :], ctxt[q * GB + b, r]).then_inc(kbd_ready, 16)

            load_front(0)
            with nc.allow_non_contiguous_dma(reason="small vectors, once"):
                for to, of in loads:
                    sp.dma_start(to, of).then_inc(w_loaded, 16)
            load_front(1)
            sp.wait_ge(consts, 1)
            load_back(0)
            rows = xs_dram.rearrange("(n p) d -> p n d", p=P)
            sp.dma_start(rows, zrow[:, :].unsqueeze(1).broadcast_to([P, TILES, DM])).then_inc(zero_rows, 16)
            load_front(2)
            with sp.Fori(1, NG - 2) as g:
                load_front(g + 2)
                load_back(g)
                keep_x2(g - 1)
            for g in (NG - 2, NG - 1):
                load_back(g)
                keep_x2(g - 1)
            keep_x2(NG - 1)

            sp.wait_ge(be_done, BJ * NG)
            sp.wait_ge(x2_kept, 16 * NG)
            sp.wait_ge(route, N_ROUTE)
            sp.wait_ge(gate_exp, 1)
            for e in range(NE):
                sp.dma_start(w1_s[:, e * KC * FH:(e + 1) * KC * FH].rearrange("p (c n) -> p c n", c=KC),
                             we1[e].rearrange("(c p) n -> p c n", p=P)).then_inc(w1_ready[e], 16)
                sp.dma_start(w2_s[:, e * HC * DM:(e + 1) * HC * DM].rearrange("p (c n) -> p c n", c=HC),
                             we2[e].rearrange("(c p) n -> p c n", p=P)).then_inc(w2_ready[e], 16)

            def load_x(i, m, k):
                need(sp, xt_turned, i - 1)
                sp.dma_start(xt[k][:], xs_dram[bass.ds(i * P, P), :]).then_inc(xt_ready[k], 16)

            def expert_of(i):
                return sp.value_load(tile_expert[0:1, bass.ds(i, 1)], min_val=0, max_val=NE - 1)

            def load_b1(i, m, k, e):
                need(sp, upb_done, (i - 1) * 2)
                sp.dma_start(b1_s[k][:], be1[bass.ds(e, 1), :].broadcast_to([P, FH])).then_inc(b1_ready[k], 16)

            def load_b2(i, m, k, e):
                need(sp, yo_done, i - 1)
                sp.dma_start(b2_s[k][:], be2[bass.ds(e, 1), :].broadcast_to([P, DM])).then_inc(b2_ready[k], 16)

            def store(i, m, k):
                sp.wait_ge(yo_done, i + 1)
                sp.dma_start(ys_dram[bass.ds(i * P, P), :], yo[k][:]).then_inc(ys_stored[k], 16)

            def step(j, m, k):
                static = isinstance(j, int)
                e = None
                if not static or j + 1 < TILES:
                    e = expert_of(j + 1)
                    load_b1(j + 1, m + k, 1 - k, e)
                if not static or j + 3 < TILES:
                    load_x(j + 3, m + 1 + k, 1 - k)
                if not static or j >= 1:
                    store(j - 1, m - 1 + k, 1 - k)
                if e is not None:
                    load_b2(j + 1, m + k, 1 - k, e)

            sp.wait_ge(scattered, 16 * TOPK * BATCH)
            load_x(0, 0, 0)
            load_x(1, 0, 1)
            e = expert_of(0)
            load_b1(0, 0, 0, e)
            load_b2(0, 0, 0, e)
            load_x(2, 1, 0)
            first, turns = 2, (TILES - 3 - 2) // 2
            for j in range(first):
                step(j, j // 2, j % 2)
            with sp.Fori(first // 2, first // 2 + turns) as m:
                for k in range(2):
                    step(m * 2 + k, m, k)
            for j in range(first + 2 * turns, TILES + 1):
                step(j, j // 2, j % 2)
            for b in range(BATCH):
                sp.wait_ge(fin_done, b + 1)
                sp.dma_start(out[b], res[:, b, :]).then_inc(stored, 16)
            sp.wait_ge(stored, 16 * BATCH)

        @block.tensor
        def _(pe):
            def front(f, p, n):
                def job(k):
                    need(pe, fe_done, f * FJ + k)

                if n == 1:
                    job(0)
                    pe.wait_ge(xn_done, f + 1)
                    for c in range(KC):
                        for b in range(GB):
                            t = pe.transpose(p_f[:, (c * GB + b) * P:(c * GB + b + 1) * P],
                                             xn[:, b, c * P:(c + 1) * P], ident[:])
                    t.then_inc(fj_done, 1)
                if 2 <= n < 6:
                    k = n - 2
                    job(1 + k)
                    for jj in range(2):
                        col = (2 * k + jj) * P
                        for c in range(KC):
                            m = pe.matmul(p_f[:, jj * GT:(jj + 1) * GT], w_in_s[:, c, col:col + P],
                                          xnT[:, c, :, :].rearrange("p b s -> p (b s)"),
                                          start=c == 0, stop=c == KC - 1)
                    m.then_inc(fj_done, 1)
                if n == 9:
                    job(7)
                    for b in range(GB):
                        for c in range(JC):
                            m = pe.matmul(p_f[:, b * 2 * NS:(b + 1) * 2 * NS], xs[p][:, c, b, :],
                                          wx_s[:, c, 0:2 * NS], start=c == 0, stop=c == JC - 1)
                    m.then_inc(fj_done, 1)
                if 7 <= n < 9:
                    k = n - 7
                    job(5 + k)
                    pe.wait_ge(silu_done, f + 1)
                    for jj in range(2):
                        col = 2 * NS + (2 * k + jj) * P
                        for c in range(JC):
                            m = pe.matmul(p_f[:, jj * GT:(jj + 1) * GT], wx_s[:, c, col:col + P],
                                          xs[p][:, c, :, :].rearrange("p b s -> p (b s)"),
                                          start=c == 0, stop=c == JC - 1)
                    m.then_inc(fj_done, 1)
                if 11 <= n < 13:
                    b = n - 11
                    job(8 + b)
                    pe.wait_ge(dtx_done, f + 1)
                    for j in range(JC):
                        t = pe.transpose(p_f[:, j * P:(j + 1) * P], dtx[:, j, b, :], ident[:])
                    t.then_inc(fj_done, 1)

            def turn_u(g, p, n):
                k = g * NS + n
                pe.wait_ge(u_done, k + 1)
                need(pe, scan_done, k - 1)
                for j in range(JC):
                    for b in range(GB):
                        t = pe.transpose(p_bx[n % 2][:, j, b, :], u[n % LAG][:, b, j * P:(j + 1) * P], ident[:])
                t.then_inc(bx_done, 1)

            def turn_h(g, p, n):
                k = g * NS + n
                pe.wait_ge(scan_done, k + 1)
                for b in range(GB):
                    need(pe, acc_done, (k - 1) * GB + b + 1)
                    for j in range(JC):
                        t = pe.transpose(p_y[b][:, j * P:(j + 1) * P], h[n % LAG][:, j, b, :], ident[:])
                    t.then_inc(yt_done, 1)

            def turn_rows(rows):
                for c in range(KC):
                    for b in range(GB):
                        t = pe.transpose(p_b[:, (c * GB + b) * P:(c * GB + b + 1) * P],
                                         rows[:, b, c * P:(c + 1) * P], ident[:])
                t.then_inc(bj_done, 1)

            def back(q, p, n, at=(0, 1)):
                def job(k):
                    need(pe, be_done, q * BJ + k)

                def sum_turned(k):
                    job(J_SUM + k)
                    pe.wait_ge(acc_done, (q + 1) * NS * GB)
                    for jj in range(2):
                        j = 2 * k + jj
                        for b in range(GB):
                            t = pe.transpose(p_b[:, (jj * GB + b) * P:(jj * GB + b + 1) * P],
                                             acc[p][:, b, j * P:(j + 1) * P], ident[:])
                    t.then_inc(bj_done, 1)

                def scores(b, k):
                    job(J_SCORE[b] + k)
                    pe.wait_ge(kbd_ready, (q + 1) * 16 * HPC * GB)
                    c, half = k // 2, k % 2
                    pe.matmul(p_b[:], x1T[:, c, b, :],
                              kbd[:, b, c, 4 * half:4 * half + 4, :].rearrange("p h s -> p (h s)"),
                              start=True, stop=True).then_inc(bj_done, 1)

                def weights_turned(b, k):
                    job(J_TURN[b] + k)
                    pe.wait_ge(exp_done, GB * q + b + 1)
                    for hh in range(4):
                        t = pe.transpose(p_b[:, hh * P:(hh + 1) * P], s_s[b][:, 4 * k + hh, :], ident[:])
                    t.then_inc(bj_done, 1)

                def attend(b):
                    job(J_ATT[b])
                    pe.wait_ge(vaug_done, q + 1)
                    for hh in range(HEADS):
                        m = pe.matmul(p_b[:, hh * VW:(hh + 1) * VW], pT[:, hh, :], vaug[:, b, hh, :],
                                      start=True, stop=True)
                    m.then_inc(bj_done, 1)

                for side in at:
                    if n == 0:
                        sum_turned(side)
                    if n == 1 and side == 1:
                        job(J_OUT)
                        pe.wait_ge(yg_done, q + 1)
                        for b in range(GB):
                            for j in range(JC):
                                m = pe.matmul(p_b[:, b * DM:(b + 1) * DM], y[:, j, b, :], wo_s[:, j, :],
                                              start=j == 0, stop=j == JC - 1)
                        m.then_inc(bj_done, 1)
                    if n == 2 and side == 1:
                        job(J_X1T)
                        pe.wait_ge(x1_done, q + 1)
                        turn_rows(x1)
                    if 3 <= n < 7:
                        scores((n - 3) // 2, ((n - 3) % 2) * 2 + side)
                    if 7 <= n < 9:
                        weights_turned(0, (n - 7) * 2 + side)
                    if n == 9 and side == 0:
                        attend(0)
                    if 9 <= n < 12 and 0 <= 2 * (n - 9) + side - 1 < 4:
                        weights_turned(1, 2 * (n - 9) + side - 1)
                    if n == 11 and side == 1:
                        attend(1)
                    if n == 13 and side == 0:
                        job(J_X2T)
                        pe.wait_ge(x2_done, q + 1)
                        turn_rows(x2)
                    if n == 14 and side == 0:
                        job(J_RH)
                        for m_ in range(KC):
                            for c in range(KC):
                                m = pe.matmul(p_b[:, m_ * GT:(m_ + 1) * GT], rw1_s[:, c, m_ * P:(m_ + 1) * P],
                                              x2T[:, c, :, :].rearrange("p b s -> p (b s)"),
                                              start=c == 0, stop=c == KC - 1)
                        m.then_inc(bj_done, 1)
                    if n == 15 and side == 0:
                        job(J_LOGIT)
                        for b in range(GB):
                            for c in range(KC):
                                m = pe.matmul(p_b[:, b * NE:(b + 1) * NE], rh[:, c, b, :], rw2_s[:, c, :],
                                              start=c == 0, stop=c == KC - 1)
                        m.then_inc(bj_done, 1)

            def start():
                turn_u(0, 0, 0)
                turn_u(0, 0, 1)

            def slot(g, p, n, first=False, last=False):
                turn_h(g, p, n)
                if not (last and n >= NS - 2):
                    turn_u(*ahead(g, p, n, 2))
                if not first:
                    back(g - 1, 1 - p, n, at=(0,))
                if not last:
                    front(g + 1, 1 - p, n)
                if not first:
                    back(g - 1, 1 - p, n, at=(1,))

            pe.wait_ge(prepared, 1)
            all_groups(pe, front, start, slot, back)

            pe.wait_ge(route_c, 4)
            pe.wait_ge(route, R_PICKS)
            flat = picks[:].rearrange("p b e -> p (b e)")
            pe.matmul(p_h[0][:, 0:BATCH * NE], lower[:], flat, start=True, stop=True)
            pe.matmul(p_h[1][:, 0:BATCH * NE], ones_sq[:], flat, start=True, stop=True).then_inc(ranks, 1)

            def turn_x(m, k):
                i = m * 2 + k
                pe.wait_ge(xt_ready[k], (m + 1) * 16)
                need(pe, xtT_done, i - 1)
                for c in range(KC):
                    t = pe.transpose(p_x[k][:, c * P:(c + 1) * P], xt[k][:, c * P:(c + 1) * P], ident[:])
                t.then_inc(xt_turned, 1)

            def up(i, k, e):
                pe.wait_ge(xtT_done, i + 1)
                for half in range(2):
                    need(pe, upb_done, (i - 1) * 2 + half + 1)
                    for c in range(KC):
                        m = pe.matmul(p_h[half][:], xtT[k][:, c, :],
                                      w1_s[:, bass.ds(e * (KC * FH) + (c * FH + half * 512), 512)],
                                      start=c == 0, stop=c == KC - 1)
                    m.then_inc(up_done, 1)

            def turn_hs(i, k):
                pe.wait_ge(hs_done, i + 1)
                for half in range(2):
                    need(pe, hT_done, (i - 1) * 2 + half + 1)
                    for c in range(4):
                        col = (half * 4 + c) * P
                        t = pe.transpose(p_hT[half][:, c * P:(c + 1) * P], hs[k][:, col:col + P], ident[:])
                    t.then_inc(ht_turned, 1)

            def down(i, k, e):
                need(pe, yo_done, i - 1)
                for half in range(2):
                    pe.wait_ge(hT_done, i * 2 + (half + 1))
                    for c in range(half * 4, half * 4 + 4):
                        m = pe.matmul(p_o[k][:, 0:DM], hT[:, c, :],
                                      w2_s[:, bass.ds(e * (HC * DM) + c * DM, DM)],
                                      start=c == 0, stop=c == HC - 1)
                m.then_inc(down_done, 1)

            def expert_of(i):
                return pe.value_load(tile_expert[0:1, bass.ds(i, 1)], min_val=0, max_val=NE - 1)

            def tile(m, k, first=False, last=False):
                i = m * 2 + k
                if not last:
                    turn_x(m + k, 1 - k)
                if not first:
                    turn_hs(i - 1, 1 - k)
                e = expert_of(i)
                up(i, k, e)
                if not first:
                    down(i - 1, 1 - k, expert_of(i - 1))

            for e in range(NE):
                pe.wait_ge(w1_ready[e], 16)
                pe.wait_ge(w2_ready[e], 16)
            turn_x(0, 0)
            tile(0, 0, first=True)
            tile(0, 1)
            with pe.Fori(1, TILES // 2) as m:
                tile(m, 0)
                tile(m, 1)
            tile(TILES // 2, 0, last=True)
            turn_hs(TILES - 1, 0)
            down(TILES - 1, 0, expert_of(TILES - 1))

        @block.scalar
        def _(act):
            def front(f, p, n):
                fj = f * FJ

                def read_out(k, to, of):
                    act.wait_ge(fj_done, fj + (k + 1))
                    act.activation(to, of, ACT.Copy).then_inc(fe_done, 1)

                if n == 0:
                    act.wait_ge(xf_ready, (f + 1) * 16)
                    need(act, rms_step, 3 * f)
                    for b in range(GB):
                        s = act.activation(sq_junk[:], xf[:, b, :], ACT.Square, scale=DM ** -0.5,
                                           accum_out=ssq[:, b:b + 1])
                        s.then_inc(ssq_done, 1)
                        act.wait_ge(ssq_done, GB * f + b + 1)
                if n == 2:
                    read_out(0, xnT[:].rearrange("p c b s -> p (c b s)"), p_f[:])
                if 3 <= n < 5:
                    k = n - 3
                    read_out(1 + k, xpad[:, 2 * k:2 * k + 2, :, TAPS - 1:].rearrange("p j b s -> p (j b) s"),
                             p_f[:].rearrange("p (a s) -> p a s", s=SEQ))
                if 5 <= n < 7:
                    k = n - 5
                    read_out(3 + k, sz[p][:, 2 * k:2 * k + 2].rearrange("p j b s -> p (j b s)"), p_f[:])
                if n == 6:
                    act.wait_ge(conv_step, (f + 1) * TAPS)
                    act.wait_ge(fe_done, fj + 5)
                    act.activation(xs[p][:], xc[:], ACT.Silu).then_inc(silu_done, 1)
                    act.activation(sz[p][:], sz[p][:], ACT.Silu)
                    act.preload_act_table_set("natural_log_exp_and_others")
                if 8 <= n < 10:
                    k = n - 8
                    act.wait_ge(fj_done, fj + (6 + k))
                    to = slice(2 * k, 2 * k + 2)
                    act.activation(dabs[:, to].rearrange("p j b s -> p (j b s)"), p_f[:], ACT.Abs).then_inc(sp_step, 1)
                    act.activation(dpos[:, to].rearrange("p j b s -> p (j b s)"), p_f[:], ACT.Relu).then_inc(fe_done, 1)
                if n == 9:
                    act.wait_ge(sp_step, f * 4 + 2)
                    act.activation(dabs[:], dabs[:], ACT.Exp, scale=-1.0).then_inc(sp_step, 1)
                    act.wait_ge(sp_step, f * 4 + 3)
                    act.activation(dabs[:], dabs[:], ACT.Ln, bias=ones_col[:]).then_inc(sp_step, 1)
                if n == 12:
                    for b in range(GB):
                        read_out(8 + b, dtxT[p][:, b, :], p_f[:])

            def decay(g, p, n):
                k = g * NS + n
                act.wait_ge(dt_done, g + 1)
                need(act, scan_done, k - 1)
                for j in range(JC):
                    a = act.activation(da[n % LAG][:, j, :, 1:], dt[p][:, j, :, 1:], ACT.Exp,
                                       scale=a_s[:, j, n:n + 1])
                a.then_inc(da_done, 1)

            def back(q, p, n, at=(0, 1)):
                bj = q * BJ

                def read_out(k, to, of):
                    act.wait_ge(bj_done, bj + (k + 1))
                    act.activation(to, of, ACT.Copy).then_inc(be_done, 1)

                def weights(b):
                    act.wait_ge(ssub_done, GB * q + b + 1)
                    act.activation(s_s[b][:], s_s[b][:], ACT.Exp).then_inc(exp_done, 1)

                def turned(b, k):
                    read_out(J_TURN[b] + k, pT[:, 4 * k:4 * k + 4, :].rearrange("p h s -> p (h s)"), p_b[:])

                if 0 in at:
                    if n == 3:
                        read_out(J_X1T, x1T[:].rearrange("p c b s -> p (c b s)"), p_b[:])
                    if n in (8, 9):
                        turned(0, (n - 8) * 2 + 1)
                    if n in (10, 11):
                        turned(1, (n - 10) * 2)
                if 1 in at:
                    if n in (6, 8):
                        weights((n - 6) // 2)
                    if n in (7, 8):
                        turned(0, (n - 7) * 2)
                    if n in (10, 11):
                        turned(1, (n - 10) * 2 + 1)
                    if n == 13:
                        read_out(J_X2T, x2T[:].rearrange("p c b s -> p (c b s)"), p_b[:])
                    if n == 14:
                        act.wait_ge(bj_done, bj + J_RH + 1)
                        for m in range(KC):
                            a = act.activation(rh[:, m].rearrange("p b s -> p (b s)"), p_b[:, m * GT:(m + 1) * GT],
                                               ACT.Silu, bias=rb1_s[:, m:m + 1])
                        a.then_inc(be_done, 1)
                        act.preload_act_table_set("natural_log_exp_and_others")

            def start():
                decay(0, 0, 0)
                decay(0, 0, 1)

            def slot(g, p, n, first=False, last=False):
                if not first:
                    back(g - 1, 1 - p, n, at=(0,))
                if not last:
                    front(g + 1, 1 - p, n)
                if not (last and n >= NS - 2):
                    decay(*ahead(g, p, n, 2))
                if not first:
                    back(g - 1, 1 - p, n, at=(1,))

            act.wait_ge(w_loaded, 16 * 14)
            act.activation(a_s[:], a_s[:], ACT.Exp).then_inc(a_ready, 1)
            act.wait_ge(prepared, 1)
            all_groups(act, front, start, slot, back)

            act.wait_ge(route, R_DLT)
            act.activation(e2[:], dlt[:], ACT.Exp).then_inc(gate_exp, 1)

            def tile(i, k):
                act.wait_ge(xt_turned, i + 1)
                act.activation(xtT[k][:].rearrange("p c s -> p (c s)"), p_x[k][:, 0:KC * P],
                               ACT.Copy).then_inc(xtT_done, 1)

            def hidden(i, k):
                act.wait_ge(upb_done, i * 2 + 2)
                act.activation(hs[k][:], hs[k][:], ACT.Silu).then_inc(hs_done, 1)
                act.wait_ge(ht_turned, i * 2 + 1)
                need(act, down_done, i)
                act.activation(hT[:, 0:4, :].rearrange("p c s -> p (c s)"), p_hT[0][:], ACT.Copy).then_inc(hT_done, 1)
                act.wait_ge(ht_turned, i * 2 + 2)
                act.activation(hT[:, 4:8, :].rearrange("p c s -> p (c s)"), p_hT[1][:], ACT.Copy).then_inc(hT_done, 1)

            def pair(i):
                for k in range(2):
                    tile(i * 2 + (k + 1), 1 - k)
                    hidden(i * 2 + k, k)

            tile(0, 0)
            pair(0)
            with act.Fori(1, (TILES - 1) // 2) as i:
                pair(i)
            hidden(TILES - 1, 0)

        @block.gpsimd
        def _(pool):
            pool.memset(ident[:], 0.0).then_inc(route_c, 1)
            pool.wait_ge(route_c, 1)
            pool.affine_select(out=ident[:], in_=ident[:], compare_op=ALU.not_equal, fill=1.0, base=0,
                               pattern=[[-1, P]], channel_multiplier=1)
            pool.memset(eps_pow[:], -0.5)
            pool.memset(rms_eps[:], RMS_EPS)
            pool.memset(ones_col[:], 1.0)
            pool.memset(causal[:], NEG).then_inc(route_c, 1)
            pool.wait_ge(route_c, 2)
            pool.affine_select(out=causal[:], in_=causal[:], compare_op=ALU.is_ge, fill=0.0, base=0,
                               pattern=[[-1, SEQ]], channel_multiplier=1)
            pool.memset(zrow[:], 0.0)
            pool.memset(vaug[:], 1.0)
            pool.memset(xpad[:, :, :, 0:TAPS - 1], 0.0)
            for k in range(LAG):
                pool.memset(da[k][:, :, :, 0:1], 0.0)
            pool.memset(kbd[:], 0.0).then_inc(consts, 1)

            def front(f, p, n):
                if n == 0:
                    pool.wait_ge(ssq_done, (f + 1) * GB)
                    pool.tensor_tensor(msq[:], ssq[:], rms_eps[:], ALU.add).then_inc(rms_step, 1)
                    pool.wait_ge(rms_step, f * 3 + 1)
                    need(pool, xn_done, f)
                    pool.tensor_tensor(rrms[:], msq[:], eps_pow[:, 0:GB], ALU.pow).then_inc(rms_step, 2)

            def input_of(g, p, n):
                k = g * NS + n
                if n == 0:
                    pool.wait_ge(fe_done, (g + 1) * FJ)
                need(pool, bx_done, k - 1)
                pool.tensor_tensor(u[n % LAG][:], dtxT[p][:], bc[p][:, :, n:n + 1].broadcast_to([P, GB, DI]),
                                   ALU.mult).then_inc(u_done, 1)

            def back(q, p, n):
                if n == 1:
                    pool.wait_ge(be_done, q * BJ + J_SUM + 2)
                    pool.wait_ge(fe_done, q * FJ + 7)
                    pool.tensor_tensor(y[:], y[:], sz[p][:], ALU.mult).then_inc(yg_done, 1)
                if n == 2:
                    pool.wait_ge(ctx_ready, (q + 1) * 16)
                    pool.wait_ge(var_done, q * 2 + 1)
                    pool.tensor_tensor(rstd[:], var[:], eps_pow[:, 0:GB], ALU.pow).then_inc(rstd_done, 1)
                    pool.tensor_copy(vaug[:, :, :, 0:HD].rearrange("p b h d -> p (b h) d"),
                                     ctx_s[:].rearrange("p b (h d) -> p (b h) d", d=HD)).then_inc(vaug_done, 1)
                if n in (5, 7):
                    b = (n - 5) // 2
                    pool.wait_ge(smax_done, GB * q + b + 1)
                    pool.tensor_tensor(s_s[b][:], s_s[b][:], smax[b][:].unsqueeze(2).broadcast_to([P, HEADS, SEQ]),
                                       ALU.subtract).then_inc(ssub_done, 1)
                if n == 12:
                    pool.wait_ge(var_done, q * 2 + 2)
                    pool.tensor_tensor(rstd2[:], var2[:], eps_pow[:, 0:GB], ALU.pow).then_inc(rstd_done, 1)

            def start():
                input_of(0, 0, 0)
                input_of(0, 0, 1)
                input_of(0, 0, 2)

            def slot(g, p, n, first=False, last=False):
                if not last:
                    front(g + 1, 1 - p, n)
                if not (last and n >= NS - 3):
                    input_of(*ahead(g, p, n, 3))
                if not first:
                    back(g - 1, 1 - p, n)

            pool.wait_ge(prepared, 1)
            all_groups(pool, front, start, slot, back)

            pool.wait_ge(be_done, BJ * NG)
            pool.iota(iota_e[:], pattern=[[1, NE]], base=0, channel_multiplier=0, allow_small_or_imprecise_dtypes=True)
            pool.iota(iota_i[:], pattern=[[1, TILES]], base=0, channel_multiplier=0,
                      allow_small_or_imprecise_dtypes=True)
            pool.memset(ones_sq[:], 1.0)
            pool.memset(keep_on[:], 1.0).then_inc(route_c, 1)
            pool.wait_ge(route_c, 3)
            pool.memset(keep_on[:, :, 0:1], 0.0)
            pool.affine_select(out=lower[:], in_=ones_sq[:], compare_op=ALU.is_ge, fill=0.0, base=-1,
                               pattern=[[1, P]], channel_multiplier=-1).then_inc(route_c, 1)

            pool.wait_ge(zero_rows, 16)
            pool.wait_ge(route, N_ROUTE)
            for b in range(BATCH):
                for k in range(TOPK):
                    pool.indirect_dma_start(
                        out=xs_dram[:, :], out_offset=bass.IndirectOffsetOnAxis(ap=slots_i[:, k, b:b + 1], axis=0),
                        in_=x2_all[:, b, :], in_offset=None).then_inc(scattered, 16)
            for k in range(2):
                pool.wait_ge(ys_stored[k], 16 * ((TILES + 1 - k) // 2))
            for b in range(BATCH):
                for k in range(TOPK):
                    pool.indirect_dma_start(
                        out=yg[k][:, b, :], out_offset=None, in_=ys_dram[:, :],
                        in_offset=bass.IndirectOffsetOnAxis(ap=slots_i[:, k, b:b + 1], axis=0)).then_inc(gathered[b], 16)
            pool.wait_ge(mix_step, 4 * BATCH + 1)
            pool.tensor_tensor(rstd3[:], var3[:], eps_pow[:], ALU.pow).then_inc(fin_rstd, 1)

        @block.vector
        def _(dve):
            def front(f, p, n):
                fj = f * FJ
                if n == 0:
                    dve.wait_ge(rms_step, f * 3 + 3)
                    for b in range(GB):
                        s = dve.tensor_scalar(xn[:, b, :], xf[:, b, :], rrms[:, b:b + 1], None, ALU.mult)
                    s.then_inc(xn_done, 1)
                if n in (4, 5):
                    for k in ((0, 1, 2), (3,))[n - 4]:
                        if k:
                            dve.wait_ge(conv_step, f * TAPS + k)
                        else:
                            dve.wait_ge(fe_done, fj + 3)
                            need(dve, silu_done, f)
                        for j in range(JC):
                            of, w = xpad[:, j, :, k:k + SEQ], convw_s[:, j, k:k + 1]
                            if k == 0:
                                s = dve.tensor_scalar(xc[:, j], of, w, convb_s[:, j:j + 1], ALU.mult, ALU.add)
                            else:
                                s = dve.scalar_tensor_tensor(out=xc[:, j], in0=of, scalar=w, in1=xc[:, j],
                                                             op0=ALU.mult, op1=ALU.add)
                        s.then_inc(conv_step, 1)
                if n == 10:
                    dve.wait_ge(fj_done, fj + 8)
                    dve.tensor_copy(bc[p][:].rearrange("p b n -> p (b n)"), p_f[:, 0:GB * 2 * NS]).then_inc(fe_done, 1)
                if n == 10:
                    dve.wait_ge(sp_step, f * 4 + 4)
                    dve.tensor_tensor(dt[p][:], dpos[:], dabs[:], ALU.add).then_inc(dt_done, 1)
                    dve.wait_ge(dt_done, f + 1)
                    dve.tensor_tensor(dtx[:], dt[p][:], xs[p][:], ALU.mult).then_inc(dtx_done, 1)

            def scan(g, p, n):
                k = g * NS + n
                dve.wait_ge(da_done, k + 1)
                dve.wait_ge(bx_done, k + 1)
                need(dve, yt_done, (k - 1) * GB)
                dve.tensor_tensor_scan(out=h[n % LAG][:].rearrange("p j b s -> p (j b s)"),
                                       data0=da[n % LAG][:].rearrange("p j b s -> p (j b s)"),
                                       data1=p_bx[n % 2][:].rearrange("p j b s -> p (j b s)"),
                                       initial=0.0, op0=ALU.mult, op1=ALU.add).then_inc(scan_done, 1)

            def sum_states(g, p, n):
                k = g * NS + n
                for b in range(GB):
                    dve.wait_ge(yt_done, k * GB + (b + 1))
                    c = bc[p][:, b, NS + n:NS + n + 1]
                    if n == 0:
                        dve.tensor_scalar(acc[p][:, b, :], p_y[b][:], c, None, ALU.mult).then_inc(acc_done, 1)
                    else:
                        dve.wait_ge(acc_done, (k - 1) * GB + (b + 1))
                        dve.scalar_tensor_tensor(out=acc[p][:, b, :], in0=p_y[b][:], scalar=c, in1=acc[p][:, b, :],
                                                 op0=ALU.mult, op1=ALU.add).then_inc(acc_done, 1)

            def norm_stats(src, st, m, vr, done):
                for b in range(GB):
                    s = dve.bn_stats(st[:, b, :], src[:, b, :])
                s.then_inc(ln_step, 1)
                dve.wait_ge(ln_step, done + 1)
                dve.tensor_copy(counts[:], st[:, :, 0:1].rearrange("p b o -> p (b o)"))
                for b in range(GB):
                    s = dve.bn_aggr(m[:, b, :], st[:, b, :])
                s.then_inc(ln_step, 1)
                dve.wait_ge(ln_step, done + 2)
                dve.tensor_scalar(vr[:], m[:, :, 1:2].rearrange("p b o -> p (b o)"), LN_EPS, None,
                                  ALU.add).then_inc(var_done, 1)

            def norm_apply(to, src, m, rs):
                for b in range(GB):
                    s = dve.tensor_scalar(to[:, b, :], src[:, b, :], m[:, b, 0:1], rs[:, b:b + 1],
                                          ALU.subtract, ALU.mult)
                return s

            def back(q, p, n, at=(0, 1)):
                bj = q * BJ

                def sum_read(k):
                    dve.wait_ge(bj_done, bj + J_SUM + (k + 1))
                    for jj in range(2):
                        j = 2 * k + jj
                        s = dve.scalar_tensor_tensor(out=y[:, j].rearrange("p b s -> p (b s)"),
                                                     in0=xs[p][:, j].rearrange("p b s -> p (b s)"),
                                                     scalar=dpar_s[:, j:j + 1], in1=p_b[:, jj * GT:(jj + 1) * GT],
                                                     op0=ALU.mult, op1=ALU.add)
                    s.then_inc(be_done, 1)

                def scores(b, k):
                    dve.wait_ge(bj_done, bj + J_SCORE[b] + (k + 1))
                    bias = neg_bias[:, bass.ds(q * GB + b, 1), :].broadcast_to([P, 4, SEQ])
                    dve.scalar_tensor_tensor(out=s_s[b][:, 4 * k:4 * k + 4, :],
                                             in0=p_b[:].rearrange("p (h s) -> p h s", s=SEQ),
                                             scalar=1.0 / HD ** 0.5, in1=bias, op0=ALU.mult,
                                             op1=ALU.subtract).then_inc(be_done, 1)

                def attended(b):
                    dve.wait_ge(bj_done, bj + J_ATT[b] + 1)
                    heads = p_b[:, 0:HEADS * VW].rearrange("p (h w) -> p h w", w=VW)
                    a0 = (q * GB + b) * 3
                    dve.reciprocal(rsum[:], heads[:, :, HD:VW].rearrange("p h o -> p (h o)")).then_inc(att_step, 1)
                    dve.wait_ge(att_step, a0 + 1)
                    dve.tensor_scalar(rsum[:], rsum[:], qmask[:, bass.ds(q * GB + b, 1)], None,
                                      ALU.mult).then_inc(att_step, 1)
                    dve.wait_ge(att_step, a0 + 2)
                    dve.tensor_tensor(v2[:, b, :].rearrange("p (h d) -> p h d", d=HD), heads[:, :, 0:HD],
                                      rsum[:].unsqueeze(2).broadcast_to([P, HEADS, HD]), ALU.mult).then_inc(be_done, 1)
                    dve.wait_ge(be_done, bj + J_ATT[b] + 1)
                    dve.tensor_tensor(v2[:, b, :], v2[:, b, :], x1[:, b, :], ALU.add).then_inc(att_step, 1)

                if 0 in at:
                    if n == 1:
                        sum_read(1)
                    if n == 2:
                        dve.wait_ge(bj_done, bj + J_OUT + 1)
                        dve.wait_ge(xb_ready, (q + 1) * 16)
                        dve.scalar_tensor_tensor(out=v[:].rearrange("p b d -> p (b d)"),
                                                 in0=xb[:].rearrange("p b d -> p (b d)"), scalar=2.0, in1=p_b[:],
                                                 op0=ALU.mult, op1=ALU.add).then_inc(be_done, 1)
                        dve.wait_ge(be_done, bj + J_OUT + 1)
                        norm_stats(v, stats, mv, var, q * 4)
                    if n in (4, 6):
                        scores((n - 4) // 2, 1)
                    if n in (5, 7):
                        b = (n - 5) // 2
                        scores(b, 3)
                        dve.wait_ge(be_done, bj + J_SCORE[b] + 4)
                        dve.tensor_reduce(smax[b][:], s_s[b][:], X, ALU.max).then_inc(smax_done, 1)
                    if n == 12:
                        attended(1)
                        dve.wait_ge(att_step, (q + 1) * 3 * GB)
                        norm_stats(v2, stats2, mv2, var2, q * 4 + 2)
                if 1 in at:
                    if n == 0:
                        sum_read(0)
                    if n == 2:
                        dve.wait_ge(rstd_done, q * 2 + 1)
                        norm_apply(x1, v, mv, rstd).then_inc(x1_done, 1)
                    if 3 <= n < 7:
                        scores((n - 3) // 2, ((n - 3) % 2) * 2)
                    if n == 9:
                        attended(0)
                    if n == 12:
                        dve.wait_ge(rstd_done, q * 2 + 2)
                        need(dve, x2_kept, q * 16)
                        norm_apply(x2, v2, mv2, rstd2).then_inc(x2_done, 1)
                    if n == 15:
                        dve.wait_ge(bj_done, bj + J_LOGIT + 1)
                        dve.tensor_tensor(logits[:, bass.ds(q * GB, GB), :],
                                          p_b[:, 0:GB * NE].rearrange("p (b e) -> p b e", e=NE),
                                          rb2_s[:].unsqueeze(1).broadcast_to([P, GB, NE]), ALU.add).then_inc(be_done, 1)

            def slot(g, p, n, first=False, last=False):
                if not (last and n == NS - 1):
                    scan(*ahead(g, p, n, 1))
                if not first:
                    back(g - 1, 1 - p, n, at=(0,))
                sum_states(g, p, n)
                if not last:
                    front(g + 1, 1 - p, n)
                if not first:
                    back(g - 1, 1 - p, n, at=(1,))

            dve.wait_ge(w_loaded, 16 * 14)
            for c in range(KC):
                dve.tensor_scalar(w_in_s[:, c, :], w_in_s[:, c, :], norm_s[:, c:c + 1], None, ALU.mult)
            dve.wait_ge(a_ready, 1)
            dve.tensor_scalar(a_s[:], a_s[:], -1.0, None, ALU.mult)
            dve.tensor_copy(qmask[:], maskt_s[:])
            dve.wait_ge(consts, 1)
            dve.tensor_tensor(neg_bias[:], mask_s[:], causal[:].unsqueeze(1).broadcast_to([P, BATCH, SEQ]),
                              ALU.mult).then_inc(prepared, 1)
            all_groups(dve, front, lambda: scan(0, 0, 0), slot, back)

            steps = [0]

            def step(ins):
                ins.then_inc(route, 1)
                steps[0] += 1
                dve.wait_ge(route, steps[0])

            dve.wait_ge(be_done, BJ * NG)
            dve.wait_ge(x2_kept, 16 * NG)
            for b in range(BATCH):
                s = dve.max(m8[:, b, :], logits[:, b, :])
            step(s)
            for b in range(BATCH):
                s = dve.max_index(mi[:, b, :], m8[:, b, :], logits[:, b, :])
            step(s)
            step(dve.tensor_tensor(dlt[:], m8[:, :, 1], m8[:, :, 0], ALU.subtract))
            assert steps[0] == R_DLT
            step(dve.tensor_copy(mif[:], mi[:, :, 0:TOPK]))
            dve.wait_ge(route_c, 4)
            for k in range(TOPK):
                s = dve.tensor_tensor(pick[k][:], mif[:, :, k:k + 1].broadcast_to([P, BATCH, NE]),
                                      iota_e[:].unsqueeze(1).broadcast_to([P, BATCH, NE]), ALU.is_equal)
            step(s)
            step(dve.tensor_tensor(picks[:], pick[0][:], pick[1][:], ALU.add))
            assert steps[0] == R_PICKS
            dve.wait_ge(ranks, 1)
            step(dve.tensor_copy(tot[:], p_h[1][:, 0:BATCH * NE].rearrange("p (b e) -> p e b", e=NE)))
            step(dve.tensor_tensor_scan(out=incl[:].rearrange("p e b -> p (e b)"),
                                        data0=keep_on[:].rearrange("p e b -> p (e b)"),
                                        data1=tot[:].rearrange("p e b -> p (e b)"), initial=0.0,
                                        op0=ALU.mult, op1=ALU.add))
            step(dve.tensor_scalar(cnt_f[:], incl[:, :, BATCH - 1], float(P - 1), None, ALU.add))
            step(dve.tensor_copy(cnt_i[:], cnt_f[:]))
            step(dve.tensor_single_scalar(nt_i[:], cnt_i[:], 7, ALU.arith_shift_right))
            step(dve.tensor_copy(nt_f[:], nt_i[:]))
            step(dve.tensor_tensor_scan(out=cum[:], data0=ones_sq[:, 0:NE], data1=nt_f[:], initial=0.0,
                                        op0=ALU.mult, op1=ALU.add))
            step(dve.tensor_tensor(base[:], cum[:], nt_f[:], ALU.subtract))
            step(dve.tensor_scalar(base[:], base[:], float(P), None, ALU.mult))
            step(dve.tensor_tensor(incl[:], incl[:], tot[:], ALU.subtract))
            step(dve.tensor_tensor(incl[:], incl[:], base[:].unsqueeze(2).broadcast_to([P, NE, BATCH]), ALU.add))
            step(dve.tensor_tensor(row[:], p_h[0][:, 0:BATCH * NE].rearrange("p (b e) -> p b e", e=NE),
                                   incl[:].rearrange("p e b -> p b e"), ALU.add))
            for k in range(TOPK):
                s = dve.tensor_tensor(rowk[k][:], row[:], pick[k][:], ALU.mult)
            step(s)
            for k in range(TOPK):
                s = dve.tensor_reduce(rowf[:, k, :], rowk[k][:], X, ALU.add)
            step(s)
            step(dve.tensor_copy(slots_i[:], rowf[:]))
            step(dve.tensor_tensor(ge[:], iota_i[:].unsqueeze(2).broadcast_to([P, TILES, NE - 1]),
                                   cum[:, 0:NE - 1].unsqueeze(1).broadcast_to([P, TILES, NE - 1]), ALU.is_ge))
            step(dve.tensor_reduce(te_f[:], ge[:], X, ALU.add))
            step(dve.tensor_copy(tile_expert[:], te_f[:]))
            dve.wait_ge(gate_exp, 1)
            step(dve.tensor_scalar(e2p[:], e2[:], 1.0, None, ALU.add))
            step(dve.reciprocal(gate[:, 0, :], e2p[:]))
            step(dve.tensor_tensor(gate[:, 1, :], gate[:, 0, :], e2[:], ALU.mult))
            assert steps[0] == N_ROUTE, steps[0]

            def add_b1(m, k):
                i = m * 2 + k
                dve.wait_ge(b1_ready[k], (m + 1) * 16)
                need(dve, ht_turned, (i - 1) * 2)
                for half in range(2):
                    dve.wait_ge(up_done, i * 2 + (half + 1))
                    dve.tensor_tensor(hs[k][:, half * 512:(half + 1) * 512], p_h[half][:],
                                      b1_s[k][:, half * 512:(half + 1) * 512], ALU.add).then_inc(upb_done, 1)

            def add_b2(m, k):
                i = m * 2 + k
                dve.wait_ge(down_done, i + 1)
                dve.wait_ge(b2_ready[k], (m + 1) * 16)
                need(dve, ys_stored[k], m * 16)
                dve.tensor_tensor(yo[k][:], p_o[k][:, 0:DM], b2_s[k][:], ALU.add).then_inc(yo_done, 1)

            def pair(m):
                for k in range(2):
                    add_b1(m + k, 1 - k)
                    add_b2(m, k)

            add_b1(0, 0)
            pair(0)
            with dve.Fori(1, (TILES - 1) // 2) as i:
                pair(i)
            add_b2(TILES // 2, 0)

            for b in range(BATCH):
                dve.wait_ge(gathered[b], 32)
                dve.tensor_scalar(v3[:, b, :], x2_all[:, b, :], 2.0, None, ALU.mult).then_inc(mix_step, 1)
                for k in range(TOPK):
                    dve.wait_ge(mix_step, 4 * b + 1 + k)
                    dve.scalar_tensor_tensor(out=v3[:, b, :], in0=yg[k][:, b, :], scalar=gate[:, k, b:b + 1],
                                             in1=v3[:, b, :], op0=ALU.mult, op1=ALU.add).then_inc(mix_step, 1)
                dve.wait_ge(mix_step, 4 * b + 3)
                dve.bn_stats(stats3[:, b, :], v3[:, b, :]).then_inc(mix_step, 1)
            dve.wait_ge(mix_step, 4 * BATCH)
            for b in range(BATCH):
                s = dve.bn_aggr(mv3[:, b, :], stats3[:, b, :])
            s.then_inc(route, 1)
            dve.wait_ge(route, N_ROUTE + 1)
            dve.tensor_scalar(var3[:], mv3[:, :, 1], LN_EPS, None, ALU.add).then_inc(mix_step, 1)
            dve.wait_ge(fin_rstd, 1)
            for b in range(BATCH):
                dve.tensor_scalar(res[:, b, :], v3[:, b, :], mv3[:, b, 0:1], rstd3[:, b:b + 1],
                                  ALU.subtract, ALU.mult).then_inc(fin_done, 1)


R_DLT, R_PICKS, N_ROUTE = 3, 6, 27


def x_rows(t, g):
    return t[bass.ds(g * GB, GB)].rearrange("b s d -> s b d")


def kernel(x, ctx_1024, mask_BxS2_bf1, L0_attn_norm_w, L0_attn_w_in, L0_attn_conv_w, L0_attn_conv_b,
           L0_attn_w_xproj, L0_attn_A_log, L0_attn_D_param, L0_attn_w_out, L0_ffn_rw1, L0_ffn_rb1, L0_ffn_rw2,
           L0_ffn_rb2, L0_ffn_we1, L0_ffn_be1, L0_ffn_we2, L0_ffn_be2):
    import concourse.bacc as bacc
    from concourse.bass_utils import run_bass_kernel_spmd

    ctx = np.asarray(ctx_1024)
    mask = np.asarray(mask_BxS2_bf1).view(np.uint8)
    arrays = {
        "x": x, "ctxk": ctx,
        "ctxt": ctx.transpose(0, 2, 1).reshape(BATCH, KC, P, SEQ).transpose(0, 2, 1, 3),
        "mask": mask, "maskt": mask.T,
        "norm_w": L0_attn_norm_w, "w_in": L0_attn_w_in, "conv_w": L0_attn_conv_w, "conv_b": L0_attn_conv_b,
        "w_xproj": L0_attn_w_xproj, "a_log": L0_attn_A_log, "d_par": L0_attn_D_param, "w_out": L0_attn_w_out,
        "rw1": L0_ffn_rw1, "rb1": L0_ffn_rb1, "rw2": L0_ffn_rw2, "rb2": L0_ffn_rb2,
        "we1": L0_ffn_we1, "be1": L0_ffn_be1, "we2": L0_ffn_we2, "be2": L0_ffn_be2,
    }
    arrays = {f"in_{n}": np.ascontiguousarray(a) for n, a in arrays.items()}
    nc = bacc.Bacc("TRN2", target_bir_lowering=False, num_devices=1)
    args = [nc.dram_tensor(n, a.shape, mybir.dt.from_np(a.dtype), kind="ExternalInput").ap()
            for n, a in arrays.items()]
    out = nc.dram_tensor("out", [BATCH, SEQ, DM], F32, kind="ExternalOutput").ap()
    decoder_layer(nc, *args, out)
    r = run_bass_kernel_spmd(nc, [arrays], core_ids=[0])
    return r.results[0]["out"]
```

```python
from contextlib import ExitStack

import concourse.bass as bass
import numpy as np
from concourse import mybir

F32 = mybir.dt.float32
U8 = mybir.dt.uint8
I32 = mybir.dt.int32
U32 = mybir.dt.uint32
F32R = mybir.dt.float32r
ALU = mybir.AluOpType
ACT = mybir.ActivationFunctionType
X = mybir.AxisListType.X

P = 128
BATCH, SEQ, DM = 16, 128, 256
DI = 512
NS = 16
TAPS = 4
HEADS, HD = 16, 16
NE, FH, TOPK = 8, 1024, 2
GB = 2
NG = BATCH // GB
GT = GB * SEQ
KC = DM // P
JC = DI // P
HC = FH // P
HPC = P // HD
VW = HD + 1
DS = 2
FB = 4
EW = KC * FH + HC * DM
Q = 32
NEG = 999999.0
RMS_EPS, LN_EPS = 1e-6, 1e-5
TOKENS = BATCH * SEQ
TILES = (TOKENS * TOPK + NE * (P - 1)) // P
FJ = 9
CJ = 8
SJ = 4
AJ = 15
F_XNT, F_IN, F_DELTA, F_B, F_C = 0, 1, (5, 7), 6, 8
C_SUM, C_OUT, C_X1T = 0, 2, 3
C_SCORE = [4 + 2 * b for b in range(2)]
A_TURN = [6 * b for b in range(2)]
A_ATT = [4 + 6 * b for b in range(2)]
A_ATTT = [5 + 6 * b for b in range(2)]
A_X2T, A_RH, A_LOGIT = 12, 13, 14
CHUNK = 4
LAG = 2


def decoder_layer(nc, x, ctxk, ctxt, mask, maskt, norm_w, w_in, conv_w, conv_b, w_xproj, a_log, d_par,
                  w_out, rw1, rb1, rw2, rb2, we1, be1, we2, be2, out):
    xs_dram = nc.dram_tensor("expert_rows_in", [TILES * P, DM], F32, kind="Internal").ap()
    b_dram = nc.dram_tensor("b_by_state", [NG, NS, GT], F32, kind="Internal").ap()
    ys_dram = nc.dram_tensor("expert_rows_out", [TILES * P, DM], F32, kind="Internal").ap()

    top = ExitStack()
    with top:
        def sem(name):
            return top.enter_context(nc.semaphore(name))

        def keep(name, shape, dt=F32):
            return top.enter_context(nc.sbuf_tensor(name, shape, dt))

        ident = keep("ident", [P, P])
        x2_all = keep("x2_all", [P, BATCH, DM])
        logits = keep("logits", [P, BATCH, NE])
        eps_pow = keep("eps_pow", [P, BATCH])
        rms_eps = keep("rms_eps", [P, GB])
        ones_col = keep("ones_col", [P, 1])
        qmask = keep("qmask", [P, BATCH])
        slots_i = keep("slots_i", [P, TOPK, BATCH], U32)
        gate = keep("gate", [P, TOPK, BATCH])
        tile_expert = keep("tile_expert", [P, TILES], I32)

        grp = ExitStack()

        def sb(name, shape, dt=F32):
            return grp.enter_context(nc.sbuf_tensor(name, shape, dt))

        w_in_s = sb("w_in_s", [P, KC, 2 * DI])
        wx_s = sb("wx_s", [P, JC, 2 * NS + DI])
        xf = sb("xf", [P, GB, DM])
        xn = sb("xn", [P, GB, DM])
        xnT = sb("xnT", [P, KC, GB, SEQ])
        xpad = sb("xpad", [P, JC, GB, TAPS - 1 + SEQ])
        xc = sb("xc", [P, JC, GB, SEQ])
        dabs = sb("dabs", [P, JC, GB, SEQ])
        dpos = sb("dpos", [P, JC, GB, SEQ])
        norm_s = sb("norm_s", [P, KC])
        convw_s = sb("convw_s", [P, JC, TAPS])
        convb_s = sb("convb_s", [P, JC])
        sq_junk = sb("sq_junk", [P, DM])
        dt = [sb(f"dt{i}", [P, JC, GB, SEQ]) for i in range(2)]
        dtx = [sb(f"dtx{i}", [P, JC, GB, SEQ]) for i in range(2)]
        b_all = [sb(f"b_all{i}", [P, CHUNK, GB, SEQ]) for i in range(2)]
        u = [sb(f"u{i}", [P, JC, GB, SEQ]) for i in range(LAG)]
        da = [sb(f"da{i}", [P, JC, GB, SEQ]) for i in range(LAG)]
        h = [sb(f"h{i}", [P, JC, GB, SEQ]) for i in range(LAG)]
        cc = [sb(f"cc{i}", [P, GB, NS]) for i in range(2)]
        a_s = sb("a_s", [P, JC, NS])
        wo_s = sb("wo_s", [P, JC, DM])
        dpar_s = sb("dpar_s", [P, JC])
        xs = [sb(f"xs{i}", [P, JC, GB, SEQ]) for i in range(2)]
        sz = [sb(f"sz{i}", [P, JC, GB, SEQ]) for i in range(2)]
        acc = [sb(f"acc{i}", [P, GB, DI]) for i in range(2)]
        xb = sb("xb", [P, GB, DM])
        y = sb("y", [P, JC, GB, SEQ])
        v = sb("v", [P, GB, DM])
        x1T = sb("x1T", [P, KC, GB, SEQ])
        kbd = sb("kbd", [P, GB, KC, HPC // 2, SEQ])
        neg_bias = sb("neg_bias", [P, BATCH, SEQ])
        mask_s = sb("mask_s", [P, BATCH, SEQ], U8)
        causal = sb("causal", [P, SEQ])
        rw1_s = sb("rw1_s", [P, KC, DM])
        rb1_s = sb("rb1_s", [P, KC])
        rw2_s = sb("rw2_s", [P, KC, NE])
        rb2_s = sb("rb2_s", [P, NE])
        maskt_s = sb("maskt_s", [P, BATCH], U8)
        zrow = sb("zrow", [P, DM])
        ssq = sb("ssq", [P, GB])
        msq = sb("msq", [P, GB])
        rrms = sb("rrms", [P, GB])
        b_rows = sb("b_rows", [NS, GT])
        stats = sb("stats", [P, GB, 6])
        mv = sb("mv", [P, GB, 2])
        var = sb("var", [P, GB])
        rstd = sb("rstd", [P, GB])
        counts = sb("counts", [P, GB])
        x1 = [sb(f"x1_{i}", [P, GB, DM]) for i in range(2)]
        ctx_s = sb("ctx_s", [P, GB, DM])
        vaug = sb("vaug", [P, GB, HEADS * VW + Q - VW])
        s_s = [sb(f"s_s{b}", [P, HEADS, SEQ]) for b in range(GB)]
        smax = [sb(f"smax{b}", [P, HEADS]) for b in range(GB)]
        pT = sb("pT", [P, HEADS, SEQ])
        oT = sb("oT", [P, HEADS * Q])
        rsum = sb("rsum", [P, HEADS])
        v2 = sb("v2", [P, GB, DM])
        stats2 = sb("stats2", [P, GB, 6])
        mv2 = sb("mv2", [P, GB, 2])
        var2 = sb("var2", [P, GB])
        rstd2 = sb("rstd2", [P, GB])
        x2 = sb("x2", [P, GB, DM])
        x2T = sb("x2T", [P, KC, GB, SEQ])
        rh = x2T
        grp.close()

        ex = ExitStack()

        def eb(name, shape, dt=F32):
            return ex.enter_context(nc.sbuf_tensor(name, shape, dt))

        w_s = eb("w_s", [P, NE * EW])

        rt = ExitStack()

        def rb(name, shape, dt=F32):
            return rt.enter_context(nc.sbuf_tensor(name, shape, dt))

        m8 = rb("m8", [P, BATCH, 8])
        mi = rb("mi", [P, BATCH, 8], U32)
        mif = rb("mif", [P, BATCH, TOPK])
        iota_e = rb("iota_e", [P, NE])
        iota_i = rb("iota_i", [P, TILES])
        lower = rb("lower", [P, P])
        ones_sq = rb("ones_sq", [P, P])
        pick = [rb(f"pick{k}", [P, BATCH, NE]) for k in range(TOPK)]
        picks = rb("picks", [P, BATCH, NE])
        tot = rb("tot", [P, NE, BATCH])
        keep_on = rb("keep_on", [P, NE, BATCH])
        incl = rb("incl", [P, NE, BATCH])
        cnt_f = rb("cnt_f", [P, NE])
        cnt_i = rb("cnt_i", [P, NE], I32)
        nt_i = rb("nt_i", [P, NE], I32)
        nt_f = rb("nt_f", [P, NE])
        cum = rb("cum", [P, NE])
        base = rb("base", [P, NE])
        row = rb("row", [P, BATCH, NE])
        rowk = [rb(f"rowk{k}", [P, BATCH, NE]) for k in range(TOPK)]
        rowf = rb("rowf", [P, TOPK, BATCH])
        dlt = rb("dlt", [P, BATCH])
        e2 = rb("e2", [P, BATCH])
        e2p = rb("e2p", [P, BATCH])
        ge = rb("ge", [P, TILES, NE - 1])
        te_f = rb("te_f", [P, TILES])
        rt.close()

        xt = [eb(f"xt{i}", [P, DM]) for i in range(2)]
        xh = [eb(f"xh{i}", [P, KC, P], F32R) for i in range(2)]
        xl = [eb(f"xl{i}", [P, KC, P], F32R) for i in range(2)]
        uph = [eb(f"uph{i}", [P, KC, 512], F32R) for i in range(2)]
        upl = [eb(f"upl{i}", [P, KC, 512], F32R) for i in range(2)]
        dnh = [eb(f"dnh{i}", [P, HC // 2, DM], F32R) for i in range(2)]
        dnl = [eb(f"dnl{i}", [P, HC // 2, DM], F32R) for i in range(2)]
        b1_s = [eb(f"b1_s{i}", [P, FH]) for i in range(2)]
        b2_s = [eb(f"b2_s{i}", [P, DM]) for i in range(2)]
        hs = eb("hs", [P, FH])
        hh = eb("hh", [P, HC, P], F32R)
        hl = eb("hl", [P, HC, P], F32R)
        yo = [eb(f"yo{i}", [P, DM]) for i in range(2)]
        ex.close()

        fin = ExitStack()

        def fb(name, shape, dt=F32):
            return fin.enter_context(nc.sbuf_tensor(name, shape, dt))

        yg = [fb(f"yg{k}", [P, BATCH, DM]) for k in range(TOPK)]
        v3 = fb("v3", [P, BATCH, DM])
        stats3 = fb("stats3", [P, BATCH, 6])
        mv3 = fb("mv3", [P, BATCH, 2])
        var3 = fb("var3", [P, BATCH])
        rstd3 = fb("rstd3", [P, BATCH])
        res = fb("res", [P, BATCH, DM])
        fin.close()

        pg = ExitStack()

        def pb(name, shape):
            return pg.enter_context(nc.psum_tensor(name, shape, F32))

        p_y = [[pb(f"p_y{i}_{b}", [P, DI]) for b in range(GB)] for i in range(2)]
        p_f = [pb(f"p_f{i}", [P, 512]) for i in range(2)]
        p_c = pb("p_c", [P, 512])
        p_a = pb("p_a", [P, 512])
        pg.close()
        px = ExitStack()

        def qb(name, shape):
            return px.enter_context(nc.psum_tensor(name, shape, F32))

        p_h = [qb(f"p_h{i}", [P, 512]) for i in range(2)]
        p_hT = [qb(f"p_hT{i}", [P, 512]) for i in range(2)]
        p_o = [qb(f"p_o{i}", [P, 512]) for i in range(2)]
        p_x = [qb(f"p_x{i}", [P, 512]) for i in range(2)]
        px.close()

        w_loaded = sem("w_loaded")
        zero_rows = sem("zero_rows")
        consts = sem("consts")
        prepared = sem("prepared")
        a_ready = sem("a_ready")
        xf_ready = sem("xf_ready")
        ssq_done = sem("ssq_done")
        rms_step = sem("rms_step")
        xn_done = sem("xn_done")
        fj_done = sem("fj_done")
        fe_done = [sem(f"fe_done{i}") for i in range(2)]
        conv_step = sem("conv_step")
        silu_done = sem("silu_done")
        sp_step = sem("sp_step")
        dt_done = sem("dt_done")
        dtx_done = sem("dtx_done")
        u_done = sem("u_done")
        da_done = sem("da_done")
        b_stored = sem("b_stored")
        b_ready = [sem(f"b_ready{i}") for i in range(2)]
        scan_done = sem("scan_done")
        yt_done = sem("yt_done")
        acc_done = sem("acc_done")
        xb_ready = sem("xb_ready")
        ctx_ready = sem("ctx_ready")
        kbd_ready = sem("kbd_ready")
        sj_done = sem("sj_done")
        cj_done = sem("cj_done")
        ce_done = sem("ce_done")
        aj_done = sem("aj_done")
        ae_done = sem("ae_done")
        yg_done = sem("yg_done")
        vaug_done = sem("vaug_done")
        ln_step = sem("ln_step")
        ln2_step = sem("ln2_step")
        var_done = sem("var_done")
        var2_done = sem("var2_done")
        rstd_done = sem("rstd_done")
        rstd2_done = sem("rstd2_done")
        x1_done = sem("x1_done")
        smax_done = sem("smax_done")
        ssub_done = sem("ssub_done")
        exp_done = sem("exp_done")
        att_step = sem("att_step")
        x2_done = sem("x2_done")
        x2_kept = sem("x2_kept")
        route = sem("route")
        gate_exp = sem("gate_exp")
        route_c = sem("route_c")
        ranks = sem("ranks")
        scattered = sem("scattered")
        w1_ready = [sem(f"w1_ready{e}") for e in range(NE)]
        w2_ready = [sem(f"w2_ready{e}") for e in range(NE)]
        xt_ready = [sem(f"xt_ready{k}") for k in range(2)]
        b1_ready = [sem(f"b1_ready{k}") for k in range(2)]
        b2_ready = [sem(f"b2_ready{k}") for k in range(2)]
        xt_turned = sem("xt_turned")
        up_done = sem("up_done")
        upb_done = sem("upb_done")
        hs_done = sem("hs_done")
        ht_turned = sem("ht_turned")
        hh_done = sem("hh_done")
        xh_done = sem("xh_done")
        xl_done = sem("xl_done")
        uph_done = sem("uph_done")
        upl_done = sem("upl_done")
        dnh_done = sem("dnh_done")
        dnl_done = sem("dnl_done")
        dnl_more = sem("dnl_more")
        hl_done = sem("hl_done")
        down_done = sem("down_done")
        yo_done = sem("yo_done")
        ys_stored = [sem(f"ys_stored{k}") for k in range(2)]
        gathered = [sem(f"gathered{b}") for b in range(BATCH)]
        doubled = sem("doubled")
        mix_step = sem("mix_step")
        fin_stats = sem("fin_stats")
        fin_var = sem("fin_var")
        fin_rstd = sem("fin_rstd")
        fin_done = sem("fin_done")
        stored = sem("stored")

        def need(eng, s, value):
            if isinstance(value, int) and value <= 0:
                return
            eng.wait_ge(s, value)

        def before_front(f, bank):
            if bank == 0:
                return f * ((FJ + 1) // 2)
            if isinstance(f, int) and f < 3:
                return f * (FJ // 2)
            return f * (FJ // 2 + SJ) - 2 * SJ

        def front_free(f, k):
            return fe_done[k % 2], before_front(f, k % 2) + (k // 2 + 1)

        def front_read(f, k):
            return fe_done[k % 2], before_front(f, k % 2) + (k // 2 + 2)

        def scores_free(q, k):
            if isinstance(q, int) and q + 2 >= NG:
                return fe_done[1], NG * (FJ // 2) + (q * SJ + k + 1)
            return fe_done[1], q * (FJ // 2 + SJ) + (3 * (FJ // 2) + k + 1)

        def scores_read(q, k):
            sem_, count = scores_free(q, k)
            return sem_, count + 1

        def close_free(q, k):
            return ce_done, q * CJ + (k + 1)

        def close_read(q, k):
            return ce_done, q * CJ + (k + 2)

        def attend_free(q, k):
            return ae_done, q * AJ + (k + 1)

        def attend_read(q, k):
            return ae_done, q * AJ + (k + 2)

        def turned_bank(q, k):
            return p_y[0][0] if isinstance(q, int) and q >= NG - 2 and k % 2 else p_a


        block = top.enter_context(nc.Block())

        def all_groups(eng, norm, front, start, slot):
            for n in range(NS):
                norm(0, 0, n)
            for n in range(NS):
                front(0, 0, n)
                norm(1, 1, n)
            start()
            for g in range(2):
                for n in range(NS):
                    slot(g, g % 2, n)
            with eng.Fori(1, (NG - 2) // 2) as i:
                for k in range(2):
                    for n in range(NS):
                        slot(i * 2 + k, k, n)
            for g in range((NG - 2) // 2 * 2, NG + 2):
                for n in range(NS):
                    slot(g, g % 2, n)

        def all_tiles(eng, step):
            for i in range(3):
                step(i, i // 2, i % 2)
            with eng.Fori(2, TILES // 2) as m:
                step(m * 2 - 1, m - 1, 1)
                step(m * 2, m, 0)
            for i in range(TILES // 2 * 2 - 1, TILES):
                step(i, i // 2, i % 2)

        def has_next(i):
            return not isinstance(i, int) or i + 1 < TILES

        def expert_of(eng, i):
            return eng.value_load(tile_expert[0:1, bass.ds(i, 1)], min_val=0, max_val=NE - 1)

        def up_weights(e, half):
            return w_s[:, bass.ds(e * EW, KC * FH)].rearrange("p (c h n) -> p c h n", c=KC, h=2)[:, :, half, :]

        def down_weights(e, half, first, last):
            return w_s[:, bass.ds(e * EW + (KC * FH + (half * HC // 2 + first) * DM), (last - first) * DM)] \
                .rearrange("p (c n) -> p c n", n=DM)

        def is_on(g, by=0):
            return not isinstance(g, int) or 0 <= g + by < NG

        def ahead(g, p, n, by):
            return (g, p, n + by) if n + by < NS else (g + 1, 1 - p, n + by - NS)

        def has_state(g, n, by):
            return is_on(g, 1) or (is_on(g) and n + by < NS)

        @block.sync
        def _(sp):
            loads = [
                (w_in_s[:], w_in.rearrange("(c p) n -> p c n", p=P)),
                (norm_s[:], norm_w.rearrange("(c p) -> p c", p=P)),
                (convw_s[:], conv_w.rearrange("(c p) o k -> p c (o k)", p=P)),
                (convb_s[:], conv_b.rearrange("(c p) -> p c", p=P)),
                (wx_s[:], w_xproj.rearrange("(c p) n -> p c n", p=P)),
                (a_s[:], a_log.rearrange("(c p) n -> p c n", p=P)),
                (dpar_s[:], d_par.rearrange("(c p) -> p c", p=P)),
                (wo_s[:], w_out.rearrange("(c p) n -> p c n", p=P)),
                (rw1_s[:], rw1.rearrange("(c p) n -> p c n", p=P)),
                (rb1_s[:], rb1.rearrange("(c p) -> p c", p=P)),
                (rw2_s[:], rw2.rearrange("(c p) n -> p c n", p=P)),
                (rb2_s[:], rb2.rearrange("(o n) -> o n", o=1).broadcast_to([P, NE])),
                (mask_s[:], mask.rearrange("(o b) s -> o b s", o=1).broadcast_to([P, BATCH, SEQ])),
                (maskt_s[:], maskt),
            ]

            def load_front(f):
                need(sp, xn_done, f)
                sp.dma_start(xf[:], x_rows(x, f)).then_inc(xf_ready, 16)

            def keep_x2(q):
                sp.wait_ge(x2_done, q + 1)
                sp.dma_start(x2_all[:, bass.ds(q * GB, GB), :], x2[:]).then_inc(x2_kept, 16)

            def load_residual(q):
                if not (isinstance(q, int) and q == 0):
                    sp.wait_ge(*close_read(q - 1, C_OUT))
                sp.dma_start(xb[:], x_rows(x, q)).then_inc(xb_ready, 16)

            def load_values(q):
                need(sp, vaug_done, q)
                sp.dma_start(ctx_s[:], x_rows(ctxk, q)).then_inc(ctx_ready, 16)

            def load_keys(q):
                need(sp, smax_done, q * GB)
                for hh in range(HPC):
                    r = slice(HD * hh, HD * hh + HD)
                    sp.dma_start(kbd[r, :, :, hh % 4, :], ctxt[r, bass.ds(q * GB, GB)]).then_inc(kbd_ready, 16)

            def store_b(f):
                sp.wait_ge(*front_read(f, F_B))
                sp.dma_start(b_dram[bass.ds(f, 1)].rearrange("o n t -> (o n) t"), b_rows[:]).then_inc(b_stored, 16)

            def load_b(f, c):
                if c == 0:
                    sp.wait_ge(b_stored, (f + 1) * 16)
                else:
                    need(sp, u_done, f * NS + CHUNK * (c - 1))
                sp.dma_start(b_all[c % 2][:], b_dram[bass.ds(f, 1), CHUNK * c:CHUNK * (c + 1)]
                             .broadcast_to([P, CHUNK, GT])).then_inc(b_ready[c % 2], 16)

            load_front(0)
            with nc.allow_non_contiguous_dma(reason="small vectors, once"):
                for to, of in loads:
                    sp.dma_start(to, of).then_inc(w_loaded, 16)
            load_front(1)
            store_b(0)
            load_b(0, 0)
            load_b(0, 1)
            sp.wait_ge(consts, 1)
            load_residual(0)
            load_keys(0)
            rows = xs_dram.rearrange("(n p) d -> p n d", p=P)
            sp.dma_start(rows, zrow[:, :].unsqueeze(1).broadcast_to([P, TILES, DM])).then_inc(zero_rows, 16)

            def load_experts(first, last):
                for e in range(first, last):
                    w1 = w_s[:, e * EW:e * EW + KC * FH]
                    w2 = w_s[:, e * EW + KC * FH:(e + 1) * EW]
                    sp.dma_start(w1.rearrange("p (c n) -> p c n", c=KC),
                                 we1[e].rearrange("(c p) n -> p c n", p=P)).then_inc(w1_ready[e], 16)
                    sp.dma_start(w2.rearrange("p (c n) -> p c n", c=HC),
                                 we2[e].rearrange("(c p) n -> p c n", p=P)).then_inc(w2_ready[e], 16)

            def during(g):
                if is_on(g):
                    load_b(g, 2)
                if is_on(g, 2):
                    load_front(g + 2)
                if is_on(g, -1):
                    load_values(g - 1)
                if is_on(g):
                    load_b(g, 3)
                    if not (isinstance(g, int) and g == 0):
                        load_residual(g)
                if isinstance(g, int) and g == NG - 1:
                    sp.wait_ge(dt_done, NG)
                    sp.wait_ge(fj_done, FJ * NG)
                    load_experts(0, 2)
                if isinstance(g, int) and g == NG:
                    sp.wait_ge(acc_done, NG * NS * GB)
                    load_experts(2, 5)
                if isinstance(g, int) and g == NG + 1:
                    sp.wait_ge(smax_done, NG * GB)
                    load_experts(5, NE)
                if is_on(g, -2):
                    keep_x2(g - 2)
                if is_on(g, 1):
                    store_b(g + 1)
                    load_b(g + 1, 0)
                if is_on(g, 1):
                    load_b(g + 1, 1)
                if is_on(g) and not (isinstance(g, int) and g == 0):
                    load_keys(g)

            for g in range(2):
                during(g)
            with sp.Fori(2, (NG - 2) // 2 * 2) as g:
                during(g)
            for g in range((NG - 2) // 2 * 2, NG + 2):
                during(g)

            def load_x(i, m, k):
                need(sp, xt_turned, i - 1)
                sp.dma_start(xt[k][:], xs_dram[bass.ds(i * P, P), :]).then_inc(xt_ready[k], 16)

            def expert_of(i):
                return sp.value_load(tile_expert[0:1, bass.ds(i, 1)], min_val=0, max_val=NE - 1)

            def load_b1(i, m, k, e):
                need(sp, upb_done, (i - 1) * 2)
                sp.dma_start(b1_s[k][:], be1[bass.ds(e, 1), :].broadcast_to([P, FH])).then_inc(b1_ready[k], 16)

            def load_b2(i, m, k, e):
                need(sp, yo_done, i - 1)
                sp.dma_start(b2_s[k][:], be2[bass.ds(e, 1), :].broadcast_to([P, DM])).then_inc(b2_ready[k], 16)

            def store(i, m, k):
                sp.wait_ge(yo_done, i + 1)
                sp.dma_start(ys_dram[bass.ds(i * P, P), :], yo[k][:]).then_inc(ys_stored[k], 16)

            def step(j, m, k):
                static = isinstance(j, int)
                e = None
                if not static or j + 1 < TILES:
                    e = expert_of(j + 1)
                    load_b1(j + 1, m + k, 1 - k, e)
                if not static or j + 3 < TILES:
                    load_x(j + 3, m + 1 + k, 1 - k)
                if not static or j >= 1:
                    store(j - 1, m - 1 + k, 1 - k)
                if e is not None:
                    load_b2(j + 1, m + k, 1 - k, e)

            sp.wait_ge(scattered, 16 * TOPK * BATCH)
            load_x(0, 0, 0)
            load_x(1, 0, 1)
            e = expert_of(0)
            load_b1(0, 0, 0, e)
            load_b2(0, 0, 0, e)
            load_x(2, 1, 0)
            first, turns = 2, (TILES - 3 - 2) // 2
            for j in range(first):
                step(j, j // 2, j % 2)
            with sp.Fori(first // 2, first // 2 + turns) as m:
                for k in range(2):
                    step(m * 2 + k, m, k)
            for j in range(first + 2 * turns, TILES + 1):
                step(j, j // 2, j % 2)
            for b in range(BATCH):
                sp.wait_ge(fin_done, b + 1)
                sp.dma_start(out[b], res[:, b, :]).then_inc(stored, 16)
            sp.wait_ge(stored, 16 * BATCH)

        @block.tensor
        def _(pe):
            def job_of(f, k):
                pe.wait_ge(*front_free(f, k))

            def norm(f, p, n):
                if n == 15:
                    job_of(f, F_XNT)
                    pe.wait_ge(xn_done, f + 1)
                    for c in range(KC):
                        for b in range(GB):
                            t = pe.transpose(p_f[F_XNT % 2][:, (c * GB + b) * P:(c * GB + b + 1) * P],
                                             xn[:, b, c * P:(c + 1) * P], ident[:])
                    t.then_inc(fj_done, 1)

            def front(f, p, n):
                def job(k):
                    pe.wait_ge(*front_free(f, k))

                if n < 4:
                    k = n
                    job(F_IN + k)
                    pe.wait_ge(*front_read(f, F_XNT))
                    for jj in range(2):
                        col = (2 * k + jj) * P
                        for c in range(KC):
                            m = pe.matmul(p_f[(F_IN + k) % 2][:, jj * GT:(jj + 1) * GT], w_in_s[:, c, col:col + P],
                                          xnT[:, c, :, :].rearrange("p b s -> p (b s)"),
                                          start=c == 0, stop=c == KC - 1)
                    m.then_inc(fj_done, 1)
                if n in (6, 8):
                    k = (n - 6) // 2
                    job(F_DELTA[k])
                    pe.wait_ge(silu_done, f + 1)
                    for jj in range(2):
                        col = 2 * NS + (2 * k + jj) * P
                        for c in range(JC):
                            m = pe.matmul(p_f[F_DELTA[k] % 2][:, jj * GT:(jj + 1) * GT], wx_s[:, c, col:col + P],
                                          xs[p][:, c, :, :].rearrange("p b s -> p (b s)"),
                                          start=c == 0, stop=c == JC - 1)
                    m.then_inc(fj_done, 1)
                if n == 7:
                    job(F_B)
                    for c in range(JC):
                        m = pe.matmul(p_f[F_B % 2][0:NS, 0:GT], wx_s[:, c, 0:NS],
                                      xs[p][:, c, :, :].rearrange("p b s -> p (b s)"),
                                      start=c == 0, stop=c == JC - 1)
                    m.then_inc(fj_done, 1)
                if n == 10:
                    job(F_C)
                    for b in range(GB):
                        for c in range(JC):
                            m = pe.matmul(p_f[F_C % 2][:, b * NS:(b + 1) * NS], xs[p][:, c, b, :],
                                          wx_s[:, c, NS:2 * NS], start=c == 0, stop=c == JC - 1)
                    m.then_inc(fj_done, 1)

            def turn_h(g, p, n):
                k = g * NS + n
                pe.wait_ge(scan_done, k + 1)
                for b in range(GB):
                    need(pe, acc_done, (k - 2) * GB + b + 1)
                    for j in range(JC):
                        t = pe.transpose(p_y[n % 2][b][:, j * P:(j + 1) * P], h[n % LAG][:, j, b, :], ident[:])
                    t.then_inc(yt_done, 1)

            def turn_rows(to, rows):
                for c in range(KC):
                    for b in range(GB):
                        t = pe.transpose(to[:, (c * GB + b) * P:(c * GB + b + 1) * P],
                                         rows[:, b, c * P:(c + 1) * P], ident[:])
                return t

            def close(q, p, n, at):
                def job(k):
                    pe.wait_ge(*close_free(q, k))

                def sum_turned(k):
                    job(C_SUM + k)
                    pe.wait_ge(acc_done, (q + 1) * NS * GB)
                    for jj in range(2):
                        j = 2 * k + jj
                        for b in range(GB):
                            t = pe.transpose(p_c[:, (jj * GB + b) * P:(jj * GB + b + 1) * P],
                                             acc[p][:, b, j * P:(j + 1) * P], ident[:])
                    t.then_inc(cj_done, 1)

                def scores(b, k):
                    bank = p_f[1] if k % 2 else p_c
                    if k % 2:
                        pe.wait_ge(*scores_free(q, b * 2 + k // 2))
                    else:
                        job(C_SCORE[b] + k // 2)
                    pe.wait_ge(kbd_ready, (q + 1) * 16 * HPC)
                    pe.wait_ge(prepared, 1)
                    c, r = k // 2, slice((k % 2) * (P // 2), (k % 2 + 1) * (P // 2))
                    pe.matmul(bank[:], x1T[r, c, b, :], kbd[r, b, c].rearrange("p h s -> p (h s)"),
                              start=True, stop=True).then_inc(sj_done if k % 2 else cj_done, 1)

                if at == "late" and n == 0:
                    sum_turned(0)
                if at == "mid" and n == 1:
                    sum_turned(1)
                if at == "late" and n in (4, 5):
                    b = n - 4
                    if b == 0:
                        job(C_OUT)
                        pe.wait_ge(yg_done, q + 1)
                    for j in range(JC):
                        m = pe.matmul(p_c[:, b * DM:(b + 1) * DM], y[:, j, b, :], wo_s[:, j, :],
                                      start=j == 0, stop=j == JC - 1)
                    if b == GB - 1:
                        m.then_inc(cj_done, 1)
                if at == "mid" and n == 9:
                    job(C_X1T)
                    pe.wait_ge(x1_done, q + 1)
                    turn_rows(p_c, x1[p]).then_inc(cj_done, 1)
                if 11 <= n < 15 and at == "mid":
                    scores((n - 11) // 2, (n - 11) % 2 * 2)
                    scores((n - 11) // 2, (n - 11) % 2 * 2 + 1)

            def attention(q, p, n, at):
                def job(k):
                    pe.wait_ge(*attend_free(q, k))

                def weights_turned(b, k):
                    apart = isinstance(q, int) and q >= NG - 2 and k > 0
                    pe.wait_ge(*attend_free(q, A_TURN[b] + k - apart))
                    pe.wait_ge(exp_done, GB * q + b + 1)
                    for hh in range(4):
                        t = pe.transpose(turned_bank(q, k)[:, hh * P:(hh + 1) * P], s_s[b][:, 4 * k + hh, :], ident[:])
                    t.then_inc(aj_done, 1)

                for b in range(GB):
                    if n - 4 * b in (1, 2):
                        weights_turned(b, (n - 4 * b - 1) * 2 + (at == "late"))
                    if at == "mid" and n == 3 + 4 * b:
                        job(A_ATT[b])
                        pe.wait_ge(vaug_done, q + 1)
                        for hh in range(HEADS):
                            c, r = hh // 4, slice((hh % 4) * Q, (hh % 4 + 1) * Q)
                            m = pe.matmul(p_a[r, c * SEQ:(c + 1) * SEQ], vaug[:, b, hh * VW:hh * VW + Q], pT[:, hh, :],
                                          start=True, stop=True)
                        m.then_inc(aj_done, 1)
                    if at == "mid" and n == 4 + 4 * b:
                        job(A_ATTT[b])
                        for c in range(HEADS // 4):
                            t = pe.transpose(p_a[:, c * P:(c + 1) * P], oT[:, c * P:(c + 1) * P], ident[:])
                        t.then_inc(aj_done, 1)
                if at == "mid" and n == 11:
                    job(A_X2T)
                    pe.wait_ge(x2_done, q + 1)
                    turn_rows(p_a, x2).then_inc(aj_done, 1)
                if at == "mid" and n == 12:
                    job(A_RH)
                    for m_ in range(KC):
                        for c in range(KC):
                            m = pe.matmul(p_a[:, m_ * GT:(m_ + 1) * GT], rw1_s[:, c, m_ * P:(m_ + 1) * P],
                                          x2T[:, c, :, :].rearrange("p b s -> p (b s)"),
                                          start=c == 0, stop=c == KC - 1)
                    m.then_inc(aj_done, 1)
                if at == "mid" and n == 14:
                    job(A_LOGIT)
                    for b in range(GB):
                        for c in range(KC):
                            m = pe.matmul(p_a[:, b * NE:(b + 1) * NE], rh[:, c, b, :], rw2_s[:, c, :],
                                          start=c == 0, stop=c == KC - 1)
                    m.then_inc(aj_done, 1)

            def slot(g, p, n):
                if is_on(g):
                    turn_h(g, p, n)
                for at in ("mid", "late"):
                    if is_on(g, -1):
                        close(g - 1, 1 - p, n, at)
                    if is_on(g, -2):
                        attention(g - 2, p, n, at)
                    if at == "mid" and is_on(g, 1):
                        front(g + 1, 1 - p, n)
                if is_on(g, 2):
                    norm(g + 2, p, n)

            pe.wait_ge(prepared, 1)
            all_groups(pe, norm, front, lambda: None, slot)

            pe.wait_ge(route_c, 4)
            pe.wait_ge(route, R_PICKS)
            flat = picks[:].rearrange("p b e -> p (b e)")
            pe.matmul(p_h[0][:, 0:BATCH * NE], lower[:], flat, start=True, stop=True)
            pe.matmul(p_h[1][:, 0:BATCH * NE], ones_sq[:], flat, start=True, stop=True).then_inc(ranks, 1)

            def turn_x(m, k):
                i = m * 2 + k
                pe.wait_ge(xt_ready[k], (m + 1) * 16)
                need(pe, xl_done, i - 1)
                for c in range(KC):
                    t = pe.transpose(p_x[k][:, c * P:(c + 1) * P], xt[k][:, c * P:(c + 1) * P], ident[:])
                t.then_inc(xt_turned, 1)

            def up(i, k):
                pe.wait_ge(xl_done, i + 1)
                for half in range(2):
                    need(pe, upb_done, (i - 1) * 2 + half + 1)
                    pe.wait_ge(upl_done, i * 2 + half + 1)
                    for a, w, first, last in ((xh, upl, True, False), (xl, uph, False, False), (xh, uph, False, True)):
                        for c in range(KC):
                            m = pe.matmul(p_h[half][:], a[k][:, c, :], w[half][:, c, :],
                                          start=first and c == 0, stop=last and c == KC - 1)
                    m.then_inc(up_done, 1)

            def turn_hs(i, k):
                pe.wait_ge(hs_done, i * 2 + 2)
                for half in range(2):
                    need(pe, hl_done, (i - 1) * 2 + half + 1)
                    for c in range(4):
                        col = (half * 4 + c) * P
                        t = pe.transpose(p_hT[half][:, c * P:(c + 1) * P], hs[:, col:col + P], ident[:])
                    t.then_inc(ht_turned, 1)

            def down(i, k):
                need(pe, yo_done, i - 1)
                for half in range(2):
                    pe.wait_ge(hl_done, i * 2 + (half + 1))
                    if half == 0:
                        pe.wait_ge(dnl_done, i + 1)
                    pe.wait_ge(dnl_more, i * 2 + (half + 1))
                    parts = ((hh, dnl), (hl, dnh), (hh, dnh))
                    for c in range(HC // 2):
                        for a, w in parts:
                            m = pe.matmul(p_o[k][:, 0:DM], a[:, half * 4 + c, :], w[half][:, c, :],
                                          start=half == 0 and c == 0 and a is hh and w is dnl,
                                          stop=half == 1 and c == HC // 2 - 1 and a is hh and w is dnh)
                    m.then_inc(down_done, 1)

            def tile(m, k, first=False, last=False):
                i = m * 2 + k
                if not last:
                    turn_x(m + k, 1 - k)
                if not first:
                    turn_hs(i - 1, 1 - k)
                up(i, k)
                if not first:
                    down(i - 1, 1 - k)

            turn_x(0, 0)
            tile(0, 0, first=True)
            tile(0, 1)
            with pe.Fori(1, TILES // 2) as m:
                tile(m, 0)
                tile(m, 1)
            tile(TILES // 2, 0, last=True)
            turn_hs(TILES - 1, 0)
            down(TILES - 1, 0)

        @block.scalar
        def _(act):
            def norm(f, p, n):
                if n == 12:
                    act.wait_ge(xf_ready, (f + 1) * 16)
                    need(act, rms_step, 3 * f)
                    for b in range(GB):
                        s = act.activation(sq_junk[:], xf[:, b, :], ACT.Square, scale=DM ** -0.5,
                                           accum_out=ssq[:, b:b + 1])
                        s.then_inc(ssq_done, 1)
                        act.wait_ge(ssq_done, GB * f + b + 1)
                if n == 14:
                    act.wait_ge(rms_step, f * 3 + 3)
                    for b in range(GB):
                        s = act.activation(xn[:, b, :], xf[:, b, :], ACT.Copy, scale=rrms[:, b:b + 1])
                    s.then_inc(xn_done, 1)

            def front(f, p, n):
                fj = f * FJ

                def read_out(k, to, split=None):
                    of = p_f[k % 2][:] if split is None else p_f[k % 2][:].rearrange("p (a s) -> p a s", s=split)
                    act.wait_ge(fj_done, fj + (k + 1))
                    act.activation(to, of, ACT.Copy).then_inc(fe_done[k % 2], 1)

                if n == 0:
                    read_out(F_XNT, xnT[:].rearrange("p c b s -> p (c b s)"))
                if 1 <= n < 3:
                    k = n - 1
                    read_out(F_IN + k, xpad[:, 2 * k:2 * k + 2, :, TAPS - 1:].rearrange("p j b s -> p (j b) s"), SEQ)
                if n == 2:
                    for i in range(2):
                        act.wait_ge(*front_read(f, F_IN + i))
                    for j in range(JC):
                        s = act.activation(xc[:, j], xpad[:, j, :, 0:SEQ], ACT.Identity,
                                           scale=convw_s[:, j, 0:1], bias=convb_s[:, j:j + 1])
                    s.then_inc(conv_step, 1)
                if 3 <= n < 5:
                    k = n - 3
                    if k == 0:
                        need(act, yg_done, f - 1)
                    read_out(F_IN + 2 + k, sz[p][:, 2 * k:2 * k + 2].rearrange("p j b s -> p (j b s)"))
                if n == 5:
                    act.wait_ge(conv_step, (f + 1) * TAPS)
                    for k in (2, 3):
                        act.wait_ge(*front_read(f, F_IN + k))
                    act.activation(xs[p][:], xc[:], ACT.Silu).then_inc(silu_done, 1)
                if n == 6:
                    act.activation(sz[p][:], sz[p][:], ACT.Silu)
                    act.preload_act_table_set("natural_log_exp_and_others")
                if n == 9:
                    act.wait_ge(fj_done, fj + F_B + 1)
                    need(act, b_stored, f * 16)
                    need(act, u_done, f * NS - CHUNK)
                    act.activation(b_rows[:], p_f[F_B % 2][0:NS, 0:GT], ACT.Copy).then_inc(fe_done[F_B % 2], 1)
                if n in (7, 9):
                    k = (n - 7) // 2
                    job, to = F_DELTA[k], slice(2 * k, 2 * k + 2)
                    act.wait_ge(fj_done, fj + (job + 1))
                    act.activation(dabs[:, to].rearrange("p j b s -> p (j b s)"), p_f[job % 2][:],
                                   ACT.Abs).then_inc(sp_step, 1)
                    act.activation(dpos[:, to].rearrange("p j b s -> p (j b s)"), p_f[job % 2][:],
                                   ACT.Relu).then_inc(fe_done[job % 2], 1)
                if n == 9:
                    act.wait_ge(sp_step, f * 4 + 2)
                    act.activation(dabs[:], dabs[:], ACT.Exp, scale=-1.0).then_inc(sp_step, 1)
                    act.wait_ge(sp_step, f * 4 + 3)
                    act.activation(dabs[:], dabs[:], ACT.Ln, bias=ones_col[:]).then_inc(sp_step, 1)

            def decay(g, p, n):
                k = g * NS + n
                act.wait_ge(dt_done, g + 1)
                need(act, scan_done, k - 1)
                for j in range(JC):
                    a = act.activation(da[n % LAG][:, j, :, 1:], dt[p][:, j, :, 1:], ACT.Exp,
                                       scale=a_s[:, j, n:n + 1])
                a.then_inc(da_done, 1)

            def close(q, p, n, at):
                if at == "early" and n == 10:
                    act.wait_ge(cj_done, q * CJ + (C_X1T + 1))
                    act.activation(x1T[:].rearrange("p c b s -> p (c b s)"), p_c[:], ACT.Copy).then_inc(ce_done, 1)

            def attention(q, p, n, at):
                def read_out(k, to):
                    act.wait_ge(aj_done, q * AJ + (k + 1))
                    act.activation(to, p_a[:], ACT.Copy).then_inc(ae_done, 1)

                def turned(b, k):
                    act.wait_ge(aj_done, q * AJ + (A_TURN[b] + k + 1))
                    act.activation(pT[:, 4 * k:4 * k + 4, :].rearrange("p h s -> p (h s)"), turned_bank(q, k)[:],
                                   ACT.Copy).then_inc(ae_done, 1)

                for b in range(GB):
                    if at == "mid" and n == 4 * b:
                        act.wait_ge(ssub_done, GB * q + b + 1)
                        act.activation(s_s[b][:], s_s[b][:], ACT.Exp).then_inc(exp_done, 1)
                    m = n - 4 * b
                    if at == "early" and m in (2, 3):
                        turned(b, 2 * (m - 2) + 1)
                    if at == "mid" and m in (1, 2):
                        turned(b, 2 * (m - 1))
                    if at == "early" and m == 4:
                        read_out(A_ATT[b], oT[:])
                if at == "early" and n == 12:
                    read_out(A_X2T, x2T[:].rearrange("p c b s -> p (c b s)"))
                if at == "early" and n == 13:
                    act.wait_ge(aj_done, q * AJ + (A_RH + 1))
                    for m in range(KC):
                        a = act.activation(rh[:, m].rearrange("p b s -> p (b s)"), p_a[:, m * GT:(m + 1) * GT],
                                           ACT.Silu, bias=rb1_s[:, m:m + 1])
                    a.then_inc(ae_done, 1)
                    act.preload_act_table_set("natural_log_exp_and_others")

            def start():
                decay(0, 0, 0)
                decay(0, 0, 1)

            def slot(g, p, n):
                if has_state(g, n, 2):
                    decay(*ahead(g, p, n, 2))
                for at in ("early", "mid"):
                    if is_on(g, -1):
                        close(g - 1, 1 - p, n, at)
                    if is_on(g, -2):
                        attention(g - 2, p, n, at)
                    if at == "early" and is_on(g, 1):
                        front(g + 1, 1 - p, n)
                    if at == "mid" and is_on(g, 2):
                        norm(g + 2, p, n)

            act.wait_ge(w_loaded, 16 * 14)
            act.activation(a_s[:], a_s[:], ACT.Exp).then_inc(a_ready, 1)
            act.wait_ge(prepared, 1)
            all_groups(act, norm, front, start, slot)

            act.wait_ge(route, R_DLT)
            act.activation(e2[:], dlt[:], ACT.Exp).then_inc(gate_exp, 1)

            act.wait_ge(scattered, 16 * TOPK * BATCH)
            act.activation(x2_all[:].rearrange("p b d -> p (b d)"), x2_all[:].rearrange("p b d -> p (b d)"),
                           ACT.Copy, scale=2.0).then_inc(doubled, 1)

            for e in range(NE):
                act.wait_ge(w1_ready[e], 16)
                act.wait_ge(w2_ready[e], 16)

            def round_x(i, k):
                act.wait_ge(xt_turned, i + 1)
                need(act, up_done, (i - 1) * 2)
                act.activation(xh[k][:].rearrange("p c s -> p (c s)"), p_x[k][:, 0:KC * P],
                               ACT.Copy).then_inc(xh_done, 1)

            def round_up(i, e, half):
                need(act, up_done, (i - 1) * 2 + half + 1)
                act.activation(uph[half][:], up_weights(e, half), ACT.Copy).then_inc(uph_done, 1)

            def round_down(i, e, half):
                need(act, down_done, (i - 1) * 2 + half + 1)
                act.activation(dnh[half][:], down_weights(e, half, 0, HC // 2), ACT.Copy).then_inc(dnh_done, 1)

            def round_h(i, half):
                act.wait_ge(ht_turned, i * 2 + half + 1)
                need(act, down_done, (i - 1) * 2 + half + 1)
                act.activation(hh[:, half * 4:half * 4 + 4, :].rearrange("p c s -> p (c s)"), p_hT[half][:],
                               ACT.Copy).then_inc(hh_done, 1)

            def step(i, m, k):
                if has_next(i):
                    e = expert_of(act, i + 1)
                    round_up(i + 1, e, 0)
                    round_x(i + 1, 1 - k)
                for half in range(2):
                    to = hs[:, half * 512:(half + 1) * 512]
                    act.wait_ge(upb_done, i * 2 + (half + 1))
                    act.activation(to, to, ACT.Silu).then_inc(hs_done, 1)
                if has_next(i):
                    round_up(i + 1, e, 1)
                e = expert_of(act, i)
                round_down(i, e, 0)
                round_h(i, 0)
                round_down(i, e, 1)
                round_h(i, 1)

            round_x(0, 0)
            e = expert_of(act, 0)
            round_up(0, e, 0)
            round_up(0, e, 1)
            all_tiles(act, step)

        @block.gpsimd
        def _(pool):
            pool.memset(ident[:], 0.0).then_inc(route_c, 1)
            pool.wait_ge(route_c, 1)
            pool.affine_select(out=ident[:], in_=ident[:], compare_op=ALU.not_equal, fill=1.0, base=0,
                               pattern=[[-1, P]], channel_multiplier=1)
            pool.memset(eps_pow[:], -0.5).then_inc(fe_done[0], 1)
            pool.memset(rms_eps[:], RMS_EPS).then_inc(fe_done[1], 1)
            pool.memset(ones_col[:], 1.0).then_inc(ce_done, 1)
            pool.memset(causal[:], NEG).then_inc(route_c, 1)
            pool.wait_ge(route_c, 2)
            pool.affine_select(out=causal[:], in_=causal[:], compare_op=ALU.is_ge, fill=0.0, base=0,
                               pattern=[[-1, SEQ]], channel_multiplier=1)
            pool.memset(zrow[:], 0.0).then_inc(ae_done, 1)
            pool.memset(vaug[:], 1.0).then_inc(x2_kept, 1)
            pool.memset(xpad[:, :, :, 0:TAPS - 1], 0.0)
            for k in range(LAG):
                pool.memset(da[k][:, :, :, 0:1], 0.0)
            pool.memset(kbd[:], 0.0).then_inc(consts, 1)

            def norm(f, p, n):
                if n == 13:
                    pool.wait_ge(ssq_done, (f + 1) * GB)
                    pool.tensor_tensor(msq[:], ssq[:], rms_eps[:], ALU.add).then_inc(rms_step, 1)
                    pool.wait_ge(rms_step, f * 3 + 1)
                    need(pool, xn_done, f)
                    pool.tensor_tensor(rrms[:], msq[:], eps_pow[:, 0:GB], ALU.pow).then_inc(rms_step, 2)

            def input_of(g, p, n):
                k = g * NS + n
                if n == 0:
                    pool.wait_ge(dtx_done, g + 1)
                if n % CHUNK == 0:
                    pool.wait_ge(b_ready[n // CHUNK % 2], g * 32 + (n // CHUNK // 2 + 1) * 16)
                need(pool, scan_done, k - 1)
                pool.tensor_tensor(u[n % LAG][:], dtx[p][:],
                                   b_all[n // CHUNK % 2][:, n % CHUNK].unsqueeze(1).broadcast_to([P, JC, GB, SEQ]),
                                   ALU.mult).then_inc(u_done, 1)

            def less_max(q, b):
                pool.wait_ge(smax_done, GB * q + b + 1)
                pool.tensor_tensor(s_s[b][:], s_s[b][:], smax[b][:].unsqueeze(2).broadcast_to([P, HEADS, SEQ]),
                                   ALU.subtract).then_inc(ssub_done, 1)

            def close(q, p, n):
                if n == 2:
                    pool.wait_ge(*close_read(q, C_SUM + 1))
                    pool.wait_ge(*front_read(q, F_DELTA[0]))
                    pool.tensor_tensor(y[:], y[:], sz[p][:], ALU.mult).then_inc(yg_done, 1)
                if n == 7:
                    pool.wait_ge(var_done, q + 1)
                    pool.tensor_tensor(rstd[:], var[:], eps_pow[:, 0:GB], ALU.pow).then_inc(rstd_done, 1)
                if n == 14:
                    less_max(q, 0)
                if n == 11:
                    pool.wait_ge(ctx_ready, (q + 1) * 16)
                    if not (isinstance(q, int) and q == 0):
                        pool.wait_ge(*attend_read(q - 1, A_ATT[GB - 1]))
                    pool.tensor_tensor(vaug[:, :, 0:HEADS * VW].rearrange("p b (h w) -> p b h w", w=VW)[:, :, :, 0:HD],
                                       ctx_s[:].rearrange("p b (h d) -> p b h d", d=HD),
                                       ones_col[:].unsqueeze(2).unsqueeze(3).broadcast_to([P, GB, HEADS, HD]),
                                       ALU.mult).then_inc(vaug_done, 1)
            def attention(q, p, n):
                if n == 0:
                    less_max(q, 1)
                if n == 9:
                    pool.wait_ge(var2_done, q + 1)
                    pool.tensor_tensor(rstd2[:], var2[:], eps_pow[:, 0:GB], ALU.pow).then_inc(rstd2_done, 1)

            def start():
                input_of(0, 0, 0)
                input_of(0, 0, 1)

            def slot(g, p, n):
                if has_state(g, n, 2):
                    input_of(*ahead(g, p, n, 2))
                if is_on(g, -1):
                    close(g - 1, 1 - p, n)
                if is_on(g, -2):
                    attention(g - 2, p, n)
                if is_on(g, 2):
                    norm(g + 2, p, n)

            pool.wait_ge(prepared, 1)
            all_groups(pool, norm, lambda *a: None, start, slot)

            pool.wait_ge(*attend_read(NG - 1, AJ - 1))
            pool.iota(iota_e[:], pattern=[[1, NE]], base=0, channel_multiplier=0, allow_small_or_imprecise_dtypes=True)
            pool.iota(iota_i[:], pattern=[[1, TILES]], base=0, channel_multiplier=0,
                      allow_small_or_imprecise_dtypes=True)
            pool.memset(ones_sq[:], 1.0)
            pool.memset(keep_on[:], 1.0).then_inc(route_c, 1)
            pool.wait_ge(route_c, 3)
            pool.memset(keep_on[:, :, 0:1], 0.0)
            pool.affine_select(out=lower[:], in_=ones_sq[:], compare_op=ALU.is_ge, fill=0.0, base=-1,
                               pattern=[[1, P]], channel_multiplier=-1).then_inc(route_c, 1)

            pool.wait_ge(zero_rows, 16)
            pool.wait_ge(route, N_ROUTE)
            for b in range(BATCH):
                for k in range(TOPK):
                    pool.indirect_dma_start(
                        out=xs_dram[:, :], out_offset=bass.IndirectOffsetOnAxis(ap=slots_i[:, k, b:b + 1], axis=0),
                        in_=x2_all[:, b, :], in_offset=None).then_inc(scattered, 16)

            def step(i, m, k):
                e = expert_of(pool, i)
                pool.wait_ge(dnh_done, i * 2 + 1)
                pool.tensor_tensor(dnl[0][:, DS:], down_weights(e, 0, DS, HC // 2), dnh[0][:, DS:],
                                   ALU.subtract).then_inc(dnl_more, 1)
                pool.wait_ge(dnh_done, i * 2 + 2)
                pool.tensor_tensor(dnl[1][:], down_weights(e, 1, 0, HC // 2), dnh[1][:],
                                   ALU.subtract).then_inc(dnl_more, 1)

            all_tiles(pool, step)

            def root(i):
                rows = slice(i * FB, (i + 1) * FB)
                pool.wait_ge(fin_var, i + 1)
                pool.tensor_tensor(rstd3[:, rows], var3[:, rows], eps_pow[:, rows], ALU.pow).then_inc(fin_rstd, 1)

            for k in range(2):
                pool.wait_ge(ys_stored[k], 16 * ((TILES + 1 - k) // 2))
            for b in range(BATCH):
                for k in range(TOPK):
                    pool.indirect_dma_start(
                        out=yg[k][:, b, :], out_offset=None, in_=ys_dram[:, :],
                        in_offset=bass.IndirectOffsetOnAxis(ap=slots_i[:, k, b:b + 1], axis=0)).then_inc(gathered[b], 16)
                if b > FB and b % FB == 0:
                    root(b // FB - 2)
            for i in range(BATCH // FB - 2, BATCH // FB):
                root(i)

        @block.vector
        def _(dve):
            def front(f, p, n):
                fj = f * FJ
                if n in (3, 4):
                    for k in ((1,), (2, 3))[n - 3]:
                        dve.wait_ge(conv_step, f * TAPS + k)
                        for j in range(JC):
                            s = dve.scalar_tensor_tensor(out=xc[:, j], in0=xpad[:, j, :, k:k + SEQ],
                                                         scalar=convw_s[:, j, k:k + 1], in1=xc[:, j],
                                                         op0=ALU.mult, op1=ALU.add)
                        s.then_inc(conv_step, 1)
                if n == 11:
                    dve.wait_ge(fj_done, fj + F_C + 1)
                    dve.tensor_copy(cc[p][:].rearrange("p b n -> p (b n)"),
                                    p_f[F_C % 2][:, 0:GB * NS]).then_inc(fe_done[F_C % 2], 1)
                if n == 10:
                    dve.wait_ge(sp_step, f * 4 + 4)
                    dve.tensor_tensor(dt[p][:], dpos[:], dabs[:], ALU.add).then_inc(dt_done, 1)
                    dve.wait_ge(dt_done, f + 1)
                    dve.tensor_tensor(dtx[p][:], dt[p][:], xs[p][:], ALU.mult).then_inc(dtx_done, 1)

            def scan(g, p, n):
                k = g * NS + n
                dve.wait_ge(da_done, k + 1)
                dve.wait_ge(u_done, k + 1)
                need(dve, yt_done, (k - 1) * GB)
                dve.tensor_tensor_scan(out=h[n % LAG][:].rearrange("p j b s -> p (j b s)"),
                                       data0=da[n % LAG][:].rearrange("p j b s -> p (j b s)"),
                                       data1=u[n % LAG][:].rearrange("p j b s -> p (j b s)"),
                                       initial=0.0, op0=ALU.mult, op1=ALU.add).then_inc(scan_done, 1)

            def sum_states(g, p, n):
                k = g * NS + n
                for b in range(GB):
                    dve.wait_ge(yt_done, k * GB + (b + 1))
                    c = cc[p][:, b, n:n + 1]
                    if n == 0:
                        dve.tensor_scalar(acc[p][:, b, :], p_y[n % 2][b][:], c, None, ALU.mult).then_inc(acc_done, 1)
                    else:
                        dve.wait_ge(acc_done, (k - 1) * GB + (b + 1))
                        dve.scalar_tensor_tensor(out=acc[p][:, b, :], in0=p_y[n % 2][b][:], scalar=c, in1=acc[p][:, b, :],
                                                 op0=ALU.mult, op1=ALU.add).then_inc(acc_done, 1)

            def norm_stats(src, st, m, vr, ln_step, done, var_done):
                for b in range(GB):
                    s = dve.bn_stats(st[:, b, :], src[:, b, :])
                s.then_inc(ln_step, 1)
                dve.wait_ge(ln_step, done + 1)
                dve.tensor_copy(counts[:], st[:, :, 0:1].rearrange("p b o -> p (b o)"))
                for b in range(GB):
                    s = dve.bn_aggr(m[:, b, :], st[:, b, :])
                s.then_inc(ln_step, 1)
                dve.wait_ge(ln_step, done + 2)
                dve.tensor_scalar(vr[:], m[:, :, 1:2].rearrange("p b o -> p (b o)"), LN_EPS, None,
                                  ALU.add).then_inc(var_done, 1)

            def norm_apply(to, src, m, rs):
                for b in range(GB):
                    s = dve.tensor_scalar(to[:, b, :], src[:, b, :], m[:, b, 0:1], rs[:, b:b + 1],
                                          ALU.subtract, ALU.mult)
                return s

            def close(q, p, n, at):
                def sum_read(k):
                    dve.wait_ge(cj_done, q * CJ + (C_SUM + k + 1))
                    for jj in range(2):
                        j = 2 * k + jj
                        s = dve.scalar_tensor_tensor(out=y[:, j].rearrange("p b s -> p (b s)"),
                                                     in0=xs[p][:, j].rearrange("p b s -> p (b s)"),
                                                     scalar=dpar_s[:, j:j + 1], in1=p_c[:, jj * GT:(jj + 1) * GT],
                                                     op0=ALU.mult, op1=ALU.add)
                    s.then_inc(ce_done, 1)

                def scores(b, k):
                    if k % 2:
                        dve.wait_ge(sj_done, q * SJ + (b * 2 + k // 2 + 1))
                    else:
                        dve.wait_ge(cj_done, q * CJ + (C_SCORE[b] + k // 2 + 1))
                    bias = neg_bias[:, bass.ds(q * GB + b, 1), :].broadcast_to([P, 4, SEQ])
                    dve.scalar_tensor_tensor(out=s_s[b][:, 4 * k:4 * k + 4, :],
                                             in0=(p_f[1] if k % 2 else p_c)[:].rearrange("p (h s) -> p h s", s=SEQ),
                                             scalar=1.0 / HD ** 0.5, in1=bias, op0=ALU.mult,
                                             op1=ALU.subtract).then_inc(fe_done[1] if k % 2 else ce_done, 1)

                def greatest(b):
                    dve.wait_ge(*close_read(q, C_SCORE[b] + 1))
                    dve.wait_ge(*scores_read(q, b * 2 + 1))
                    dve.tensor_reduce(smax[b][:], s_s[b][:], X, ALU.max).then_inc(smax_done, 1)

                if at == "early" and n in (1, 2):
                    sum_read(n - 1)
                if at == "mid" and n == 6:
                    dve.wait_ge(cj_done, q * CJ + (C_OUT + 1))
                    dve.wait_ge(xb_ready, (q + 1) * 16)
                    dve.scalar_tensor_tensor(out=v[:].rearrange("p b d -> p (b d)"),
                                             in0=xb[:].rearrange("p b d -> p (b d)"), scalar=2.0, in1=p_c[:],
                                             op0=ALU.mult, op1=ALU.add).then_inc(ce_done, 1)
                    dve.wait_ge(*close_read(q, C_OUT))
                    norm_stats(v, stats, mv, var, ln_step, q * 2, var_done)
                if at == "early" and n == 8:
                    dve.wait_ge(rstd_done, q + 1)
                    norm_apply(x1[p], v, mv, rstd).then_inc(x1_done, 1)
                if at == "mid" and 11 <= n < 15:
                    scores((n - 11) // 2, (n - 11) % 2 * 2)
                if at == "early" and 12 <= n < 16:
                    scores((n - 12) // 2, (n - 12) % 2 * 2 + 1)
                if at == "mid" and n in (13, 15):
                    greatest((n - 13) // 2)

            def attention(q, p, n, at):
                def attended(b):
                    dve.wait_ge(aj_done, q * AJ + (A_ATTT[b] + 1))
                    heads = p_a[:].rearrange("p (h w) -> p h w", w=Q)
                    a0 = (q * GB + b) * 3
                    dve.reciprocal(rsum[:], heads[:, :, HD:HD + 1].rearrange("p h o -> p (h o)")).then_inc(att_step, 1)
                    dve.wait_ge(att_step, a0 + 1)
                    dve.tensor_scalar(rsum[:], rsum[:], qmask[:, bass.ds(q * GB + b, 1)], None,
                                      ALU.mult).then_inc(att_step, 1)
                    dve.wait_ge(att_step, a0 + 2)
                    dve.tensor_tensor(v2[:, b, :].rearrange("p (h d) -> p h d", d=HD), heads[:, :, 0:HD],
                                      rsum[:].unsqueeze(2).broadcast_to([P, HEADS, HD]), ALU.mult).then_inc(ae_done, 1)
                    dve.wait_ge(*attend_read(q, A_ATTT[b]))
                    dve.tensor_tensor(v2[:, b, :], v2[:, b, :], x1[p][:, b, :], ALU.add).then_inc(att_step, 1)

                if at == "early" and n in (5, 9):
                    attended((n - 5) // 4)
                if at == "early" and n == 9:
                    dve.wait_ge(att_step, (q + 1) * 3 * GB)
                    norm_stats(v2, stats2, mv2, var2, ln2_step, q * 2, var2_done)
                if at == "early" and n == 10:
                    dve.wait_ge(rstd2_done, q + 1)
                    dve.wait_ge(x2_kept, q * 16 + 1)
                    norm_apply(x2, v2, mv2, rstd2).then_inc(x2_done, 1)
                if at == "early" and n == 15:
                    dve.wait_ge(aj_done, q * AJ + (A_LOGIT + 1))
                    dve.tensor_tensor(logits[:, bass.ds(q * GB, GB), :],
                                      p_a[:, 0:GB * NE].rearrange("p (b e) -> p b e", e=NE),
                                      rb2_s[:].unsqueeze(1).broadcast_to([P, GB, NE]), ALU.add).then_inc(ae_done, 1)

            def slot(g, p, n):
                if has_state(g, n, 1):
                    scan(*ahead(g, p, n, 1))
                for at in ("early", "mid"):
                    if is_on(g, -1):
                        close(g - 1, 1 - p, n, at)
                    if is_on(g, -2):
                        attention(g - 2, p, n, at)
                    if at == "early":
                        if n and is_on(g):
                            sum_states(g, p, n - 1)
                        if n == 0 and is_on(g, -1):
                            sum_states(g - 1, 1 - p, NS - 1)
                if is_on(g, 1):
                    front(g + 1, 1 - p, n)

            dve.wait_ge(w_loaded, 16 * 14)
            for c in range(KC):
                dve.tensor_scalar(w_in_s[:, c, :], w_in_s[:, c, :], norm_s[:, c:c + 1], None, ALU.mult)
            dve.wait_ge(a_ready, 1)
            dve.tensor_scalar(a_s[:], a_s[:], -1.0, None, ALU.mult)
            dve.tensor_copy(qmask[:], maskt_s[:])
            dve.wait_ge(consts, 1)
            dve.tensor_tensor(neg_bias[:], mask_s[:], causal[:].unsqueeze(1).broadcast_to([P, BATCH, SEQ]),
                              ALU.mult).then_inc(prepared, 1)
            all_groups(dve, lambda *a: None, front, lambda: scan(0, 0, 0), slot)

            steps = [0]

            def step(ins):
                ins.then_inc(route, 1)
                steps[0] += 1
                dve.wait_ge(route, steps[0])

            dve.wait_ge(*attend_read(NG - 1, AJ - 1))
            dve.wait_ge(x2_kept, 16 * NG + 1)
            for b in range(BATCH):
                s = dve.max(m8[:, b, :], logits[:, b, :])
            step(s)
            for b in range(BATCH):
                s = dve.max_index(mi[:, b, :], m8[:, b, :], logits[:, b, :])
            step(s)
            step(dve.tensor_tensor(dlt[:], m8[:, :, 1], m8[:, :, 0], ALU.subtract))
            assert steps[0] == R_DLT
            step(dve.tensor_copy(mif[:], mi[:, :, 0:TOPK]))
            dve.wait_ge(route_c, 4)
            for k in range(TOPK):
                s = dve.tensor_tensor(pick[k][:], mif[:, :, k:k + 1].broadcast_to([P, BATCH, NE]),
                                      iota_e[:].unsqueeze(1).broadcast_to([P, BATCH, NE]), ALU.is_equal)
            step(s)
            step(dve.tensor_tensor(picks[:], pick[0][:], pick[1][:], ALU.add))
            assert steps[0] == R_PICKS
            dve.wait_ge(ranks, 1)
            step(dve.tensor_copy(tot[:], p_h[1][:, 0:BATCH * NE].rearrange("p (b e) -> p e b", e=NE)))
            step(dve.tensor_tensor_scan(out=incl[:].rearrange("p e b -> p (e b)"),
                                        data0=keep_on[:].rearrange("p e b -> p (e b)"),
                                        data1=tot[:].rearrange("p e b -> p (e b)"), initial=0.0,
                                        op0=ALU.mult, op1=ALU.add))
            step(dve.tensor_scalar(cnt_f[:], incl[:, :, BATCH - 1], float(P - 1), None, ALU.add))
            step(dve.tensor_copy(cnt_i[:], cnt_f[:]))
            step(dve.tensor_single_scalar(nt_i[:], cnt_i[:], 7, ALU.arith_shift_right))
            step(dve.tensor_copy(nt_f[:], nt_i[:]))
            step(dve.tensor_tensor_scan(out=cum[:], data0=ones_sq[:, 0:NE], data1=nt_f[:], initial=0.0,
                                        op0=ALU.mult, op1=ALU.add))
            step(dve.tensor_tensor(base[:], cum[:], nt_f[:], ALU.subtract))
            step(dve.tensor_scalar(base[:], base[:], float(P), None, ALU.mult))
            step(dve.tensor_tensor(incl[:], incl[:], tot[:], ALU.subtract))
            step(dve.tensor_tensor(incl[:], incl[:], base[:].unsqueeze(2).broadcast_to([P, NE, BATCH]), ALU.add))
            step(dve.tensor_tensor(row[:], p_h[0][:, 0:BATCH * NE].rearrange("p (b e) -> p b e", e=NE),
                                   incl[:].rearrange("p e b -> p b e"), ALU.add))
            for k in range(TOPK):
                s = dve.tensor_tensor(rowk[k][:], row[:], pick[k][:], ALU.mult)
            step(s)
            for k in range(TOPK):
                s = dve.tensor_reduce(rowf[:, k, :], rowk[k][:], X, ALU.add)
            step(s)
            step(dve.tensor_copy(slots_i[:], rowf[:]))
            step(dve.tensor_tensor(ge[:], iota_i[:].unsqueeze(2).broadcast_to([P, TILES, NE - 1]),
                                   cum[:, 0:NE - 1].unsqueeze(1).broadcast_to([P, TILES, NE - 1]), ALU.is_ge))
            step(dve.tensor_reduce(te_f[:], ge[:], X, ALU.add))
            step(dve.tensor_copy(tile_expert[:], te_f[:]))
            dve.wait_ge(gate_exp, 1)
            step(dve.tensor_scalar(e2p[:], e2[:], 1.0, None, ALU.add))
            step(dve.reciprocal(gate[:, 0, :], e2p[:]))
            step(dve.tensor_tensor(gate[:, 1, :], gate[:, 0, :], e2[:], ALU.mult))
            assert steps[0] == N_ROUTE, steps[0]

            def add_b1(i, m, k, half):
                if half == 0:
                    dve.wait_ge(b1_ready[k], (m + 1) * 16)
                    need(dve, ht_turned, i * 2)
                dve.wait_ge(up_done, i * 2 + (half + 1))
                dve.tensor_tensor(hs[:, half * 512:(half + 1) * 512], p_h[half][:],
                                  b1_s[k][:, half * 512:(half + 1) * 512], ALU.add).then_inc(upb_done, 1)

            def add_b2(i, m, k):
                dve.wait_ge(down_done, i * 2 + 2)
                dve.wait_ge(b2_ready[k], (m + 1) * 16)
                need(dve, ys_stored[k], m * 16)
                dve.tensor_tensor(yo[k][:], p_o[k][:, 0:DM], b2_s[k][:], ALU.add).then_inc(yo_done, 1)

            def rest_x(i, k):
                dve.wait_ge(xh_done, i + 1)
                dve.tensor_tensor(xl[k][:].rearrange("p c s -> p (c s)"), p_x[k][:, 0:KC * P],
                                  xh[k][:].rearrange("p c s -> p (c s)"), ALU.subtract).then_inc(xl_done, 1)

            def rest_up(i, e, half):
                dve.wait_ge(uph_done, i * 2 + (half + 1))
                dve.tensor_tensor(upl[half][:], up_weights(e, half), uph[half][:], ALU.subtract).then_inc(upl_done, 1)

            def rest_down(i, e):
                dve.wait_ge(dnh_done, i * 2 + 1)
                dve.tensor_tensor(dnl[0][:, 0:DS], down_weights(e, 0, 0, DS), dnh[0][:, 0:DS],
                                  ALU.subtract).then_inc(dnl_done, 1)

            def rest_h(i, half):
                dve.wait_ge(hh_done, i * 2 + (half + 1))
                to = slice(half * 4, half * 4 + 4)
                dve.tensor_tensor(hl[:, to, :].rearrange("p c s -> p (c s)"), p_hT[half][:],
                                  hh[:, to, :].rearrange("p c s -> p (c s)"), ALU.subtract).then_inc(hl_done, 1)

            def step(i, m, k):
                add_b1(i, m, k, 0)
                add_b1(i, m, k, 1)
                if has_next(i):
                    rest_x(i + 1, 1 - k)
                if has_next(i):
                    e = expert_of(dve, i + 1)
                    rest_up(i + 1, e, 0)
                if not isinstance(i, int) or i:
                    add_b2(i - 1, m - 1 + k, 1 - k)
                if has_next(i):
                    rest_up(i + 1, e, 1)
                rest_down(i, expert_of(dve, i))
                rest_h(i, 0)
                rest_h(i, 1)

            rest_x(0, 0)
            e = expert_of(dve, 0)
            rest_up(0, e, 0)
            rest_up(0, e, 1)
            all_tiles(dve, step)
            add_b2(TILES - 1, TILES // 2, 0)

            def mixed(b):
                dve.wait_ge(gathered[b], 32)
                for k in range(TOPK):
                    if k:
                        dve.wait_ge(mix_step, 3 * b + 1)
                    dve.scalar_tensor_tensor(out=v3[:, b, :], in0=yg[k][:, b, :], scalar=gate[:, k, b:b + 1],
                                             in1=(v3 if k else x2_all)[:, b, :], op0=ALU.mult,
                                             op1=ALU.add).then_inc(mix_step, 1)
                dve.wait_ge(mix_step, 3 * b + 2)
                dve.bn_stats(stats3[:, b, :], v3[:, b, :]).then_inc(mix_step, 1)

            def spread(i):
                rows = slice(i * FB, (i + 1) * FB)
                dve.wait_ge(mix_step, 3 * FB * (i + 1))
                for b in range(i * FB, (i + 1) * FB):
                    s = dve.bn_aggr(mv3[:, b, :], stats3[:, b, :])
                s.then_inc(fin_stats, 1)
                dve.wait_ge(fin_stats, i + 1)
                dve.tensor_scalar(var3[:, rows], mv3[:, rows, 1], LN_EPS, None, ALU.add).then_inc(fin_var, 1)

            def normed(i):
                dve.wait_ge(fin_rstd, i + 1)
                for b in range(i * FB, (i + 1) * FB):
                    dve.tensor_scalar(res[:, b, :], v3[:, b, :], mv3[:, b, 0:1], rstd3[:, b:b + 1],
                                      ALU.subtract, ALU.mult).then_inc(fin_done, 1)

            dve.wait_ge(doubled, 1)
            for i in range(BATCH // FB):
                for b in range(i * FB, (i + 1) * FB):
                    mixed(b)
                spread(i)
                if i:
                    normed(i - 1)
            normed(BATCH // FB - 1)


R_DLT, R_PICKS, N_ROUTE = 3, 6, 27


def x_rows(t, g):
    return t[bass.ds(g * GB, GB)].rearrange("b s d -> s b d")


def kernel(x, ctx_1024, mask_BxS2_bf1, L0_attn_norm_w, L0_attn_w_in, L0_attn_conv_w, L0_attn_conv_b,
           L0_attn_w_xproj, L0_attn_A_log, L0_attn_D_param, L0_attn_w_out, L0_ffn_rw1, L0_ffn_rb1, L0_ffn_rw2,
           L0_ffn_rb2, L0_ffn_we1, L0_ffn_be1, L0_ffn_we2, L0_ffn_be2):
    import concourse.bacc as bacc
    from concourse.bass_utils import run_bass_kernel_spmd

    ctx = np.asarray(ctx_1024)
    mask = np.asarray(mask_BxS2_bf1).view(np.uint8)
    arrays = {
        "x": x, "ctxk": ctx,
        "ctxt": ctx.transpose(0, 2, 1).reshape(BATCH, KC, P, SEQ).transpose(2, 0, 1, 3),
        "mask": mask, "maskt": mask.T,
        "norm_w": L0_attn_norm_w, "w_in": L0_attn_w_in, "conv_w": L0_attn_conv_w, "conv_b": L0_attn_conv_b,
        "w_xproj": L0_attn_w_xproj, "a_log": L0_attn_A_log, "d_par": L0_attn_D_param, "w_out": L0_attn_w_out,
        "rw1": L0_ffn_rw1, "rb1": L0_ffn_rb1, "rw2": L0_ffn_rw2, "rb2": L0_ffn_rb2,
        "we1": L0_ffn_we1, "be1": L0_ffn_be1, "we2": L0_ffn_we2, "be2": L0_ffn_be2,
    }
    arrays = {f"in_{n}": np.ascontiguousarray(a) for n, a in arrays.items()}
    nc = bacc.Bacc("TRN2", target_bir_lowering=False, num_devices=1)
    args = [nc.dram_tensor(n, a.shape, mybir.dt.from_np(a.dtype), kind="ExternalInput").ap()
            for n, a in arrays.items()]
    out = nc.dram_tensor("out", [BATCH, SEQ, DM], F32, kind="ExternalOutput").ap()
    decoder_layer(nc, *args, out)
    r = run_bass_kernel_spmd(nc, [arrays], core_ids=[0])
    return r.results[0]["out"]
```
